# Optimizing a Trainium2 kernel written in Bass

```python
import numpy as np
import jax
import jax.numpy as jnp

def _softmax(x, axis=-1):
    return jax.nn.softmax(x, axis=axis)

def _gelu(x):
    return jax.nn.gelu(x, approximate=True)

def _silu(x):
    return jax.nn.silu(x)

def _sigmoid(x):
    return jax.nn.sigmoid(x)

def _layernorm(x, axis=-1, eps=1e-05):
    m = jnp.mean(x, axis=axis, keepdims=True)
    v = jnp.var(x, axis=axis, keepdims=True)
    return (x - m) / jnp.sqrt(v + eps)

def _scatter_add(tgt, idx, src, axis=0):
    return tgt.at[idx].add(src)

def _segment_sum(src, seg, n):
    return jax.ops.segment_sum(src, seg, n)
kernel_name = 'mk_gps_d1_gnn_r8_112815'

def setup_inputs(seed: int=0):
    np.random.seed(seed)
    _w = jnp.asarray

    def _rec_inputs():
        import jax
        import jax.numpy as jnp
        _gk = jax.random.key(seed)
        x = -0.0002117 + 1 * jax.random.normal(jax.random.fold_in(_gk, 1), (1250, 512), jnp.float32)
        _s = jax.random.randint(jax.random.fold_in(_gk, 2), (10000,), 0, 1250, jnp.int32)
        _d = jax.random.randint(jax.random.fold_in(_gk, 3), (10000,), 0, 1250, jnp.int32)
        _loop = jnp.arange(1250, dtype=jnp.int32)
        src = jnp.concatenate([_s, _d, _loop])
        dst = jnp.concatenate([_d, _s, _loop])
        _o = jnp.argsort(dst, stable=True)
        src = src[_o]
        dst = dst[_o]
        edge_weight = jax.random.uniform(jax.random.fold_in(_gk, 12), (21250,), jnp.float32, 0.0, 0.999999)
        return (x, src, dst, edge_weight)
    x, src, dst, edge_weight = _rec_inputs()

    def _L0_gnn_setup():
        import jax, jax.numpy as jnp
        import numpy as np
        N_NODES = 6250
        N_EDGES = 200000
        IN_F = 512
        OUT_F = 512
        key = jax.random.key(seed)
        k1, k2, k3, k4, k5 = jax.random.split(key, 5)
        input = jax.random.normal(k1, (N_NODES, IN_F), dtype=jnp.float32)
        edge_index = jax.random.randint(k2, (2, N_EDGES), 0, N_NODES, dtype=jnp.int64)
        edge_vals = jax.random.uniform(k3, (N_EDGES,), dtype=jnp.float32)
        stdv = 1.0 / np.sqrt(OUT_F)
        weight = jax.random.uniform(k4, (IN_F, OUT_F), dtype=jnp.float32, minval=-stdv, maxval=stdv)
        bias = jax.random.uniform(k5, (OUT_F,), dtype=jnp.float32, minval=-stdv, maxval=stdv)
        return {'input': input, 'edge_index': edge_index, 'edge_vals': edge_vals, 'weight': weight, 'bias': bias}
    _L0_gnn_all = _L0_gnn_setup()
    _L0_gnn_in = {k: v for k, v in _L0_gnn_all.items() if k in ('weight', 'bias')}
    del _L0_gnn_all

    def _L0_mix_setup():
        import jax, jax.numpy as jnp
        import numpy as np
        DIM = 512
        HEADS = 8
        DIM_HEAD = 64
        SLICE = 32
        INNER = HEADS * DIM_HEAD
        key = jax.random.key(seed)
        ks = jax.random.split(key, 8)
        B, N = (8, 1024)
        s = 0.02
        return {'x': jax.random.normal(ks[0], (B, N, DIM), dtype=jnp.float32), 'W_in': jax.random.normal(ks[1], (DIM, INNER), dtype=jnp.float32) * s, 'b_in': jnp.zeros((INNER,), dtype=jnp.float32), 'Wq': jax.random.normal(ks[2], (DIM_HEAD, SLICE), dtype=jnp.float32) * s, 'Wk': jax.random.normal(ks[3], (DIM_HEAD, SLICE), dtype=jnp.float32) * s, 'Wv': jax.random.normal(ks[4], (DIM_HEAD, DIM_HEAD), dtype=jnp.float32) * s, 'W_out': jax.random.normal(ks[5], (INNER, DIM), dtype=jnp.float32) * s, 'b_out': jnp.zeros((DIM,), dtype=jnp.float32)}
    _L0_mix_all = _L0_mix_setup()
    _L0_mix_in = {k: v for k, v in _L0_mix_all.items() if k in ('W_in', 'b_in', 'Wq', 'Wk', 'Wv', 'W_out', 'b_out')}
    del _L0_mix_all

    def _L0_ffn_setup():
        import jax, jax.numpy as jnp
        import numpy as np
        B, S, D = (32, 512, 512)
        E, H, O, K = (8, 256, 512, 2)
        key = jax.random.key(seed)
        ks = jax.random.split(key, 5)
        sc = lambda k, shape, scale: jax.random.normal(k, shape, jnp.float32) * scale
        return {'x': sc(ks[0], (B, S, D), 1.0), 'attn_w': sc(ks[1], (D, 1), 0.05), 'attn_b': jnp.zeros((1,), jnp.float32), 'gate_w': sc(ks[2], (D, E), 0.05), 'gate_b': jnp.zeros((E,), jnp.float32), 'w1': sc(ks[3], (E, D, H), 0.02), 'b1': jnp.zeros((E, H), jnp.float32), 'w2': sc(ks[4], (E, H, O), 0.02), 'b2': jnp.zeros((E, O), jnp.float32)}
    _L0_ffn_all = _L0_ffn_setup()
    _L0_ffn_in = {k: v for k, v in _L0_ffn_all.items() if k in ('attn_w', 'attn_b', 'gate_w', 'gate_b', 'w1', 'b1', 'w2', 'b2')}
    del _L0_ffn_all
    return {'x': x, 'src': src, 'dst': dst, 'edge_weight': edge_weight, 'L0_gnn_weight': _L0_gnn_in['weight'], 'L0_gnn_bias': _L0_gnn_in['bias'], 'L0_mix_W_in': _L0_mix_in['W_in'], 'L0_mix_b_in': _L0_mix_in['b_in'], 'L0_mix_Wq': _L0_mix_in['Wq'], 'L0_mix_Wk': _L0_mix_in['Wk'], 'L0_mix_Wv': _L0_mix_in['Wv'], 'L0_mix_W_out': _L0_mix_in['W_out'], 'L0_mix_b_out': _L0_mix_in['b_out'], 'L0_ffn_attn_w': _L0_ffn_in['attn_w'], 'L0_ffn_attn_b': _L0_ffn_in['attn_b'], 'L0_ffn_gate_w': _L0_ffn_in['gate_w'], 'L0_ffn_gate_b': _L0_ffn_in['gate_b'], 'L0_ffn_w1': _L0_ffn_in['w1'], 'L0_ffn_b1': _L0_ffn_in['b1'], 'L0_ffn_w2': _L0_ffn_in['w2'], 'L0_ffn_b2': _L0_ffn_in['b2']}

def reference(x, src, dst, edge_weight, L0_gnn_weight, L0_gnn_bias, L0_mix_W_in, L0_mix_b_in, L0_mix_Wq, L0_mix_Wk, L0_mix_Wv, L0_mix_W_out, L0_mix_b_out, L0_ffn_attn_w, L0_ffn_attn_b, L0_ffn_gate_w, L0_ffn_gate_b, L0_ffn_w1, L0_ffn_b1, L0_ffn_w2, L0_ffn_b2):
    import jax
    import jax.numpy as jnp

    def _L0_gnn_ref(input, edge_index, edge_vals, weight, bias):
        import jax, jax.numpy as jnp
        import numpy as np
        N_NODES = 6250
        N_EDGES = 200000
        IN_F = 512
        OUT_F = 512
        support = jnp.matmul(input, weight)
        dst, src = (edge_index[0], edge_index[1])
        messages = support[src] * edge_vals[:, None]
        output = jax.ops.segment_sum(messages, dst, num_segments=input.shape[0])
        return output + bias

    def _L0_mix_ref(x, W_in, b_in, Wq, Wk, Wv, W_out, b_out):
        import jax, jax.numpy as jnp
        import numpy as np
        DIM = 512
        HEADS = 8
        DIM_HEAD = 64
        SLICE = 32
        INNER = HEADS * DIM_HEAD
        B, N, C = x.shape
        x_mid = (x @ W_in + b_in).reshape(B, N, HEADS, DIM_HEAD).transpose(0, 2, 1, 3)
        q = x_mid @ Wq
        k = x_mid @ Wk
        v = x_mid @ Wv
        q = jax.nn.softmax(q, axis=-1)
        k = jax.nn.softmax(k, axis=-2)
        kv = jnp.einsum('bhns,bhnc->bhsc', k, v)
        qkv = jnp.einsum('bhns,bhsc->bhnc', q, kv)
        qkv = qkv.transpose(0, 2, 1, 3).reshape(B, N, INNER)
        return qkv @ W_out + b_out

    def _L0_ffn_ref(x, attn_w, attn_b, gate_w, gate_b, w1, b1, w2, b2):
        import jax, jax.numpy as jnp
        import numpy as np
        B, S, D = (32, 512, 512)
        E, H, O, K = (8, 256, 512, 2)
        scores = x @ attn_w + attn_b
        aw = jax.nn.softmax(scores, axis=1)
        pooled = jnp.sum(x * aw, axis=1)
        gates = jax.nn.softmax(pooled @ gate_w + gate_b, axis=-1)
        _, idx = jax.lax.top_k(gates, K)
        mask = jnp.sum(jax.nn.one_hot(idx, E, dtype=gates.dtype), axis=-2)
        g = gates * mask
        g = g / (jnp.sum(g, axis=-1, keepdims=True) + 1e-09)
        h = jax.nn.gelu(jnp.einsum('bsd,edh->ebsh', x, w1) + b1[:, None, None, :], approximate=False)
        eo = jax.nn.gelu(jnp.einsum('ebsh,eho->ebso', h, w2) + b2[:, None, None, :], approximate=False)
        return jnp.einsum('ebso,be->bso', eo, g)
    edge_index = jnp.stack([src, dst])
    xn = _layernorm(x, axis=-1)
    x = x + _L0_gnn_ref(xn, edge_index, edge_weight, L0_gnn_weight, L0_gnn_bias) + _L0_mix_ref(xn[None], L0_mix_W_in, L0_mix_b_in, L0_mix_Wq, L0_mix_Wk, L0_mix_Wv, L0_mix_W_out, L0_mix_b_out)[0]
    x = x + _L0_ffn_ref(_layernorm(x, axis=-1)[None], L0_ffn_attn_w, L0_ffn_attn_b, L0_ffn_gate_w, L0_ffn_gate_b, L0_ffn_w1, L0_ffn_b1, L0_ffn_w2, L0_ffn_b2)[0]
    return x

_drawn_inputs = setup_inputs


def setup_inputs(seed=0):
    import zlib

    import numpy as np

    out = dict(_drawn_inputs(seed))
    spreads = {'L0_mix_b_in': (0.0, 0.344),
     'L0_mix_b_out': (0.0, 0.1),
     'L0_ffn_gate_b': (0.0, 0.8),
     'L0_ffn_b1': (0.0, 0.8),
     'L0_ffn_b2': (0.0, 0.372)}
    factors = {'L0_gnn_bias': 3.875,
     'L0_mix_W_in': 8.0,
     'L0_mix_Wq': 8.0,
     'L0_mix_Wk': 8.0,
     'L0_mix_Wv': 3.404,
     'L0_mix_W_out': 3.378,
     'L0_ffn_w1': 3.306,
     'L0_ffn_w2': 3.092}
    for name, (base, spread) in spreads.items():
        noise = np.random.default_rng([zlib.crc32(name.encode()), seed]).standard_normal(out[name].shape)
        drawn = base * np.exp(spread * noise) if base else spread * noise
        out[name] = jnp.asarray(drawn.astype(out[name].dtype))
    for name, factor in factors.items():
        out[name] = (out[name] * factor).astype(out[name].dtype)
    return out
```

```python
from contextlib import ExitStack

import numpy as np
import concourse.bass as bass
from concourse import mybir

ALU = mybir.AluOpType
ACT = mybir.ActivationFunctionType
AX = mybir.AxisListType
F32, F16, BF16 = mybir.dt.float32, mybir.dt.float16, mybir.dt.bfloat16
I32, U32 = mybir.dt.int32, mybir.dt.uint32

P = 128
EPS = 1e-5
FAR = -1e30


def build(nc, x, src, dst, edge_weight, gnn_w, gnn_b, w_in, b_in, wq, wk, wv, w_out, b_out,
          attn_w, attn_b, gate_w, gate_b, w1, b1, w2, b2, out):
    N, D = x.shape
    NE = src.shape[0]
    HD, SL = wq.shape
    NH = D // HD
    NX, _, H = w1.shape
    T = (N + P - 1) // P
    NP = T * P
    TAIL = N - (T - 1) * P
    C = D // P
    HC = H // P
    RB = 16
    SEG = P // RB
    SPAN = NP // SEG
    BY_SPAN = (1 << 21) // SPAN + 1
    NB = NP // RB
    WIN = 3
    WE = WIN * P
    NT = NB * WIN
    GB = 512 // SPAN
    NG = (NB + GB - 1) // GB
    EP = 125
    EC = NE // EP
    LOW = 8
    BH = NB // LOW
    assert EP * EC == NE and D == 512 and NB <= P and NB % LOW == 0
    assert RB == SEG * 2 and P * N < 1 << 24 and (NP - 1) * BY_SPAN < 1 << 24
    assert all((i * BY_SPAN) >> 21 == i // SPAN for i in range(NP))
    Q = 4
    RING = 3
    SLOTS = [2, 1, 1] * T + [3, 3, 4, 4, 3, 3]
    assert sum(SLOTS) * Q == NT

    adj = nc.dram_tensor("adjacency", (NP, NP), F32).ap()
    adj_blocks = adj.rearrange("(b r) (h l) -> b (r h) l", r=RB, h=SEG)

    ctx = ExitStack()
    with ctx:
        def sb(name, shape, dt=F32):
            return ctx.enter_context(nc.sbuf_tensor(name, shape, dt))

        def sem(name):
            return ctx.enter_context(nc.semaphore(name))

        bank = [ctx.enter_context(nc.psum_tensor(f"bank{i}", [P, 512], F32)) for i in range(8)]

        ident = sb("ident", [P, P])
        ones = sb("ones", [P, P])
        iota_i = sb("iota_i", [P, SPAN], I32)
        iota_h = sb("iota_h", [P, SPAN], F16)
        part_i = sb("part_i", [P, 1], I32)
        low_i = sb("low_i", [P, 1], I32)
        part_f = sb("part_f", [P, 1])
        low_f = sb("low_f", [P, 1])
        base_f = sb("base_f", [P, 1])
        low_mask = sb("low_mask", [P, LOW])
        is_high = sb("is_high", [BH, BH, LOW])
        above_high = sb("above_high", [BH, BH, LOW])
        tail_far = sb("tail_far", [P, 1])
        x_sb = sb("x_sb", [P, T, D])
        xn = sb("xn", [P, T, D])
        support = sb("support", [P, T, D])
        w_in_sb = sb("w_in_sb", [P, C, D])
        w_vo = sb("w_vo", [P, C, D])
        two_qk = sb("two_qk", [P, 2, 2, SL])
        two_v = sb("two_v", [P, P])
        two_vt = sb("two_vt", [P, P])
        b_in_col = sb("b_in_col", [P, C])
        b_qk = sb("b_qk", [P, D])
        b_qk_row = b_qk[0:1, :]
        b_sum = sb("b_sum", [P, D])
        dst_all = sb("dst_all", [EP, EC], I32)
        src_all = sb("src_all", [EP, EC], I32)
        w_all = sb("w_all", [EP, EC])
        hi_i = sb("hi_i", [EP, EC], I32)
        lo_i = sb("lo_i", [EP, EC], I32)
        hi_h = sb("hi_h", [EP, EC], F16)
        lo_h = sb("lo_h", [EP, EC], F16)
        count_sb = sb("count_sb", [BH, LOW + 1])
        start_parts = sb("start_parts", [NB, LOW])
        start_f = sb("start_f", [NB, 2])
        start_u = sb("start_u", [NB, 1], U32)
        wgt_w = sb("wgt_w", [NB, WE])
        covered = sb("covered", [NB, 1])
        missing_i = sb("missing_i", [1, 1], I32)
        key_h = sb("key_h", [P, NT], F16)
        place_h = sb("place_h", [P, NT], F16)
        wgt_b = sb("wgt_b", [P, 3, NT], BF16)
        iota_q = sb("iota_q", [P, SPAN, Q], F16)
        stage = sb("stage", [P, 2, GB, SPAN])
        stats = sb("stats", [P, T, 6])
        moments = sb("moments", [P, T, 2])
        spread = sb("spread", [P, T])
        rstd = sb("rstd", [P, T])
        eps = sb("eps", [P, 1])
        q_buf = sb("q_buf", [P, 4, D // 2])
        q_red = sb("q_red", [P, T, 3, NH])
        q_t = sb("q_t", [P, 2, NP])
        k_max_t = sb("k_max_t", [P, 2])
        k_inv = sb("k_inv", [P, 2])
        mid_t = sb("mid_t", [P, C, P])


        def carve(space, at, rows, dims, dt=F32):
            n = int(np.prod(dims))
            words = n if dt in (F32, I32) else (n + 1) // 2
            flat = space[0:rows, at:at + words]
            if dt is not F32:
                flat = flat.bitcast(dt)
            names = [f"d{i}" for i in range(len(dims))]
            view = flat[:, 0:n].rearrange(f"p ({' '.join(names)}) -> p {' '.join(names)}",
                                          **dict(zip(names[1:], dims[1:]))) if len(dims) > 1 else flat
            return view, at + words

        adj_space = sb("adj_space", [P, T * NP])
        AT = adj_space[:].rearrange("p (t n) -> p t n", t=T)
        at = 0
        w_gnn, at = carve(adj_space, at, P, [C, D])
        w_out_sb, at = carve(adj_space, at, P, [C, D])
        w_in_t, at = carve(adj_space, at, P, [C, D])
        w_qk, at = carve(adj_space, at, P, [C, D])
        hot_hi, at = carve(adj_space, at, EP, [EC, BH], BF16)
        below_lo, at = carve(adj_space, at, EP, [EC, LOW + 1], BF16)
        dst_w, at = carve(adj_space, at, NB, [WE], I32)
        src_w, at = carve(adj_space, at, NB, [WE], I32)
        t_i, at = carve(adj_space, at, NB, [4, WE], I32)
        key_w, at = carve(adj_space, at, NB, [WE])
        assert at <= T * NP
        x2_space = sb("x2_space", [P, C * NP])
        x2_t = x2_space[:].rearrange("p (c n) -> p c n", c=C)
        k_sb, at = carve(x2_space, 0, P, [T, D // 2])
        b_out_b = x2_space[:, at:at + D]
        kxn, at = carve(x2_space, at, P, [2, D])
        kxn_t, at = carve(x2_space, at, P, [C, 2, P])
        place_w, at = carve(x2_space, at, NB, [WE])
        assert at <= C * NP
        hot_space = sb("hot_space", [P, (RING * (3 * P + SPAN) + 2 * P) * Q // 2])
        hot_row, at = carve(hot_space, 0, P, [RING, 3, P, Q], BF16)
        hot_col, at = carve(hot_space, at, P, [RING, SPAN, Q], BF16)
        hot_key, at = carve(hot_space, at, P, [2, P, Q], BF16)
        wgt_r = stage[:].rearrange("p a b n -> p (a b n)")[:, 0:NT]
        junk, at = carve(hot_space, 0, P, [D])
        x_t_space = sb("x_t_space", [P, 2 * C * P])
        x_t, _ = carve(x_t_space, 0, P, [2, C, P])
        k_diag, at = carve(x_t_space, 0, P, [2, P])
        k_max, at = carve(x_t_space, at, P, [D // 2])
        z_sb, _ = carve(x_t_space, 0, P, [2, D])

        s = {}

        def S(name):
            if name not in s:
                s[name] = sem(name)
            return s[name]

        XT, SUP, QK, QT = [[(k, t) for t in range(T)] for k in ("x_t", "support", "qk", "q_t")]
        uses = [
            ["count", "edges"] + [("adj", g) for g in range(0, NG, 2)]
            + [("expert", i) for i in range(0, 2 * T, 4)],
            ["start", "weights"] + ["covered"] + [("adj", g) for g in range(1, NG, 2)]
            + [("expert", i) for i in range(1, 2 * T, 4)],
            ["two_vt", ("w_in_t", 0), ("w_in_t", 2), "b_qk_row"] + XT + ["k_max_t"]
            + [("x2_t", m) for m in range(0, T, 2)] + ["score_max"] + [("expert", i) for i in range(2, 2 * T, 4)],
            [("w_in_t", 1), ("w_in_t", 3), "b_qk"] + QT + ["k_max_b"]
            + [("x2_t", m) for m in range(1, T, 2)] + ["score_b"] + [("expert", i) for i in range(3, 2 * T, 4)],
            [("w_vo", 0), ("w_qk", 0)] + SUP[0::2] + [("kxn", 0), "mid_t"] + [("out", m) for m in range(0, T, 4)]
            + ["pooled"] + [("hid", i) for i in range(0, 12, 4)],
            [("w_vo", 1), ("w_qk", 1)] + SUP[1::2] + [("kxn", 1), ("z", 0)] + [("out", m) for m in range(1, T, 4)]
            + ["gates"] + [("hid", i) for i in range(1, 12, 4)],
            [("w_vo", 2), ("w_qk", 2)] + QK[0::2] + ["k_sum", ("kxn_t", 0), ("z", 1)]
            + [("out", m) for m in range(2, T, 4)] + ["gates_b"] + [("hid", i) for i in range(2, 12, 4)],
            [("w_vo", 3), ("w_qk", 3)] + QK[1::2] + [("kxn_t", 1)] + [("out", m) for m in range(3, T, 4)]
            + [("hid", i) for i in range(3, 12, 4)],
        ]
        turn = {use: (b, n) for b, keys in enumerate(uses) for n, use in enumerate(keys)}
        filled = [sem(f"filled{b}") for b in range(8)]
        drained = [sem(f"drained{b}") for b in range(8)]

        def pt(use):
            return bank[turn[use][0]]

        def wait_free(eng, use):
            b, n = turn[use]
            if n:
                eng.wait_ge(drained[b], n)

        def wait_filled(eng, use):
            b, n = turn[use]
            eng.wait_ge(filled[b], n + 1)

        def wait_drained(eng, use):
            b, n = turn[use]
            eng.wait_ge(drained[b], n + 1)

        def groups_ended(before, after):
            ends = [min((g + 1) * GB, NB) * WIN for g in range(NG)]
            return [g for g in range(NG) if before < ends[g] <= after]

        def slot_tiles(k):
            return Q * sum(SLOTS[:k]), Q * sum(SLOTS[:k + 1])

        g_idx = [sb(f"g_idx{i}", [1, 8], U32) for i in range(1)][0]

        scores = sb("scores", [P, T])
        aw_b = sb("aw_b", [P, D])
        ab_b = sb("ab_b", [P, 1])
        tiny = sb("tiny", [P, 64])
        gw_sb = sb("gw_sb", [P, C, NX])
        gb_row = sb("gb_row", [1, NX])
        pooled = sb("pooled", [P, C])
        gate_b2 = sb("gate_b2", [P, 2])

        hid = AT[:, 0:4, :]
        e_w1 = AT[:, 4:6, 0:C * H].rearrange("p e (c h) -> p e c h", c=C)
        e_w2 = AT[:, 6:8, 0:HC * D].rearrange("p e (c n) -> p e c n", c=HC)
        e_b2 = AT[:, 8, 0:2 * D].rearrange("p (e n) -> p e n", e=2)
        e_b1 = tiny[:, 32:32 + 2 * HC].rearrange("p (e c) -> p e c", e=2)
        pre = support[:, 0:4, :]
        post = support[:, 4:8, :]

        rep_iota = stage[:, 0, 0, 0:P]
        rep_row = stage[:, 0, 1, 0:P]
        rep_col = stage[:, 0, 2, :]
        rep_acc = stage[:, 1, 0, :]
        rep_key, at = carve(hot_space, 0, EP, [EC])
        rep_place, at = carve(hot_space, at, EP, [EC])

        block = ctx.enter_context(nc.Block())

        @block.sync
        def _(sp):
            as_list = lambda a: a.rearrange("(p c) -> p c", p=EP)
            sp.dma_start(dst_all[:], as_list(dst)).then_inc(S("dst_in"), 16)
            sp.wait_ge(S("x_pad"), 1)
            third = T // 3
            for i in range(3):
                sp.dma_start(x_sb[:, third * i:third * (i + 1), :],
                             x[P * third * i:P * third * (i + 1), :].rearrange("(t p) d -> p t d", p=P)
                             ).then_inc(S(f"x_in{i}"), 16)
            sp.dma_start(x_sb[0:TAIL, T - 1, :], x[P * (T - 1):N, :]).then_inc(S("x_tail"), 16)
            sp.dma_start(w_gnn[:], gnn_w.rearrange("(c p) n -> p c n", p=P)).then_inc(S("w_gnn_in"), 16)
            sp.dma_start(src_all[:], as_list(src)).then_inc(S("list_in"), 16)
            sp.dma_start(w_all[:], as_list(edge_weight)).then_inc(S("list_in"), 16)
            sp.dma_start(b_sum[:], gnn_b.partition_broadcast(P)).then_inc(S("b_sum_in"), 16)
            sp.dma_start(b_out_b, b_out.partition_broadcast(P)).then_inc(S("b_sum_in"), 16)
            sp.dma_start(aw_b[:], attn_w.rearrange("d o -> (d o)").partition_broadcast(P)).then_inc(S("gate_in"), 16)
            sp.dma_start(ab_b[:], attn_b.partition_broadcast(P)).then_inc(S("gate_in"), 16)
            sp.dma_start(gw_sb[:], gate_w.rearrange("(c p) e -> p c e", p=P)).then_inc(S("gate_in"), 16)
            sp.dma_start(gb_row[:], gate_b.rearrange("(o e) -> o e", o=1)).then_inc(S("gate_in"), 16)
            for g in range(NG):
                nb = min(GB, NB - g * GB)
                wait_drained(sp, ("adj", g))
                sp.dma_start(adj_blocks[g * GB:g * GB + nb].rearrange("b q l -> q b l"),
                             stage[:, g % 2, 0:nb, :]).then_inc(S(f"adj_out{g % 2}"), 16)
            for half in range(2):
                sp.wait_ge(S(f"adj_out{half}"), 16 * ((NG + 1 - half) // 2))
            sp.wait_ge(S("missing_known"), 1)
            missing = sp.value_load(missing_i[0:1, 0:1], min_val=-NE, max_val=NE)
            with sp.If(missing != 0):
                with sp.Fori(0, NB) as b:
                    sp.wait_ge(S("block_summed"), b + 1)
                    sp.dma_start(adj_blocks[bass.ds(b, 1)].rearrange("b q l -> q (b l)"),
                                 rep_acc[:]).then_inc(S("block_out"), 16)
                sp.wait_ge(S("block_out"), 16 * NB)
            with sp.Else():
                sp.nop()
            for k in range(T):
                sp.dma_start(AT[:, k, :], adj[P * k:P * (k + 1), :]).then_inc(S(f"adj_in{k}"), 16)
            sp.wait_ge(S("chosen"), 1)
            wait_filled(sp, ("out", T - 1))
            for e in range(2):
                ex = sp.value_load(g_idx[0:1, e:e + 1], min_val=0, max_val=NX - 1)
                sp.dma_start(e_w1[:, e], w1[bass.ds(ex, 1)].rearrange("e (c p) h -> p (e c) h", p=P)
                             ).then_inc(S(f"w1_in{e}"), 16)
                sp.dma_start(e_b1[:, e, :], b1[bass.ds(ex, 1)].rearrange("e (p c) -> p (e c)", p=P)
                             ).then_inc(S(f"b1_in{e}"), 16)
                sp.dma_start(e_w2[:, e], w2[bass.ds(ex, 1)].rearrange("e (p c) h -> p (e c) h", p=P)
                             ).then_inc(S(f"w2_in{e}"), 16)
                sp.dma_start(e_b2[:, e, :], b2[bass.ds(ex, 1)].rearrange("e n -> (e n)").partition_broadcast(P)
                             ).then_inc(S(f"b2_in{e}"), 16)
            for m in range(T):
                rows = P if m < T - 1 else TAIL
                sp.wait_ge(S("y_ready"), m + 1)
                sp.dma_start(out[P * m:P * m + rows, :], x_sb[0:rows, m, :]).then_inc(S("y_out"), 16)
            sp.wait_ge(S("y_out"), 16 * T)

        @block.gpsimd
        def _(pool):
            pool.memset(x_sb[:, T - 1, :], 0.0).then_inc(S("x_pad"), 1)
            pool.iota(iota_i[:], [[1, SPAN]], base=0, channel_multiplier=0).then_inc(S("iota_i"), 1)
            pool.iota(part_i[:], [[0, 1]], base=0, channel_multiplier=1).then_inc(S("iota_i"), 1)
            pool.memset(two_qk[:], 0.0).then_inc(S("two_zero"), 1)
            pool.memset(two_v[:], 0.0).then_inc(S("two_zero"), 1)
            pool.memset(ident[:], 0.0).then_inc(S("const0"), 1)
            pool.memset(is_high[:], 0.0).then_inc(S("const0"), 1)
            pool.memset(above_high[:], 1.0).then_inc(S("const0"), 1)
            pool.memset(tail_far[:], 0.0).then_inc(S("const0"), 1)
            pool.wait_ge(S("const0"), 4)
            pool.affine_select(out=ident[:], in_=ident[:], compare_op=ALU.not_equal, fill=1.0, base=0,
                               pattern=[[-1, P]], channel_multiplier=1).then_inc(S("ident"), 1)
            pool.affine_select(out=is_high[:], in_=is_high[:], compare_op=ALU.not_equal, fill=1.0, base=0,
                               pattern=[[1, BH], [0, LOW]], channel_multiplier=-1).then_inc(S("digits"), 1)
            pool.affine_select(out=above_high[:], in_=above_high[:], compare_op=ALU.is_gt, fill=0.0, base=0,
                               pattern=[[1, BH], [0, LOW]], channel_multiplier=-1).then_inc(S("digits"), 1)
            pool.affine_select(out=tail_far[:], in_=tail_far[:], compare_op=ALU.is_ge, fill=FAR, base=TAIL - 1,
                               pattern=[[0, 1]], channel_multiplier=-1).then_inc(S("const"), 1)
            pool.memset(ones[:], 1.0).then_inc(S("const"), 1)
            pool.memset(mid_t[:], 0.0).then_inc(S("const"), 1)
            pool.wait_ge(S("starts"), 1)
            for dst_sb, table in ((dst_w, dst), (src_w, src), (wgt_w, edge_weight)):
                pool.indirect_dma_start(out=dst_sb[:], out_offset=None, in_=table.rearrange("(e o) -> e o", o=1),
                                        in_offset=bass.IndirectOffsetOnAxis(ap=start_u[:], axis=0)
                                        ).then_inc(S("window_in"), 16)
            pool.wait_ge(S("b_sum_in"), 32)
            pool.tensor_tensor(b_sum[:], b_sum[:], b_out_b, ALU.add).then_inc(S("b_sum"), 1)
            pool.wait_ge(S("b_sum"), 1)
            pool.wait_ge(S("normed"), T)
            for t in range(T):
                pool.tensor_tensor(x_sb[:, t, :], x_sb[:, t, :], b_sum[:], ALU.add).then_inc(S("x_biased"), 1)

        @block.tensor
        def _(pe):
            mm = nc.tensor.matmul

            def end(ins, use):
                ins.then_inc(filled[turn[use][0]], 1)

            pe.wait_ge(S("list_hot"), 2)
            for c in range(EC):
                last = mm(pt("count")[0:BH, 0:LOW + 1], hot_hi[:, c, :], below_lo[:, c, :],
                          start=(c == 0), stop=(c == EC - 1))
            end(last, "count")
            pe.wait_ge(S("digits"), 2)
            wait_drained(pe, "count")
            mm(pt("start")[0:NB, 0:LOW + 1], is_high[:].rearrange("h a b -> h (a b)"), count_sb[:],
               start=True, stop=True)
            end(mm(pt("start")[0:NB, 16:17], above_high[:].rearrange("h a b -> h (a b)"),
                   count_sb[:, LOW:LOW + 1], start=True, stop=True), "start")
            pe.wait_ge(S("ident"), 1)
            pe.wait_ge(S("two_in"), 16 * 6)
            wait_free(pe, "two_vt")
            end(nc.tensor.transpose(pt("two_vt")[:, 0:P], two_v[:], ident[:]), "two_vt")
            pe.wait_ge(S("w_in_in"), 16)
            for p in range(C):
                wait_free(pe, ("w_in_t", p))
                for c in range(C):
                    last = nc.tensor.transpose(pt(("w_in_t", p))[:, P * c:P * c + P],
                                               w_in_sb[:, c, P * p:P * p + P], ident[:])
                end(last, ("w_in_t", p))
            pe.wait_ge(S("const"), 3)
            wait_drained(pe, "two_vt")
            pe.wait_ge(S("w_out_in"), 16)
            for p in range(C):
                end(mm(pt(("w_vo", p))[:], two_vt[:], w_out_sb[:, p, :], start=True, stop=True), ("w_vo", p))
            for m in range(C):
                wait_free(pe, ("w_qk", m))
                view = pt(("w_qk", m))[:].rearrange("p (k n) -> p k n", k=2)
                for p in range(C):
                    wait_drained(pe, ("w_in_t", p))
                    last = mm(view[:, :, 2 * SL * p:2 * SL * (p + 1)], w_in_t[:, p, P * m:P * m + P],
                              two_qk[:].rearrange("p k h s -> p k (h s)"), start=True, stop=True)
                end(last, ("w_qk", m))
            wait_free(pe, "b_qk_row")
            pe.wait_ge(S("b_in_in"), 16)
            view = pt("b_qk_row")[:].rearrange("p (k n) -> p k n", k=2)
            for p in range(C):
                last = mm(view[0:1, :, 2 * SL * p:2 * SL * (p + 1)], b_in_col[:, p:p + 1],
                          two_qk[:].rearrange("p k h s -> p k (h s)"), start=True, stop=True)
            end(last, "b_qk_row")
            wait_drained(pe, "b_qk_row")
            wait_free(pe, "b_qk")
            end(mm(pt("b_qk")[:], ones[0:1, :], b_qk_row[:], start=True, stop=True), "b_qk")
            pe.wait_ge(S("window_keys"), 3)
            wait_free(pe, "edges")
            for a, w in enumerate((key_w, place_w)):
                for c in range(WIN):
                    col = (a * WIN + c) * NB
                    last = nc.tensor.transpose(pt("edges")[:, col:col + NB], w[:, P * c:P * c + P], ident[0:NB, 0:NB])
            end(last, "edges")
            wait_free(pe, "weights")
            for c in range(WIN):
                last = nc.tensor.transpose(pt("weights")[:, NB * c:NB * c + NB], wgt_w[:, P * c:P * c + P],
                                           ident[0:NB, 0:NB])
            end(last, "weights")
            wait_free(pe, "covered")
            end(mm(pt("covered")[0:1, 0:1], covered[:], ones[0:NB, 0:1], start=True, stop=True), "covered")

            def adj_signal(a, b):
                for n in range(a, b):
                    blk, c = n // WIN, n % WIN
                    g, within = blk // GB, blk % GB
                    if within == 0 and c == 0:
                        wait_free(pe, ("adj", g))
                    pe.wait_ge(S("hot_ready"), n // Q + 1)
                    slot, i = n // Q % RING, n % Q
                    for k in range(3):
                        last = mm(pt(("adj", g))[:, SPAN * within:SPAN * (within + 1)], hot_row[:, slot, k, :, i],
                                  hot_col[:, slot, :, i], start=(c == 0 and k == 0),
                                  stop=(c == WIN - 1 and k == 2))
                    if c == WIN - 1 and (within == GB - 1 or blk == NB - 1):
                        end(last, ("adj", g))
                    elif i == Q - 1:
                        last.then_inc(S("hot_used"), 1)

            def turn_q(t):
                wait_free(pe, ("q_t", t))
                pe.wait_ge(S("q_ready"), t + 1)
                for h in range(2):
                    last = nc.tensor.transpose(pt(("q_t", t))[:, P * h:P * h + P],
                                               q_buf[:, t % 4, P * h:P * h + P], ident[:])
                end(last, ("q_t", t))

            pe.wait_ge(S("w_gnn_in"), 16)
            for t in range(T + 2):
                if t < T:
                    wait_free(pe, ("x_t", t))
                    pe.wait_ge(S("normed"), t + 1)
                    for c in range(C):
                        last = nc.tensor.transpose(pt(("x_t", t))[:, P * c:P * c + P],
                                                   xn[:, t, P * c:P * c + P], ident[:])
                    end(last, ("x_t", t))
                    adj_signal(*slot_tiles(3 * t))
                    wait_drained(pe, ("x_t", t))
                    wait_free(pe, ("support", t))
                    for c in range(C):
                        last = mm(pt(("support", t))[:], x_t[:, t % 2, c, :], w_gnn[:, c, :],
                                  start=(c == 0), stop=(c == C - 1))
                    end(last, ("support", t))
                    adj_signal(*slot_tiles(3 * t + 1))
                    wait_free(pe, ("qk", t))
                    if t == 0:
                        for m in range(C):
                            wait_drained(pe, ("w_qk", m))
                    for c in range(C):
                        last = mm(pt(("qk", t))[:], x_t[:, t % 2, c, :], w_qk[:, c, :],
                                  start=(c == 0), stop=(c == C - 1))
                    end(last, ("qk", t))
                    adj_signal(*slot_tiles(3 * t + 2))
                if t >= 2:
                    turn_q(t - 2)

            wait_free(pe, "k_max_t")
            pe.wait_ge(S("k_max"), 1)
            for h in range(2):
                last = nc.tensor.transpose(pt("k_max_t")[:, P * h:P * h + P], k_max[:, P * h:P * h + P], ident[:])
            end(last, "k_max_t")
            adj_signal(*slot_tiles(3 * T))
            wait_free(pe, "k_max_b")
            pe.wait_ge(S("k_diag"), 2)
            end(mm(pt("k_max_b")[:, 0:2 * P], ones[:], k_diag[:].rearrange("p h n -> p (h n)"),
                   start=True, stop=True), "k_max_b")
            adj_signal(*slot_tiles(3 * T + 1))
            pe.wait_ge(S("k_exp"), 1)
            for h in range(2):
                wait_free(pe, ("kxn", h))
                for t in range(T):
                    last = mm(pt(("kxn", h))[:], k_sb[:, t, P * h:P * h + P], xn[:, t, :],
                              start=(t == 0), stop=(t == T - 1))
                    if t == T - 1:
                        end(last, ("kxn", h))
                    if t % (T // 2) == T // 2 - 1:
                        adj_signal(*slot_tiles(3 * T + 2 + 2 * h + t // (T // 2)))

            pe.wait_ge(S("missing_known"), 1)
            wait_drained(pe, ("adj", NG - 1))
            wait_drained(pe, ("adj", NG - 2))
            missing = pe.value_load(missing_i[0:1, 0:1], min_val=-NE, max_val=NE)
            with pe.If(missing != 0):
                with pe.Fori(0, NB * EC) as n:
                    pe.wait_ge(S("rep_hot"), n + 1)
                    mm(bank[0][:, 0:SPAN], rep_row[:], rep_col[:], start=True, stop=True).then_inc(S("rep_done"), 1)
            with pe.Else():
                pe.nop()

            wait_free(pe, "k_sum")
            for h in range(2):
                for t in range(T):
                    last = mm(pt("k_sum")[:, h:h + 1], k_sb[:, t, P * h:P * h + P], ones[:, 0:1],
                              start=(t == 0), stop=(t == T - 1))
            end(last, "k_sum")
            for i in range(2):
                wait_free(pe, ("kxn_t", i))
                for h in range(2):
                    wait_drained(pe, ("kxn", h))
                    for j in range(2):
                        c = 2 * i + j
                        last = nc.tensor.transpose(pt(("kxn_t", i))[:, (2 * j + h) * P:(2 * j + h + 1) * P],
                                                   kxn[:, h, P * c:P * c + P], ident[:])
                end(last, ("kxn_t", i))
            wait_free(pe, "mid_t")
            for i in range(2):
                wait_drained(pe, ("kxn_t", i))
            for p in range(C):
                for c in range(C):
                    last = mm(pt("mid_t")[:, P * p:P * p + P], w_in_sb[:, c, P * p:P * p + P],
                              kxn_t[:, c, p // 2, :], start=(c == 0), stop=(c == C - 1))
            end(last, "mid_t")
            wait_drained(pe, "mid_t")
            for h in range(2):
                wait_free(pe, ("z", h))
                for j in range(2):
                    last = mm(pt(("z", h))[:], mid_t[:, 2 * h + j, :], w_vo[:, 2 * h + j, :],
                              start=(j == 0), stop=(j == 1))
                end(last, ("z", h))

            def turn_x2(m):
                wait_free(pe, ("x2_t", m))
                pe.wait_ge(S("normed2"), m + 1)
                for c in range(C):
                    last = nc.tensor.transpose(pt(("x2_t", m))[:, P * c:P * c + P],
                                               xn[:, m, P * c:P * c + P], ident[:])
                end(last, ("x2_t", m))

            for m in range(T + 2):
                if m < T:
                    wait_free(pe, ("out", m))
                    for k in range(T):
                        if m == 0:
                            pe.wait_ge(S(f"adj_in{k}"), 16)
                            wait_drained(pe, ("support", k))
                        mm(pt(("out", m))[:], AT[:, k, P * m:P * m + P], support[:, k, :], start=(k == 0), stop=False)
                    if m == 0:
                        wait_drained(pe, ("q_t", T - 1))
                    for h in range(2):
                        if m == 0:
                            wait_drained(pe, ("z", h))
                        last = mm(pt(("out", m))[:], q_t[:, h, P * m:P * m + P], z_sb[:, h, :],
                                  start=False, stop=(h == 1))
                    end(last, ("out", m))
                if m >= 2:
                    turn_x2(m - 2)

            wait_free(pe, "score_max")
            pe.wait_ge(S("score_top"), 1)
            end(nc.tensor.transpose(pt("score_max")[0:1, 0:P], tiny[:, 0:1], ident[:]), "score_max")
            wait_drained(pe, "score_max")
            wait_free(pe, "score_b")
            end(mm(pt("score_b")[:, 0:1], ones[0:1, :], tiny[0:1, 1:2], start=True, stop=True), "score_b")
            pe.wait_ge(S("score_exp"), 1)
            wait_free(pe, "pooled")
            for c in range(C):
                for t in range(T):
                    mm(pt("pooled")[:, c:c + 1], xn[:, t, P * c:P * c + P], scores[:, t:t + 1],
                       start=(t == 0), stop=(t == T - 1))
            end(mm(pt("pooled")[:, 8:9], ones[:], tiny[:, 3:4], start=True, stop=True), "pooled")
            wait_drained(pe, "pooled")
            wait_free(pe, "gates")
            for c in range(C):
                last = mm(pt("gates")[0:1, 0:NX], pooled[:, c:c + 1], gw_sb[:, c, :], start=(c == 0), stop=(c == C - 1))
            end(last, "gates")
            pe.wait_ge(S("shares"), 1)
            wait_free(pe, "gates_b")
            end(mm(pt("gates_b")[:, 0:2], ones[0:1, :], tiny[0:1, 24:26], start=True, stop=True), "gates_b")

            for i in range(12):
                e, half, chunk = i // 6, i // 3 % 2, i % 3
                n0, n1 = 512 * chunk, min(512 * (chunk + 1), NP)
                wait_free(pe, ("hid", i))
                if i % 6 == 0:
                    pe.wait_ge(S(f"w1_in{e}"), 16)
                    for m in (T - 1, T - 2):
                        wait_drained(pe, ("x2_t", m))
                for c in range(C):
                    last = mm(pt(("hid", i))[:, 0:n1 - n0], e_w1[:, e, c, half:H:HC], x2_t[:, c, n0:n1],
                              start=(c == 0), stop=(c == C - 1))
                end(last, ("hid", i))
            for m in range(T):
                for e in range(2):
                    use = ("expert", 2 * m + e)
                    wait_free(pe, use)
                    if m == 0:
                        pe.wait_ge(S(f"w2_in{e}"), 16)
                        for i in range(6 * e, 6 * e + 6):
                            wait_drained(pe, ("hid", i))
                    for c in range(HC):
                        last = mm(pt(use)[:], hid[:, 2 * e + c, P * m:P * m + P], e_w2[:, e, c, :],
                                  start=(c == 0), stop=(c == HC - 1))
                    end(last, use)

        @block.scalar
        def _(act):
            cp = nc.scalar.copy

            def drain(use, out_ap, in_ap):
                wait_filled(act, use)
                cp(out_ap, in_ap).then_inc(drained[turn[use][0]], 1)

            def drain_x2(m):
                wait_filled(act, ("x2_t", m))
                cp(x2_t[:, :, P * m:P * m + P], pt(("x2_t", m))[:].rearrange("p (c n) -> p c n", c=C)
                   ).then_inc(drained[turn[("x2_t", m)][0]], 1)

            act.dma_start(w_in_sb[:], w_in.rearrange("(c p) n -> p c n", p=P)).then_inc(S("w_in_in"), 16)
            act.wait_ge(S("two_zero"), 2)
            for i in range(2):
                act.dma_start(two_qk[HD * i:HD * i + HD, 0, i, :], wq).then_inc(S("two_in"), 16)
                act.dma_start(two_qk[HD * i:HD * i + HD, 1, i, :], wk).then_inc(S("two_in"), 16)
                act.dma_start(two_v[HD * i:HD * i + HD, HD * i:HD * i + HD], wv).then_inc(S("two_in"), 16)
            act.dma_start(w_out_sb[:], w_out.rearrange("(c p) n -> p c n", p=P)).then_inc(S("w_out_in"), 16)
            act.dma_start(b_in_col[:], b_in.rearrange("(c p) -> p c", p=P),
                          allow_slow_non_contiguous=True).then_inc(S("b_in_in"), 16)

            drain("two_vt", two_vt[:], pt("two_vt")[:, 0:P])
            for p in range(C):
                drain(("w_in_t", p), w_in_t[:, p, :], pt(("w_in_t", p))[:])
            act.wait_ge(S("variances"), 1)
            act.wait_ge(S("eps"), 1)
            nc.scalar.activation(spread[:], moments[:, :, 1], ACT.Sqrt, bias=eps[:]).then_inc(S("spread"), 1)
            for p in range(C):
                drain(("w_vo", p), w_vo[:, p, :], pt(("w_vo", p))[:])
            for m in range(C):
                drain(("w_qk", m), w_qk[:, m, :], pt(("w_qk", m))[:])
            drain("b_qk_row", b_qk_row[:], pt("b_qk_row")[0:1, :])
            drain("b_qk", b_qk[:], pt("b_qk")[:])

            def groups(k):
                for g in groups_ended(*slot_tiles(k)):
                    nb = min(GB, NB - g * GB)
                    if g >= 2:
                        act.wait_ge(S(f"adj_out{g % 2}"), 16 * (g // 2))
                    drain(("adj", g), stage[:, g % 2, 0:nb, :].rearrange("p b l -> p (b l)"),
                          pt(("adj", g))[:, 0:nb * SPAN])

            for t in range(T + 2):
                if t < T:
                    if t >= 2:
                        wait_filled(act, ("qk", t - 2))
                    drain(("x_t", t), x_t[:, t % 2].rearrange("p c n -> p (c n)"), pt(("x_t", t))[:])
                    groups(3 * t)
                    drain(("support", t), support[:, t, :], pt(("support", t))[:])
                    groups(3 * t + 1)
                    groups(3 * t + 2)
                if 1 <= t <= T:
                    act.wait_ge(S("q_less"), t)
                    nc.scalar.activation(q_buf[:, (t - 1) % 4, :], q_buf[:, (t - 1) % 4, :], ACT.Exp
                                         ).then_inc(S("q_exp"), 1)
                if t >= 2:
                    wait_filled(act, ("q_t", t - 2))
                    cp(q_t[:, :, P * (t - 2):P * (t - 1)],
                       pt(("q_t", t - 2))[:, 0:2 * P].rearrange("p (h n) -> p h n", h=2)
                       ).then_inc(drained[turn[("q_t", t - 2)][0]], 1)
            groups(3 * T)
            groups(3 * T + 1)
            act.wait_ge(S("k_less"), 1)
            nc.scalar.activation(k_sb[:], k_sb[:], ACT.Exp).then_inc(S("k_exp"), 1)
            for k in range(3 * T + 2, len(SLOTS)):
                groups(k)
            for i in range(2):
                drain(("kxn_t", i), kxn_t[:, 2 * i:2 * i + 2].rearrange("p c h n -> p (c h n)"), pt(("kxn_t", i))[:])
            for h in range(2):
                drain(("z", h), z_sb[:, h, :], pt(("z", h))[:])
            for m in range(T):
                act.wait_ge(S("moments2"), m + 1)
                nc.scalar.activation(spread[:, m:m + 1], moments[:, m, 1:2], ACT.Sqrt, bias=eps[:]
                                     ).then_inc(S("spread2"), 1)
                if m >= 2:
                    drain_x2(m - 2)
            drain_x2(T - 2)
            drain_x2(T - 1)
            act.wait_ge(S("score_far"), 1)
            nc.scalar.activation(scores[:], scores[:], ACT.Exp, bias=tiny[:, 2:3], accum_out=tiny[:, 3:4]
                                 ).then_inc(S("score_exp"), 1)
            act.wait_ge(S("gate_less"), 1)
            nc.scalar.activation(tiny[0:1, 8:8 + NX], tiny[0:1, 8:8 + NX], ACT.Exp, accum_out=tiny[0:1, 5:6]
                                 ).then_inc(S("gate_exp"), 1)
            for i in range(12):
                e, half, chunk = i // 6, i // 3 % 2, i % 3
                n0, n1 = 512 * chunk, min(512 * (chunk + 1), NP)
                wait_filled(act, ("hid", i))
                if i % 6 == 0:
                    act.wait_ge(S(f"b1_in{e}"), 16)
                nc.scalar.activation(hid[:, 2 * e + half, n0:n1], pt(("hid", i))[:, 0:n1 - n0], ACT.Gelu,
                                     bias=e_b1[:, e, half:half + 1]).then_inc(drained[turn[("hid", i)][0]], 1)
            for i in range(2 * T):
                act.wait_ge(S("pre"), i + 1)
                if i >= 4:
                    act.wait_ge(S("y_ready"), (i - 4) // 2 + 1)
                nc.scalar.activation(post[:, i % 4, :], pre[:, i % 4, :], ACT.Gelu).then_inc(S("post"), 1)

        @block.vector
        def _(v):
            link_count = [0]

            def link(ins):
                link_count[0] += 1
                ins.then_inc(S("v_link"), 1)
                v.wait_ge(S("v_link"), link_count[0])

            tt, ts, tr = nc.vector.tensor_tensor, nc.vector.tensor_scalar, nc.vector.tensor_reduce
            v.memset(eps[:], EPS).then_inc(S("eps"), 1)
            v.wait_ge(S("dst_in"), 16)
            link(ts(hi_i[:], dst_all[:], 7, None, ALU.logical_shift_right))
            link(ts(lo_i[:], dst_all[:], 4, 7, ALU.logical_shift_right, ALU.bitwise_and))
            link(nc.vector.tensor_copy(hi_h[:], hi_i[:]))
            v.wait_ge(S("iota_i"), 2)
            nc.vector.tensor_copy(iota_h[:], iota_i[:]).then_inc(S("iota_h"), 1)
            v.wait_ge(S("iota_h"), 1)
            link(nc.vector.tensor_copy(lo_h[:], lo_i[:]))
            tt(hot_hi[:], hi_h[:].unsqueeze(2).to_broadcast([EP, EC, BH]),
               iota_h[0:EP, 0:BH].unsqueeze(1).to_broadcast([EP, EC, BH]), ALU.is_equal).then_inc(S("list_hot"), 1)
            tt(below_lo[:], lo_h[:].unsqueeze(2).to_broadcast([EP, EC, LOW + 1]),
               iota_h[0:EP, 0:LOW + 1].unsqueeze(1).to_broadcast([EP, EC, LOW + 1]), ALU.is_lt
               ).then_inc(S("list_hot"), 1)
            nc.vector.tensor_copy(iota_q[:], iota_i[:].unsqueeze(2).to_broadcast([P, SPAN, Q]))
            link(nc.vector.tensor_copy(part_f[:], part_i[:]))
            link(ts(low_i[:], part_i[:], LOW - 1, None, ALU.bitwise_and))
            link(nc.vector.tensor_copy(low_f[:], low_i[:]))
            link(ts(low_mask[:], iota_h[:, 0:LOW], low_f[:], None, ALU.is_equal))
            link(ts(base_f[:], part_f[:], float(P), None, ALU.mult))

            def moments_of(t):
                link(nc.vector.bn_stats(stats[:, t, :], x_sb[:, t, :]))
                return nc.vector.bn_aggr(moments[:, t, :], stats[:, t, :])

            v.wait_ge(S("x_in0"), 16)
            for t in range(2):
                link(moments_of(t))
            wait_filled(v, "count")
            nc.vector.tensor_copy(count_sb[:], pt("count")[0:BH, 0:LOW + 1]).then_inc(drained[0], 1)
            wait_filled(v, "start")
            link(tt(start_parts[:], pt("start")[0:NB, 0:LOW], low_mask[0:NB, :], ALU.mult))
            link(tr(start_f[:, 0:1], start_parts[:], AX.X, ALU.add))
            tt(start_f[:, 1:2], start_f[:, 0:1], pt("start")[0:NB, 16:17], ALU.add).then_inc(drained[1], 1)
            wait_drained(v, "start")
            ts(start_u[:], start_f[:, 1:2], float(NE - WE), None, ALU.min).then_inc(S("starts"), 1)
            for t in range(2, T):
                if t % 3 == 0 and t < T - 1:
                    v.wait_ge(S(f"x_in{t // 3}"), 16)
                if t == T - 1:
                    v.wait_ge(S("x_tail"), 16)
                ins = moments_of(t)
                if t < T - 1:
                    link(ins)
                else:
                    ins.then_inc(S("variances"), 1)
            v.wait_ge(S("variances"), 1)
            v.wait_ge(S("spread"), 1)
            link(nc.vector.reciprocal(rstd[:], spread[:]))
            for t in range(T):
                ts(xn[:, t, :], x_sb[:, t, :], moments[:, t, 0:1], rstd[:, t:t + 1], ALU.subtract, ALU.mult
                   ).then_inc(S("normed"), 1)
            v.wait_ge(S("window_in"), 48)
            link(ts(t_i[:, 0, :], dst_w[:], 3, None, ALU.logical_shift_left))
            link(ts(t_i[:, 3, :], src_w[:], float(BY_SPAN), None, ALU.mult))
            link(ts(t_i[:, 1, :], t_i[:, 3, :], 21, None, ALU.logical_shift_right))
            link(tt(t_i[:, 2, :], t_i[:, 0, :], t_i[:, 1, :], ALU.bitwise_or))
            ts(key_w[:], t_i[:, 2, :], base_f[0:NB, :], None, ALU.subtract).then_inc(S("window_keys"), 1)
            nc.vector.scalar_tensor_tensor(out=place_w[:], in0=t_i[:, 1, :], scalar=float(-SPAN), in1=src_w[:],
                                           op0=ALU.mult, op1=ALU.add).then_inc(S("window_keys"), 1)
            link(ts(t_i[:, 0, :], dst_w[:], 4, None, ALU.logical_shift_right))
            link(ts(t_i[:, 1, :], t_i[:, 0, :], part_f[0:NB, :], None, ALU.is_equal))
            tr(covered[:], t_i[:, 1, :], AX.X, ALU.add).then_inc(S("window_keys"), 1)
            wait_filled(v, "edges")
            by_tile = lambda a: a.rearrange("p (c b) -> p c b", c=WIN)
            to_tile = lambda a: a.rearrange("p (b c) -> p c b", c=WIN)
            link(nc.vector.tensor_copy(to_tile(key_h[:]), by_tile(pt("edges")[:, 0:NT])))
            nc.vector.tensor_copy(to_tile(place_h[:]), by_tile(pt("edges")[:, NT:2 * NT])).then_inc(drained[0], 1)
            wait_drained(v, "edges")
            wait_filled(v, "weights")
            wgt = by_tile(pt("weights")[:, 0:NT])
            rest = by_tile(wgt_r)
            link(nc.vector.tensor_copy(to_tile(wgt_b[:, 0, :]), wgt))
            tt(rest, wgt, to_tile(wgt_b[:, 0, :]), ALU.subtract).then_inc(drained[1], 1)
            wait_drained(v, "weights")
            link(nc.vector.tensor_copy(to_tile(wgt_b[:, 1, :]), rest))
            link(tt(to_tile(wgt_b[:, 2, :]), rest, to_tile(wgt_b[:, 1, :]), ALU.subtract))
            wait_filled(v, "covered")
            link(ts(tiny[0:1, 60:61], pt("covered")[0:1, 0:1], -1.0, float(NE), ALU.mult, ALU.add))
            nc.vector.tensor_copy(missing_i[:], tiny[0:1, 60:61]).then_inc(drained[1], 1)
            wait_drained(v, "covered")
            v.sem_inc(S("missing_known"), 1)

            def edge_tiles(a, b):
                for lot in range(a // Q, b // Q):
                    slot, tiles = lot % RING, slice(Q * lot, Q * (lot + 1))
                    if lot >= RING:
                        ends = [min((g + 1) * GB, NB) * WIN for g in range(NG)]
                        used = Q * (lot - RING + 1)
                        if used in ends:
                            wait_filled(v, ("adj", ends.index(used)))
                        else:
                            v.wait_ge(S("hot_used"), sum(n not in ends for n in range(Q, used + 1, Q)))
                    tt(hot_key[:, lot % 2], key_h[:, tiles].unsqueeze(1).to_broadcast([P, P, Q]), iota_q[:, 0:P, :],
                       ALU.is_equal).then_inc(S("hot_key"), 1)
                    tt(hot_col[:, slot], place_h[:, tiles].unsqueeze(1).to_broadcast([P, SPAN, Q]), iota_q[:],
                       ALU.is_equal)
                    v.wait_ge(S("hot_key"), lot + 1)
                    tt(hot_row[:, slot], hot_key[:, lot % 2].unsqueeze(1).to_broadcast([P, 3, P, Q]),
                       wgt_b[:, :, tiles].unsqueeze(2).to_broadcast([P, 3, P, Q]), ALU.mult
                       ).then_inc(S("hot_ready"), 1)

            def softmax_q(t):
                wait_filled(v, ("qk", t))
                if t == 0:
                    wait_drained(v, "b_qk")
                if t >= 4:
                    wait_filled(v, ("q_t", t - 4))
                link(tt(q_buf[:, t % 4, :], pt(("qk", t))[:, 0:D // 2], b_qk[:, 0:D // 2], ALU.add))
                tt(k_sb[:, t, :], pt(("qk", t))[:, D // 2:D], b_qk[:, D // 2:D], ALU.add
                   ).then_inc(drained[turn[("qk", t)][0]], 1)
                q = q_buf[:, t % 4, :].rearrange("p (h s) -> p h s", h=NH)
                link(tr(q_red[:, t, 0, :], q, AX.X, ALU.max))
                tt(q, q, q_red[:, t, 0, :].unsqueeze(2).to_broadcast([P, NH, SL]), ALU.subtract
                   ).then_inc(S("q_less"), 1)

            def share_q(t):
                v.wait_ge(S("q_exp"), t + 1)
                q = q_buf[:, t % 4, :].rearrange("p (h s) -> p h s", h=NH)
                link(tr(q_red[:, t, 1, :], q, AX.X, ALU.add))
                link(nc.vector.reciprocal(q_red[:, t, 2, :], q_red[:, t, 1, :]))
                tt(q, q, q_red[:, t, 2, :].unsqueeze(2).to_broadcast([P, NH, SL]), ALU.mult
                   ).then_inc(S("q_ready"), 1)

            for t in range(T + 2):
                if t < T:
                    edge_tiles(*slot_tiles(3 * t))
                if 1 <= t <= T:
                    softmax_q(t - 1)
                if t < T:
                    edge_tiles(*slot_tiles(3 * t + 1))
                if t >= 2:
                    share_q(t - 2)
                if t < T:
                    edge_tiles(*slot_tiles(3 * t + 2))

            link(ts(k_sb[:, T - 1, :], k_sb[:, T - 1, :], tail_far[:], None, ALU.add))
            tr(k_max[:], k_sb[:].rearrange("p t n -> p n t"), AX.X, ALU.max).then_inc(S("k_max"), 1)
            edge_tiles(*slot_tiles(3 * T))
            wait_filled(v, "k_max_t")
            tr(k_max_t[:], pt("k_max_t")[:, 0:2 * P].rearrange("p (h n) -> p h n", h=2), AX.X, ALU.max
               ).then_inc(drained[turn["k_max_t"][0]], 1)
            wait_drained(v, "k_max_t")
            for h in range(2):
                ts(k_diag[:, h, :], ident[:], k_max_t[:, h:h + 1], None, ALU.mult).then_inc(S("k_diag"), 1)
            edge_tiles(*slot_tiles(3 * T + 1))
            wait_filled(v, "k_max_b")
            tt(k_sb[:], k_sb[:], pt("k_max_b")[:, 0:2 * P].unsqueeze(1).to_broadcast([P, T, 2 * P]), ALU.subtract
               ).then_inc(drained[turn["k_max_b"][0]], 1)
            wait_drained(v, "k_max_b")
            v.sem_inc(S("k_less"), 1)
            for k in range(3 * T + 2, len(SLOTS)):
                edge_tiles(*slot_tiles(k))

            wait_filled(v, ("adj", NG - 1))
            wait_drained(v, ("adj", NG - 1))
            wait_drained(v, ("adj", NG - 2))
            v.wait_ge(S("list_in"), 32)
            missing = v.value_load(missing_i[0:1, 0:1], min_val=-NE, max_val=NE)
            with v.If(missing != 0):
                for half in range(2):
                    v.wait_ge(S(f"adj_out{half}"), 16 * ((NG + 1 - half) // 2))
                ts(hi_i[:], dst_all[:], 3, None, ALU.logical_shift_left).then_inc(S("rep_v"), 1)
                ts(lo_i[:], src_all[:], float(BY_SPAN), None, ALU.mult).then_inc(S("rep_v"), 1)
                v.wait_ge(S("rep_v"), 2)
                ts(lo_i[:], lo_i[:], 21, None, ALU.logical_shift_right).then_inc(S("rep_v"), 1)
                v.wait_ge(S("rep_v"), 3)
                tt(hi_i[:], hi_i[:], lo_i[:], ALU.bitwise_or).then_inc(S("rep_v"), 1)
                v.wait_ge(S("rep_v"), 4)
                nc.vector.tensor_copy(rep_key, hi_i[:]).then_inc(S("rep_v"), 1)
                nc.vector.scalar_tensor_tensor(out=rep_place, in0=lo_i[:], scalar=float(-SPAN), in1=src_all[:],
                                               op0=ALU.mult, op1=ALU.add).then_inc(S("rep_v"), 1)
                ts(rep_iota, iota_i[:, 0:P], float(-P), None, ALU.add).then_inc(S("rep_v"), 1)
                v.wait_ge(S("rep_v"), 7)
                with v.Fori(0, NB) as b:
                    nc.vector.memset(rep_acc, 0.0).then_inc(S("rep_zero"), 1)
                    v.wait_ge(S("rep_zero"), b + 1)
                    ts(rep_iota, rep_iota, float(P), None, ALU.add).then_inc(S("rep_moved"), 1)
                    with v.Fori(0, EC) as c:
                        v.wait_ge(S("rep_moved"), b + 1)
                        ts(rep_row[0:EP, :], rep_iota[0:EP, :], rep_key[:, bass.ds(c, 1)], None, ALU.is_equal)
                        ts(rep_col[0:EP, :], iota_i[0:EP, :], rep_place[:, bass.ds(c, 1)],
                           w_all[:, bass.ds(c, 1)], ALU.is_equal, ALU.mult).then_inc(S("rep_hot"), 1)
                        v.wait_ge(S("rep_done"), b * EC + c + 1)
                        tt(rep_acc, rep_acc, bank[0][:, 0:SPAN], ALU.add).then_inc(S("rep_added"), 1)
                        v.wait_ge(S("rep_added"), b * EC + c + 1)
                        v.nop()
                    v.sem_inc(S("block_summed"), 1)
                    v.wait_ge(S("block_out"), 16 * b + 16)
                    v.nop()
            with v.Else():
                v.nop()

            wait_filled(v, "k_sum")
            nc.vector.reciprocal(k_inv[:], pt("k_sum")[:, 0:2]).then_inc(drained[turn["k_sum"][0]], 1)
            wait_drained(v, "k_sum")
            v.wait_ge(S("b_sum"), 1)
            for h in range(2):
                wait_filled(v, ("kxn", h))
                ts(kxn[:, h, :], pt(("kxn", h))[:], k_inv[:, h:h + 1], None, ALU.mult
                   ).then_inc(drained[turn[("kxn", h)][0]], 1)
            wait_filled(v, "mid_t")
            v.wait_ge(S("b_in_in"), 16)
            for p in range(C):
                for i in range(2):
                    rows = slice(HD * i, HD * i + HD)
                    col = 2 * SL * (p % 2) + SL * i
                    last = ts(mid_t[rows, p, col:col + SL], pt("mid_t")[rows, P * p + col:P * p + col + SL],
                              b_in_col[rows, p:p + 1], None, ALU.add)
                    if (p, i) == (C - 1, 1):
                        last.then_inc(drained[turn["mid_t"][0]], 1)
                    else:
                        link(last)

            v.wait_ge(S("x_biased"), T)
            v.wait_ge(S("gate_in"), 64)
            for m in range(T + 1):
                if m < T:
                    wait_filled(v, ("out", m))
                    tt(x_sb[:, m, :], x_sb[:, m, :], pt(("out", m))[:], ALU.add
                       ).then_inc(drained[turn[("out", m)][0]], 1)
                    wait_drained(v, ("out", m))
                    moments_of(m).then_inc(S("moments2"), 1)
                if m >= 1:
                    t = m - 1
                    v.wait_ge(S("spread2"), t + 1)
                    v.wait_ge(S("moments2"), t + 1)
                    link(nc.vector.reciprocal(rstd[:, t:t + 1], spread[:, t:t + 1]))
                    ts(xn[:, t, :], x_sb[:, t, :], moments[:, t, 0:1], rstd[:, t:t + 1], ALU.subtract, ALU.mult
                       ).then_inc(S("normed2"), 1)
                    v.wait_ge(S("normed2"), t + 1)
                    link(nc.vector.tensor_tensor_reduce(out=junk[:], in0=xn[:, t, :], in1=aw_b[:], scale=1.0, scalar=0.0,
                                                        op0=ALU.mult, op1=ALU.add, accum_out=scores[:, t:t + 1]))
            link(ts(scores[:], scores[:], ab_b[:], None, ALU.add))
            link(ts(scores[:, T - 1:T], scores[:, T - 1:T], tail_far[:], None, ALU.add))
            tr(tiny[:, 0:1], scores[:], AX.X, ALU.max).then_inc(S("score_top"), 1)
            wait_filled(v, "score_max")
            tr(tiny[0:1, 1:2], pt("score_max")[0:1, 0:P], AX.X, ALU.max).then_inc(drained[turn["score_max"][0]], 1)
            wait_filled(v, "score_b")
            ts(tiny[:, 2:3], pt("score_b")[:, 0:1], -1.0, None, ALU.mult).then_inc(drained[turn["score_b"][0]], 1)
            wait_drained(v, "score_b")
            v.sem_inc(S("score_far"), 1)
            wait_filled(v, "pooled")
            link(nc.vector.reciprocal(tiny[:, 4:5], pt("pooled")[:, 8:9]))
            ts(pooled[:], pt("pooled")[:, 0:C], tiny[:, 4:5], None, ALU.mult).then_inc(drained[turn["pooled"][0]], 1)
            wait_filled(v, "gates")
            tt(tiny[0:1, 8:8 + NX], pt("gates")[0:1, 0:NX], gb_row[:], ALU.add).then_inc(drained[turn["gates"][0]], 1)
            wait_drained(v, "gates")
            link(tr(tiny[0:1, 6:7], tiny[0:1, 8:8 + NX], AX.X, ALU.max))
            ts(tiny[0:1, 8:8 + NX], tiny[0:1, 8:8 + NX], tiny[0:1, 6:7], None, ALU.subtract).then_inc(S("gate_less"), 1)
            v.wait_ge(S("gate_exp"), 1)
            link(nc.vector.reciprocal(tiny[0:1, 7:8], tiny[0:1, 5:6]))
            link(ts(tiny[0:1, 8:8 + NX], tiny[0:1, 8:8 + NX], tiny[0:1, 7:8], None, ALU.mult))
            link(nc.vector.max(tiny[0:1, 16:24], tiny[0:1, 8:8 + NX]))
            nc.vector.max_index(g_idx[:], tiny[0:1, 16:24], tiny[0:1, 8:8 + NX]).then_inc(S("chosen"), 1)
            link(tt(tiny[0:1, 26:27], tiny[0:1, 16:17], tiny[0:1, 17:18], ALU.add))
            link(ts(tiny[0:1, 26:27], tiny[0:1, 26:27], 1e-9, None, ALU.add))
            link(nc.vector.reciprocal(tiny[0:1, 27:28], tiny[0:1, 26:27]))
            ts(tiny[0:1, 24:26], tiny[0:1, 16:18], tiny[0:1, 27:28], None, ALU.mult).then_inc(S("shares"), 1)
            wait_filled(v, "gates_b")
            nc.vector.tensor_copy(gate_b2[:], pt("gates_b")[:, 0:2]).then_inc(drained[turn["gates_b"][0]], 1)
            wait_drained(v, "gates_b")

            def combine(m):
                v.wait_ge(S("post"), 2 * m + 2)
                link(nc.vector.scalar_tensor_tensor(out=x_sb[:, m, :], in0=post[:, 2 * m % 4, :], scalar=gate_b2[:, 0:1],
                                                    in1=x_sb[:, m, :], op0=ALU.mult, op1=ALU.add))
                nc.vector.scalar_tensor_tensor(out=x_sb[:, m, :], in0=post[:, (2 * m + 1) % 4, :],
                                               scalar=gate_b2[:, 1:2], in1=x_sb[:, m, :], op0=ALU.mult,
                                               op1=ALU.add).then_inc(S("y_ready"), 1)

            for m in range(T):
                for e in range(2):
                    i = 2 * m + e
                    wait_filled(v, ("expert", i))
                    if m == 0:
                        v.wait_ge(S(f"b2_in{e}"), 16)
                    if i >= 4:
                        v.wait_ge(S("post"), i - 3)
                    tt(pre[:, i % 4, :], pt(("expert", i))[:], e_b2[:, e, :], ALU.add
                       ).then_inc(drained[turn[("expert", i)][0]], 1)
                    wait_drained(v, ("expert", i))
                    v.sem_inc(S("pre"), 1)
                if m >= 1:
                    combine(m - 1)
            combine(T - 1)


_INS = ["x", "src", "dst", "edge_weight", "L0_gnn_weight", "L0_gnn_bias", "L0_mix_W_in", "L0_mix_b_in", "L0_mix_Wq",
        "L0_mix_Wk", "L0_mix_Wv", "L0_mix_W_out", "L0_mix_b_out", "L0_ffn_attn_w", "L0_ffn_attn_b", "L0_ffn_gate_w",
        "L0_ffn_gate_b", "L0_ffn_w1", "L0_ffn_b1", "L0_ffn_w2", "L0_ffn_b2"]


def kernel(**inputs):
    import concourse.bacc as bacc
    from concourse.bass_utils import run_bass_kernel_spmd

    nc = bacc.Bacc("TRN2", target_bir_lowering=False, num_devices=1)
    arrays, args = {}, []
    for name in _INS:
        a = np.ascontiguousarray(inputs[name])
        arrays[f"in_{name}"] = a
        args.append(nc.dram_tensor(f"in_{name}", a.shape, mybir.dt.from_np(a.dtype), kind="ExternalInput").ap())
    shape = tuple(inputs["x"].shape)
    args.append(nc.dram_tensor("out_y", shape, F32, kind="ExternalOutput").ap())
    build(nc, *args)
    r = run_bass_kernel_spmd(nc, [arrays], core_ids=[0])
    return r.results[0]["out_y"]
```

```python
from contextlib import ExitStack

import numpy as np
import concourse.bass as bass
from concourse import mybir

ALU = mybir.AluOpType
ACT = mybir.ActivationFunctionType
AX = mybir.AxisListType
F32, F16, BF16 = mybir.dt.float32, mybir.dt.float16, mybir.dt.bfloat16
I32, U32 = mybir.dt.int32, mybir.dt.uint32
F32R = mybir.dt.float32r

P = 128
EPS = 1e-5
FAR = -1e30


def build(nc, x, src, dst, edge_weight, gnn_w, gnn_b, w_in, b_in, wq, wk, wv, w_out, b_out,
          attn_w, attn_b, gate_w, gate_b, w1, b1, w2, b2, out):
    N, D = x.shape
    NE = src.shape[0]
    HD, SL = wq.shape
    NH = D // HD
    NX, _, H = w1.shape
    T = (N + P - 1) // P
    NP = T * P
    TAIL = N - (T - 1) * P
    C = D // P
    HC = H // P
    RB = 16
    SEG = P // RB
    SPAN = NP // SEG
    BY_SPAN = (1 << 21) // SPAN + 1
    NB = NP // RB
    WIN = 3
    WE = WIN * P
    NT = NB * WIN
    GB = 512 // SPAN
    NG = (NB + GB - 1) // GB
    EP = 125
    EC = NE // EP
    LOW = 8
    BH = NB // LOW
    assert EP * EC == NE and D == 512 and NB <= P and NB % LOW == 0
    assert RB == SEG * 2 and P * N < 1 << 24 and (NP - 1) * BY_SPAN < 1 << 24
    assert all((i * BY_SPAN) >> 21 == i // SPAN for i in range(NP))
    Q = 4
    RING = 3
    SLOTS = [2, 1, 1] * T + [3, 3, 4, 4, 3, 3]
    assert sum(SLOTS) * Q == NT

    adj = nc.dram_tensor("adjacency", (NP, NP), F32).ap()
    adj_blocks = adj.rearrange("(b r) (h l) -> b (r h) l", r=RB, h=SEG)

    ctx = ExitStack()
    with ctx:
        place = {}

        def sb(name, shape, dt=F32):
            tensor = ctx.enter_context(nc.sbuf_tensor(name, shape, dt))
            place[name] = nc.sbuf_base - int(np.prod(shape[1:])) * (2 if dt in (F16, BF16) else 4)
            return tensor

        def over(name, shape, dt, space, at=0):
            return nc.alloc_sbuf_tensor_at(name, shape, dt, offset=place[space] + at)

        def sem(name):
            return ctx.enter_context(nc.semaphore(name))

        bank = [ctx.enter_context(nc.psum_tensor(f"bank{i}", [P, 512], F32)) for i in range(8)]

        ident = sb("ident", [P, P])
        ones = sb("ones", [P, P])
        iota_i = sb("iota_i", [P, SPAN], I32)
        iota_h = sb("iota_h", [P, SPAN], F16)
        part_i = sb("part_i", [P, 1], I32)
        low_i = sb("low_i", [P, 1], I32)
        part_f = sb("part_f", [P, 1])
        low_f = sb("low_f", [P, 1])
        base_f = sb("base_f", [P, 1])
        low_mask = sb("low_mask", [P, LOW])
        is_high = sb("is_high", [BH, BH, LOW])
        above_high = sb("above_high", [BH, BH, LOW])
        tail_far = sb("tail_far", [P, 1])
        x_sb = sb("x_sb", [P, T, D])
        xn = sb("xn", [P, T, D])
        support = sb("support", [P, T, D])
        w_in_sb = sb("w_in_sb", [P, C, D])
        w_vo = sb("w_vo", [P, C, D])
        two_qk = sb("two_qk", [P, 2, 2, SL])
        two_v = sb("two_v", [P, P])
        two_vt = sb("two_vt", [P, P])
        b_in_col = sb("b_in_col", [P, C])
        b_qk = sb("b_qk", [P, D])
        b_qk_row = b_qk[0:1, :]
        b_sum = sb("b_sum", [P, D])
        dst_all = sb("dst_all", [EP, EC], I32)
        src_all = sb("src_all", [EP, EC], I32)
        w_all = sb("w_all", [EP, EC])
        hi_i = sb("hi_i", [EP, EC], I32)
        lo_i = sb("lo_i", [EP, EC], I32)
        hi_h = sb("hi_h", [EP, EC], F16)
        lo_h = sb("lo_h", [EP, EC], F16)
        count_sb = sb("count_sb", [BH, LOW + 1])
        start_parts = sb("start_parts", [NB, LOW])
        start_f = sb("start_f", [NB, 2])
        start_u = sb("start_u", [NB, 1], U32)
        wgt_w = sb("wgt_w", [NB, WE])
        covered = sb("covered", [NB, 1])
        missing_i = sb("missing_i", [1, 1], I32)
        key_h = sb("key_h", [P, NT], F16)
        place_h = sb("place_h", [P, NT], F16)
        wgt_b = sb("wgt_b", [P, 3, NT], BF16)
        iota_q = sb("iota_q", [P, SPAN, Q], F16)
        stage = sb("stage", [P, 2, GB, SPAN])
        stats = sb("stats", [P, T, 6])
        moments = sb("moments", [P, T, 2])
        spread = sb("spread", [P, T])
        rstd = sb("rstd", [P, T])
        eps = sb("eps", [P, 1])
        q_buf = sb("q_buf", [P, 4, D // 2])
        q_red = sb("q_red", [P, T, 3, NH])
        q_t = sb("q_t", [P, 2, NP])
        k_max_t = sb("k_max_t", [P, 2])
        k_inv = sb("k_inv", [P, 2, P])
        mid_t = sb("mid_t", [P, C, P])


        def carve(space, at, rows, dims, dt=F32):
            n = int(np.prod(dims))
            words = n if dt in (F32, I32) else (n + 1) // 2
            flat = space[0:rows, at:at + words]
            if dt is not F32:
                flat = flat.bitcast(dt)
            names = [f"d{i}" for i in range(len(dims))]
            view = flat[:, 0:n].rearrange(f"p ({' '.join(names)}) -> p {' '.join(names)}",
                                          **dict(zip(names[1:], dims[1:]))) if len(dims) > 1 else flat
            return view, at + words

        adj_space = sb("adj_space", [P, T * NP])
        AT = adj_space[:].rearrange("p (t n) -> p t n", t=T)
        at = 0
        w_gnn, at = carve(adj_space, at, P, [C, D])
        w_out_sb, at = carve(adj_space, at, P, [C, D])
        w_in_t, at = carve(adj_space, at, P, [C, D])
        w_qk, at = carve(adj_space, at, P, [C, D])
        hot_hi, at = carve(adj_space, at, EP, [EC, BH], BF16)
        below_lo, at = carve(adj_space, at, EP, [EC, LOW + 1], BF16)
        dst_w, at = carve(adj_space, at, NB, [WE], I32)
        src_w, at = carve(adj_space, at, NB, [WE], I32)
        t_i, at = carve(adj_space, at, NB, [4, WE], I32)
        key_w, at = carve(adj_space, at, NB, [WE])
        assert at <= T * NP
        x2_space = sb("x2_space", [P, C * NP])
        k_sb, at = carve(x2_space, 0, P, [T, D // 2])
        b_out_b = x2_space[:, at:at + D]
        kxn, at = carve(x2_space, at, P, [2, D])
        kxn_t, at = carve(x2_space, at, P, [C, 2, P])
        place_w, at = carve(x2_space, at, NB, [WE])
        assert at <= C * NP
        hot_space = sb("hot_space", [P, (RING * (3 * P + SPAN) + 2 * P) * Q // 2])
        hot_row, at = carve(hot_space, 0, P, [RING, 3, P, Q], BF16)
        hot_col, at = carve(hot_space, at, P, [RING, SPAN, Q], BF16)
        hot_key, at = carve(hot_space, at, P, [2, P, Q], BF16)
        wgt_r = stage[:].rearrange("p a b n -> p (a b n)")[:, 0:NT]
        x_t_space = sb("x_t_space", [P, 2 * C * P])
        x_t, _ = carve(x_t_space, 0, P, [2, C, P])
        k_diag, at = carve(x_t_space, 0, P, [2, P])
        k_max, at = carve(x_t_space, at, P, [D // 2])
        z_sb, _ = carve(x_t_space, 0, P, [2, D])

        s = {}

        def S(name):
            if name not in s:
                s[name] = sem(name)
            return s[name]

        XT, SUP, QK, QT = [[(k, t) for t in range(T)] for k in ("x_t", "support", "qk", "q_t")]
        uses = [
            ["count", "edges"] + [("adj", g) for g in range(0, NG, 2)]
            + [("expert", i) for i in range(0, 2 * T, 4)],
            ["start", "weights"] + ["covered"] + [("adj", g) for g in range(1, NG, 2)]
            + [("expert", i) for i in range(1, 2 * T, 4)],
            ["two_vt", ("w_in_t", 0), ("w_in_t", 2), "b_qk_row"] + XT + ["k_max_t"]
            + [("x2_t", m) for m in range(0, T, 2)]  + [("expert", i) for i in range(2, 2 * T, 4)],
            [("w_in_t", 1), ("w_in_t", 3), "b_qk"] + QT + ["k_max_b"]
            + [("x2_t", m) for m in range(1, T, 2)]  + [("expert", i) for i in range(3, 2 * T, 4)],
            [("w_vo", 0), ("w_qk", 0)] + SUP[0::2] + [("kxn", 0), "mid_t"] + [("out", m) for m in range(0, T, 4)]
            + ["pooled"] + [("hid", i) for i in range(0, 12, 4)],
            [("w_vo", 1), ("w_qk", 1)] + SUP[1::2] + [("kxn", 1), ("z", 0)] + [("out", m) for m in range(1, T, 4)]
            + ["gates"] + [("hid", i) for i in range(1, 12, 4)],
            [("w_vo", 2), ("w_qk", 2)] + QK[0::2] + ["k_sum", ("kxn_t", 0), ("z", 1)]
            + [("out", m) for m in range(2, T, 4)] + ["score_max", "gates_b"] + [("hid", i) for i in range(2, 12, 4)],
            [("w_vo", 3), ("w_qk", 3)] + QK[1::2] + [("kxn_t", 1)] + [("out", m) for m in range(3, T, 4)] + ["score_b"]
            + [("hid", i) for i in range(3, 12, 4)],
        ]
        turn = {use: (b, n) for b, keys in enumerate(uses) for n, use in enumerate(keys)}
        filled = [sem(f"filled{b}") for b in range(8)]
        drained = [sem(f"drained{b}") for b in range(8)]

        def pt(use):
            return bank[turn[use][0]]

        def wait_free(eng, use):
            b, n = turn[use]
            if n:
                eng.wait_ge(drained[b], n)

        def wait_filled(eng, use):
            b, n = turn[use]
            eng.wait_ge(filled[b], n + 1)

        def wait_drained(eng, use):
            b, n = turn[use]
            eng.wait_ge(drained[b], n + 1)

        def groups_ended(before, after):
            ends = [min((g + 1) * GB, NB) * WIN for g in range(NG)]
            return [g for g in range(NG) if before < ends[g] <= after]

        def slot_tiles(k):
            return Q * sum(SLOTS[:k]), Q * sum(SLOTS[:k + 1])

        g_idx = [sb(f"g_idx{i}", [1, 8], U32) for i in range(1)][0]

        scores = sb("scores", [P, T])
        aw_b = sb("aw_b", [P, D])
        ab_b = sb("ab_b", [P, 1])
        tiny = sb("tiny", [P, 64])
        gw_sb = sb("gw_sb", [P, C, NX])
        gb_row = sb("gb_row", [1, NX])
        pooled = sb("pooled", [P, C])
        gate_b2 = sb("gate_b2", [P, 2])
        neg = sb("neg", [P, 2 * T + 1])
        fade = sb("fade", [P, T, 2])
        pool_sum = sb("pool_sum", [P, 1])
        pool_share = sb("pool_share", [P, 1])

        sup_round = over("sup_round", [P, 2, D], F32R, "q_buf")
        sup_hi = over("sup_hi", [P, T, D], F32R, "support")
        LO_A = (RING * (3 * P + SPAN) + 2 * P) * Q // 2 // D
        sup_lo_a = over("sup_lo_a", [P, LO_A, D], F32R, "hot_space")
        sup_lo_b = over("sup_lo_b", [P, T - LO_A, D], F32R, "w_in_sb")
        assert T - LO_A <= C
        sup_lo = lambda t: sup_lo_a[:, t, :] if t < LO_A else sup_lo_b[:, t - LO_A, :]
        a_hi = over("a_hi", [P, 2, T, P], F32R, "x2_space")
        a_lo = over("a_lo", [P, 2, T, P], F32R, "x2_space", 8 * T * P)
        pooling = over("pooling", [P, 4, D], F32, "w_vo")
        junk, pool_acc, pool_add = pooling[:, 0, :], pooling[:, 1, :], pooling[:, 2:4, :]
        x2_hi = over("x2_hi", [P, C, NP], F32R, "adj_space")
        x2_lo = over("x2_lo", [P, C, NP], F32R, "adj_space", 4 * C * NP)
        assert 2 * C < T
        e_w1 = AT[:, 2 * C:2 * C + 2, 0:C * H].rearrange("p e (c h) -> p e c h", c=C)
        e_w2 = over("e_w2", [P, 2, HC, D], F32, "w_in_sb")
        e_b2 = over("e_b2", [P, 2, D], F32, "w_vo")
        e_b1 = tiny[:, 32:32 + 2 * HC].rearrange("p (e c) -> p e c", e=2)
        w1_hi = over("w1_hi", [P, 2, HC, C, P], F32R, "x2_space")
        w1_lo = over("w1_lo", [P, 2, HC, C, P], F32R, "x2_space", 8 * C * H)
        w2_hi = over("w2_hi", [P, 2, HC, D], F32R, "q_t")
        w2_lo = over("w2_lo", [P, 2, HC, D], F32R, "hot_space")
        hid_hi = over("hid_hi", [P, 2 * HC, NP], F32R, "xn")
        hid_lo = over("hid_lo", [P, 2 * HC, NP], F32R, "support")
        hid = over("hid", [P, 2, 512], F32, "x_t_space")
        pre = over("pre", [P, 4, D], F32, "adj_space")
        post = over("post", [P, 4, D], F32, "adj_space", 16 * D)

        rep_iota = stage[:, 0, 0, 0:P]
        rep_row = stage[:, 0, 1, 0:P]
        rep_col = stage[:, 0, 2, :]
        rep_acc = stage[:, 1, 0, :]
        rep_key, at = carve(hot_space, 0, EP, [EC])
        rep_place, at = carve(hot_space, at, EP, [EC])

        block = ctx.enter_context(nc.Block())

        @block.sync
        def _(sp):
            as_list = lambda a: a.rearrange("(p c) -> p c", p=EP)
            sp.dma_start(dst_all[:], as_list(dst)).then_inc(S("dst_in"), 16)
            sp.wait_ge(S("x_pad"), 1)
            third = T // 3
            for i in range(3):
                sp.dma_start(x_sb[:, third * i:third * (i + 1), :],
                             x[P * third * i:P * third * (i + 1), :].rearrange("(t p) d -> p t d", p=P)
                             ).then_inc(S(f"x_in{i}"), 16)
            sp.dma_start(x_sb[0:TAIL, T - 1, :], x[P * (T - 1):N, :]).then_inc(S("x_tail"), 16)
            sp.dma_start(w_gnn[:], gnn_w.rearrange("(c p) n -> p c n", p=P)).then_inc(S("w_gnn_in"), 16)
            sp.dma_start(src_all[:], as_list(src)).then_inc(S("list_in"), 16)
            sp.dma_start(w_all[:], as_list(edge_weight)).then_inc(S("list_in"), 16)
            sp.dma_start(b_sum[:], gnn_b.partition_broadcast(P)).then_inc(S("b_sum_in"), 16)
            sp.dma_start(b_out_b, b_out.partition_broadcast(P)).then_inc(S("b_sum_in"), 16)
            sp.dma_start(aw_b[:], attn_w.rearrange("d o -> (d o)").partition_broadcast(P)).then_inc(S("gate_in"), 16)
            sp.dma_start(ab_b[:], attn_b.partition_broadcast(P)).then_inc(S("gate_in"), 16)
            sp.dma_start(gw_sb[:], gate_w.rearrange("(c p) e -> p c e", p=P)).then_inc(S("gate_in"), 16)
            sp.dma_start(gb_row[:], gate_b.rearrange("(o e) -> o e", o=1)).then_inc(S("gate_in"), 16)
            for g in range(NG):
                nb = min(GB, NB - g * GB)
                wait_drained(sp, ("adj", g))
                sp.dma_start(adj_blocks[g * GB:g * GB + nb].rearrange("b q l -> q b l"),
                             stage[:, g % 2, 0:nb, :]).then_inc(S(f"adj_out{g % 2}"), 16)
            for half in range(2):
                sp.wait_ge(S(f"adj_out{half}"), 16 * ((NG + 1 - half) // 2))
            sp.wait_ge(S("missing_known"), 1)
            missing = sp.value_load(missing_i[0:1, 0:1], min_val=-NE, max_val=NE)
            with sp.If(missing != 0):
                with sp.Fori(0, NB) as b:
                    sp.wait_ge(S("block_summed"), b + 1)
                    sp.dma_start(adj_blocks[bass.ds(b, 1)].rearrange("b q l -> q (b l)"),
                                 rep_acc[:]).then_inc(S("block_out"), 16)
                sp.wait_ge(S("block_out"), 16 * NB)
            with sp.Else():
                sp.nop()
            for k in range(T):
                sp.dma_start(AT[:, k, :], adj[P * k:P * (k + 1), :]).then_inc(S(f"adj_in{k}"), 16)
            sp.wait_ge(S("chosen"), 1)
            wait_filled(sp, ("out", T - 1))
            for e in range(2):
                ex = sp.value_load(g_idx[0:1, e:e + 1], min_val=0, max_val=NX - 1)
                sp.dma_start(e_w1[:, e], w1[bass.ds(ex, 1)].rearrange("e (c p) h -> p (e c) h", p=P)
                             ).then_inc(S(f"w1_in{e}"), 16)
                sp.dma_start(e_b1[:, e, :], b1[bass.ds(ex, 1)].rearrange("e (p c) -> p (e c)", p=P)
                             ).then_inc(S(f"b1_in{e}"), 16)
                sp.dma_start(e_w2[:, e], w2[bass.ds(ex, 1)].rearrange("e (p c) h -> p (e c) h", p=P)
                             ).then_inc(S(f"w2_in{e}"), 16)
                sp.dma_start(e_b2[:, e, :], b2[bass.ds(ex, 1)].rearrange("e n -> (e n)").partition_broadcast(P)
                             ).then_inc(S(f"b2_in{e}"), 16)
            for m in range(T):
                rows = P if m < T - 1 else TAIL
                sp.wait_ge(S("y_ready"), m + 1)
                sp.dma_start(out[P * m:P * m + rows, :], x_sb[0:rows, m, :]).then_inc(S("y_out"), 16)
            sp.wait_ge(S("y_out"), 16 * T)

        @block.gpsimd
        def _(pool):
            pool.memset(x_sb[:, T - 1, :], 0.0).then_inc(S("x_pad"), 1)
            pool.iota(iota_i[:], [[1, SPAN]], base=0, channel_multiplier=0).then_inc(S("iota_i"), 1)
            pool.iota(part_i[:], [[0, 1]], base=0, channel_multiplier=1).then_inc(S("iota_i"), 1)
            pool.memset(two_qk[:], 0.0).then_inc(S("two_zero"), 1)
            pool.memset(two_v[:], 0.0).then_inc(S("two_zero"), 1)
            pool.memset(ident[:], 0.0).then_inc(S("const0"), 1)
            pool.memset(is_high[:], 0.0).then_inc(S("const0"), 1)
            pool.memset(above_high[:], 1.0).then_inc(S("const0"), 1)
            pool.memset(tail_far[:], 0.0).then_inc(S("const0"), 1)
            pool.wait_ge(S("const0"), 4)
            pool.affine_select(out=ident[:], in_=ident[:], compare_op=ALU.not_equal, fill=1.0, base=0,
                               pattern=[[-1, P]], channel_multiplier=1).then_inc(S("ident"), 1)
            pool.affine_select(out=is_high[:], in_=is_high[:], compare_op=ALU.not_equal, fill=1.0, base=0,
                               pattern=[[1, BH], [0, LOW]], channel_multiplier=-1).then_inc(S("digits"), 1)
            pool.affine_select(out=above_high[:], in_=above_high[:], compare_op=ALU.is_gt, fill=0.0, base=0,
                               pattern=[[1, BH], [0, LOW]], channel_multiplier=-1).then_inc(S("digits"), 1)
            pool.affine_select(out=tail_far[:], in_=tail_far[:], compare_op=ALU.is_ge, fill=FAR, base=TAIL - 1,
                               pattern=[[0, 1]], channel_multiplier=-1).then_inc(S("const"), 1)
            pool.memset(ones[:], 1.0).then_inc(S("const"), 1)
            pool.memset(mid_t[:], 0.0).then_inc(S("const"), 1)
            pool.wait_ge(S("starts"), 1)
            for dst_sb, table in ((dst_w, dst), (src_w, src), (wgt_w, edge_weight)):
                pool.indirect_dma_start(out=dst_sb[:], out_offset=None, in_=table.rearrange("(e o) -> e o", o=1),
                                        in_offset=bass.IndirectOffsetOnAxis(ap=start_u[:], axis=0)
                                        ).then_inc(S("window_in"), 16)
            pool.wait_ge(S("b_sum_in"), 32)
            pool.tensor_tensor(b_sum[:], b_sum[:], b_out_b, ALU.add).then_inc(S("b_sum"), 1)
            pool.wait_ge(S("b_sum"), 1)
            pool.wait_ge(S("normed"), T)
            for t in range(T):
                pool.tensor_tensor(x_sb[:, t, :], x_sb[:, t, :], b_sum[:], ALU.add).then_inc(S("x_biased"), 1)

        @block.tensor
        def _(pe):
            mm = nc.tensor.matmul

            def end(ins, use):
                ins.then_inc(filled[turn[use][0]], 1)

            pe.wait_ge(S("list_hot"), 2)
            for c in range(EC):
                last = mm(pt("count")[0:BH, 0:LOW + 1], hot_hi[:, c, :], below_lo[:, c, :],
                          start=(c == 0), stop=(c == EC - 1))
            end(last, "count")
            pe.wait_ge(S("digits"), 2)
            wait_drained(pe, "count")
            mm(pt("start")[0:NB, 0:LOW + 1], is_high[:].rearrange("h a b -> h (a b)"), count_sb[:],
               start=True, stop=True)
            end(mm(pt("start")[0:NB, 16:17], above_high[:].rearrange("h a b -> h (a b)"),
                   count_sb[:, LOW:LOW + 1], start=True, stop=True), "start")
            pe.wait_ge(S("ident"), 1)
            pe.wait_ge(S("two_in"), 16 * 6)
            wait_free(pe, "two_vt")
            end(nc.tensor.transpose(pt("two_vt")[:, 0:P], two_v[:], ident[:]), "two_vt")
            pe.wait_ge(S("w_in_in"), 16)
            for p in range(C):
                wait_free(pe, ("w_in_t", p))
                for c in range(C):
                    last = nc.tensor.transpose(pt(("w_in_t", p))[:, P * c:P * c + P],
                                               w_in_sb[:, c, P * p:P * p + P], ident[:])
                end(last, ("w_in_t", p))
            pe.wait_ge(S("const"), 3)
            wait_drained(pe, "two_vt")
            pe.wait_ge(S("w_out_in"), 16)
            for p in range(C):
                end(mm(pt(("w_vo", p))[:], two_vt[:], w_out_sb[:, p, :], start=True, stop=True), ("w_vo", p))
            for m in range(C):
                wait_free(pe, ("w_qk", m))
                view = pt(("w_qk", m))[:].rearrange("p (k n) -> p k n", k=2)
                for p in range(C):
                    wait_drained(pe, ("w_in_t", p))
                    last = mm(view[:, :, 2 * SL * p:2 * SL * (p + 1)], w_in_t[:, p, P * m:P * m + P],
                              two_qk[:].rearrange("p k h s -> p k (h s)"), start=True, stop=True)
                end(last, ("w_qk", m))
            wait_free(pe, "b_qk_row")
            pe.wait_ge(S("b_in_in"), 16)
            view = pt("b_qk_row")[:].rearrange("p (k n) -> p k n", k=2)
            for p in range(C):
                last = mm(view[0:1, :, 2 * SL * p:2 * SL * (p + 1)], b_in_col[:, p:p + 1],
                          two_qk[:].rearrange("p k h s -> p k (h s)"), start=True, stop=True)
            end(last, "b_qk_row")
            wait_drained(pe, "b_qk_row")
            wait_free(pe, "b_qk")
            end(mm(pt("b_qk")[:], ones[0:1, :], b_qk_row[:], start=True, stop=True), "b_qk")
            pe.wait_ge(S("window_keys"), 3)
            wait_free(pe, "edges")
            for a, w in enumerate((key_w, place_w)):
                for c in range(WIN):
                    col = (a * WIN + c) * NB
                    last = nc.tensor.transpose(pt("edges")[:, col:col + NB], w[:, P * c:P * c + P], ident[0:NB, 0:NB])
            end(last, "edges")
            wait_free(pe, "weights")
            for c in range(WIN):
                last = nc.tensor.transpose(pt("weights")[:, NB * c:NB * c + NB], wgt_w[:, P * c:P * c + P],
                                           ident[0:NB, 0:NB])
            end(last, "weights")
            wait_free(pe, "covered")
            end(mm(pt("covered")[0:1, 0:1], covered[:], ones[0:NB, 0:1], start=True, stop=True), "covered")

            def adj_signal(a, b):
                for n in range(a, b):
                    blk, c = n // WIN, n % WIN
                    g, within = blk // GB, blk % GB
                    if within == 0 and c == 0:
                        wait_free(pe, ("adj", g))
                    pe.wait_ge(S("hot_ready"), n // Q + 1)
                    slot, i = n // Q % RING, n % Q
                    for k in range(3):
                        last = mm(pt(("adj", g))[:, SPAN * within:SPAN * (within + 1)], hot_row[:, slot, k, :, i],
                                  hot_col[:, slot, :, i], start=(c == 0 and k == 0),
                                  stop=(c == WIN - 1 and k == 2))
                    if c == WIN - 1 and (within == GB - 1 or blk == NB - 1):
                        end(last, ("adj", g))
                    elif i == Q - 1:
                        last.then_inc(S("hot_used"), 1)

            def turn_q(t):
                wait_free(pe, ("q_t", t))
                pe.wait_ge(S("q_ready"), t + 1)
                for h in range(2):
                    last = nc.tensor.transpose(pt(("q_t", t))[:, P * h:P * h + P],
                                               q_buf[:, t % 4, P * h:P * h + P], ident[:])
                end(last, ("q_t", t))

            pe.wait_ge(S("w_gnn_in"), 16)
            for t in range(T + 2):
                if t < T:
                    wait_free(pe, ("x_t", t))
                    pe.wait_ge(S("normed"), t + 1)
                    for c in range(C):
                        last = nc.tensor.transpose(pt(("x_t", t))[:, P * c:P * c + P],
                                                   xn[:, t, P * c:P * c + P], ident[:])
                    end(last, ("x_t", t))
                    adj_signal(*slot_tiles(3 * t))
                    wait_drained(pe, ("x_t", t))
                    wait_free(pe, ("support", t))
                    for c in range(C):
                        last = mm(pt(("support", t))[:], x_t[:, t % 2, c, :], w_gnn[:, c, :],
                                  start=(c == 0), stop=(c == C - 1))
                    end(last, ("support", t))
                    adj_signal(*slot_tiles(3 * t + 1))
                    wait_free(pe, ("qk", t))
                    if t == 0:
                        for m in range(C):
                            wait_drained(pe, ("w_qk", m))
                    for c in range(C):
                        last = mm(pt(("qk", t))[:], x_t[:, t % 2, c, :], w_qk[:, c, :],
                                  start=(c == 0), stop=(c == C - 1))
                    end(last, ("qk", t))
                    adj_signal(*slot_tiles(3 * t + 2))
                if t >= 2:
                    turn_q(t - 2)

            wait_free(pe, "k_max_t")
            pe.wait_ge(S("k_max"), 1)
            for h in range(2):
                last = nc.tensor.transpose(pt("k_max_t")[:, P * h:P * h + P], k_max[:, P * h:P * h + P], ident[:])
            end(last, "k_max_t")
            adj_signal(*slot_tiles(3 * T))
            wait_free(pe, "k_max_b")
            pe.wait_ge(S("k_diag"), 2)
            end(mm(pt("k_max_b")[:, 0:2 * P], ones[:], k_diag[:].rearrange("p h n -> p (h n)"),
                   start=True, stop=True), "k_max_b")
            adj_signal(*slot_tiles(3 * T + 1))
            pe.wait_ge(S("k_exp"), 1)
            for h in range(2):
                wait_free(pe, ("kxn", h))
                for t in range(T):
                    last = mm(pt(("kxn", h))[:], k_sb[:, t, P * h:P * h + P], xn[:, t, :],
                              start=(t == 0), stop=(t == T - 1))
                    if t == T - 1:
                        end(last, ("kxn", h))
                    if t % (T // 2) == T // 2 - 1:
                        adj_signal(*slot_tiles(3 * T + 2 + 2 * h + t // (T // 2)))

            pe.wait_ge(S("missing_known"), 1)
            wait_drained(pe, ("adj", NG - 1))
            wait_drained(pe, ("adj", NG - 2))
            missing = pe.value_load(missing_i[0:1, 0:1], min_val=-NE, max_val=NE)
            with pe.If(missing != 0):
                with pe.Fori(0, NB * EC) as n:
                    pe.wait_ge(S("rep_hot"), n + 1)
                    mm(bank[0][:, 0:SPAN], rep_row[:], rep_col[:], start=True, stop=True).then_inc(S("rep_done"), 1)
            with pe.Else():
                pe.nop()

            wait_free(pe, "k_sum")
            for t in range(T):
                last = mm(pt("k_sum")[:, 0:2 * P], ones[:], k_sb[:, t, :], start=(t == 0), stop=(t == T - 1))
            end(last, "k_sum")
            for i in range(2):
                wait_free(pe, ("kxn_t", i))
                for h in range(2):
                    wait_drained(pe, ("kxn", h))
                    for j in range(2):
                        c = 2 * i + j
                        last = nc.tensor.transpose(pt(("kxn_t", i))[:, (2 * j + h) * P:(2 * j + h + 1) * P],
                                                   kxn[:, h, P * c:P * c + P], ident[:])
                end(last, ("kxn_t", i))
            wait_free(pe, "mid_t")
            for i in range(2):
                wait_drained(pe, ("kxn_t", i))
            for p in range(C):
                for c in range(C):
                    last = mm(pt("mid_t")[:, P * p:P * p + P], w_in_sb[:, c, P * p:P * p + P],
                              kxn_t[:, c, p // 2, :], start=(c == 0), stop=(c == C - 1))
            end(last, "mid_t")
            wait_drained(pe, "mid_t")
            for h in range(2):
                wait_free(pe, ("z", h))
                for j in range(2):
                    last = mm(pt(("z", h))[:], mid_t[:, 2 * h + j, :], w_vo[:, 2 * h + j, :],
                              start=(j == 0), stop=(j == 1))
                end(last, ("z", h))

            def turn_x2(m):
                wait_free(pe, ("x2_t", m))
                pe.wait_ge(S("normed2"), m + 1)
                for c in range(C):
                    last = nc.tensor.transpose(pt(("x2_t", m))[:, P * c:P * c + P],
                                               xn[:, m, P * c:P * c + P], ident[:])
                end(last, ("x2_t", m))

            for m in range(T + 2):
                if m < T:
                    wait_free(pe, ("out", m))
                    if m:
                        pe.wait_ge(S("a_lo"), T + m)
                    for k in range(T):
                        if m == 0:
                            pe.wait_ge(S("a_lo"), k + 1)
                            pe.wait_ge(S("sup_hi"), k + 1)
                        hi, lo = a_hi[:, m % 2, k, :], a_lo[:, m % 2, k, :]
                        mm(pt(("out", m))[:], hi, sup_hi[:, k, :], start=(k == 0), stop=False)
                        mm(pt(("out", m))[:], hi, sup_lo(k), start=False, stop=False)
                        mm(pt(("out", m))[:], lo, sup_hi[:, k, :], start=False, stop=False)
                    if m == 0:
                        wait_drained(pe, ("q_t", T - 1))
                    for h in range(2):
                        if m == 0:
                            wait_drained(pe, ("z", h))
                        last = mm(pt(("out", m))[:], q_t[:, h, P * m:P * m + P], z_sb[:, h, :],
                                  start=False, stop=(h == 1))
                    end(last, ("out", m))
                if m >= 2:
                    turn_x2(m - 2)

            wait_free(pe, "score_max")
            pe.wait_ge(S("score_top"), T)
            end(nc.tensor.transpose(pt("score_max")[0:1, 0:P], neg[:, 2 * T:2 * T + 1], ident[:]), "score_max")
            wait_drained(pe, "score_max")
            wait_free(pe, "score_b")
            end(mm(pt("score_b")[:, 0:1], ones[0:1, :], tiny[0:1, 1:2], start=True, stop=True), "score_b")
            pe.wait_ge(S("pool_share"), 1)
            pe.wait_ge(S("pool_added"), 2 * T - 2)
            wait_free(pe, "pooled")
            for c in range(C):
                mm(pt("pooled")[:, c:c + 1], pool_acc[:, P * c:P * c + P], pool_share[:], start=True, stop=True)
            end(mm(pt("pooled")[0:1, 8:9], pool_share[:], pool_sum[:], start=True, stop=True), "pooled")
            wait_drained(pe, "pooled")
            wait_free(pe, "gates")
            for c in range(C):
                last = mm(pt("gates")[0:1, 0:NX], pooled[:, c:c + 1], gw_sb[:, c, :], start=(c == 0), stop=(c == C - 1))
            end(last, "gates")
            for i in range(12):
                e, half, chunk = i // 6, i // 3 % 2, i % 3
                n0, n1 = 512 * chunk, min(512 * (chunk + 1), NP)
                wait_free(pe, ("hid", i))
                if i % 6 == 0:
                    for m in (T - 1, T - 2):
                        wait_drained(pe, ("x2_t", m))
                for w, x2 in ((w1_hi, x2_hi), (w1_hi, x2_lo), (w1_lo, x2_hi)):
                    if w is w1_hi and x2 is x2_hi:
                        pe.wait_ge(S("w1_hi"), 2 * e + half + 1)
                    if w is w1_lo:
                        pe.wait_ge(S("w1_lo"), 2 * e + half + 1)
                    for c in range(C):
                        last = mm(pt(("hid", i))[:, 0:n1 - n0], w[:, e, half, c, :], x2[:, c, n0:n1],
                                  start=(w is w1_hi and x2 is x2_hi and c == 0), stop=(w is w1_lo and c == C - 1))
                end(last, ("hid", i))
                if i == 1:
                    pe.wait_ge(S("shares"), 1)
                    wait_free(pe, "gates_b")
                    end(mm(pt("gates_b")[:, 0:2], ones[0:1, :], tiny[0:1, 24:26], start=True, stop=True), "gates_b")
            for m in range(T):
                for e in range(2):
                    use = ("expert", 2 * m + e)
                    wait_free(pe, use)
                    if m == 0:
                        pe.wait_ge(S("w2_hi"), e + 1)
                        pe.wait_ge(S("w2_lo"), e + 1)
                        pe.wait_ge(S("hid_lo"), 6 * e + 6)
                    for a, w in ((hid_hi, w2_hi), (hid_lo, w2_hi), (hid_hi, w2_lo)):
                        for c in range(HC):
                            last = mm(pt(use)[:], a[:, HC * e + c, P * m:P * m + P], w[:, e, c, :],
                                      start=(a is hid_hi and w is w2_hi and c == 0),
                                      stop=(w is w2_lo and c == HC - 1))
                    end(last, use)

        @block.scalar
        def _(act):
            cp = nc.scalar.copy

            def drain(use, out_ap, in_ap):
                wait_filled(act, use)
                cp(out_ap, in_ap).then_inc(drained[turn[use][0]], 1)

            def drain_x2(m):
                wait_filled(act, ("x2_t", m))
                cp(x2_hi[:, :, P * m:P * m + P], pt(("x2_t", m))[:].rearrange("p (c n) -> p c n", c=C)
                   ).then_inc(S("x2_hi"), 1)

            def pool_tile(t):
                if t == 0:
                    return
                act.wait_ge(S("score_top"), t + 1)
                nc.scalar.activation(fade[:, t, :], neg[:, 2 * t:2 * t + 2], ACT.Exp, bias=neg[:, 2 * t + 2:2 * t + 3],
                                     scale=-1.0).then_inc(S("fade"), 1)
                act.wait_ge(S("fade"), t)
                if t >= 3:
                    act.wait_ge(S("pool_added"), 2 * (t - 2))
                nc.scalar.activation(pool_add[:, t % 2, :], xn[:, t, :], ACT.Identity, scale=fade[:, t, 1:2]
                                     ).then_inc(S("pool_add"), 1)

            act.dma_start(w_in_sb[:], w_in.rearrange("(c p) n -> p c n", p=P)).then_inc(S("w_in_in"), 16)
            act.wait_ge(S("two_zero"), 2)
            for i in range(2):
                act.dma_start(two_qk[HD * i:HD * i + HD, 0, i, :], wq).then_inc(S("two_in"), 16)
                act.dma_start(two_qk[HD * i:HD * i + HD, 1, i, :], wk).then_inc(S("two_in"), 16)
                act.dma_start(two_v[HD * i:HD * i + HD, HD * i:HD * i + HD], wv).then_inc(S("two_in"), 16)
            act.dma_start(w_out_sb[:], w_out.rearrange("(c p) n -> p c n", p=P)).then_inc(S("w_out_in"), 16)
            act.dma_start(b_in_col[:], b_in.rearrange("(c p) -> p c", p=P),
                          allow_slow_non_contiguous=True).then_inc(S("b_in_in"), 16)

            drain("two_vt", two_vt[:], pt("two_vt")[:, 0:P])
            for p in range(C):
                drain(("w_in_t", p), w_in_t[:, p, :], pt(("w_in_t", p))[:])
            act.wait_ge(S("variances"), 1)
            act.wait_ge(S("eps"), 1)
            nc.scalar.activation(spread[:], moments[:, :, 1], ACT.Sqrt, bias=eps[:]).then_inc(S("spread"), 1)
            for p in range(C):
                drain(("w_vo", p), w_vo[:, p, :], pt(("w_vo", p))[:])
            for m in range(C):
                drain(("w_qk", m), w_qk[:, m, :], pt(("w_qk", m))[:])
            drain("b_qk_row", b_qk_row[:], pt("b_qk_row")[0:1, :])
            drain("b_qk", b_qk[:], pt("b_qk")[:])

            def groups(k):
                for g in groups_ended(*slot_tiles(k)):
                    nb = min(GB, NB - g * GB)
                    if g >= 2:
                        act.wait_ge(S(f"adj_out{g % 2}"), 16 * (g // 2))
                    drain(("adj", g), stage[:, g % 2, 0:nb, :].rearrange("p b l -> p (b l)"),
                          pt(("adj", g))[:, 0:nb * SPAN])

            for t in range(T + 2):
                if t < T:
                    if t >= 2:
                        wait_filled(act, ("qk", t - 2))
                    drain(("x_t", t), x_t[:, t % 2].rearrange("p c n -> p (c n)"), pt(("x_t", t))[:])
                    groups(3 * t)
                    drain(("support", t), support[:, t, :], pt(("support", t))[:])
                    groups(3 * t + 1)
                    groups(3 * t + 2)
                if 1 <= t <= T:
                    act.wait_ge(S("q_less"), t)
                    nc.scalar.activation(q_buf[:, (t - 1) % 4, :], q_buf[:, (t - 1) % 4, :], ACT.Exp
                                         ).then_inc(S("q_exp"), 1)
                if t >= 2:
                    wait_filled(act, ("q_t", t - 2))
                    cp(q_t[:, :, P * (t - 2):P * (t - 1)],
                       pt(("q_t", t - 2))[:, 0:2 * P].rearrange("p (h n) -> p h n", h=2)
                       ).then_inc(drained[turn[("q_t", t - 2)][0]], 1)
            groups(3 * T)
            groups(3 * T + 1)
            act.wait_ge(S("k_less"), 1)
            nc.scalar.activation(k_sb[:], k_sb[:], ACT.Exp).then_inc(S("k_exp"), 1)
            for k in range(3 * T + 2, len(SLOTS)):
                groups(k)
            act.wait_ge(S("b_sum"), 1)
            for h in range(2):
                drain(("kxn", h), kxn[:, h, :], pt(("kxn", h))[:])
            def round_support(a, b):
                for t in range(a, b + 1):
                    if t < b:
                        if t >= 2:
                            act.wait_ge(S("sup_hi"), t - 1)
                        cp(sup_round[:, t % 2, :], support[:, t, :]).then_inc(S("sup_round"), 1)
                    if t > a:
                        act.wait_ge(S("sup_lo"), t)
                        cp(sup_hi[:, t - 1, :], sup_round[:, (t - 1) % 2, :].bitcast(F32)).then_inc(S("sup_hi"), 1)

            def round_a(m):
                if m == 0:
                    wait_filled(act, "mid_t")
                    for k in range(T):
                        act.wait_ge(S(f"adj_in{k}"), 16)
                        cp(a_hi[:, 0, k, :], AT[:, k, 0:P]).then_inc(S("a_hi"), 1)
                else:
                    if m >= 2:
                        wait_filled(act, ("out", m - 2))
                    cp(a_hi[:, m % 2], AT[:, :, P * m:P * m + P]).then_inc(S("a_hi"), 1)

            for t in (T - 1, T - 2):
                wait_drained(act, ("support", t))
            wait_drained(act, ("q_t", T - 1))
            round_support(0, LO_A)
            for h in range(2):
                drain(("z", h), z_sb[:, h, :], pt(("z", h))[:])
            round_support(LO_A, T)
            round_a(0)
            for m in range(T):
                if m + 1 < T:
                    round_a(m + 1)
                act.wait_ge(S("moments2"), m + 1)
                nc.scalar.activation(spread[:, m:m + 1], moments[:, m, 1:2], ACT.Sqrt, bias=eps[:]
                                     ).then_inc(S("spread2"), 1)
                if m >= 2:
                    drain_x2(m - 2)
                    pool_tile(m - 2)
            pool_tile(T - 2)
            drain_x2(T - 2)
            drain_x2(T - 1)
            pool_tile(T - 1)
            act.wait_ge(S("score_far"), 1)
            nc.scalar.activation(pool_share[:], neg[:, 2 * T:2 * T + 1], ACT.Exp, bias=tiny[:, 2:3], scale=-1.0
                                 ).then_inc(S("pool_share"), 1)
            act.wait_ge(S("gate_less"), 1)
            nc.scalar.activation(tiny[0:1, 8:8 + NX], tiny[0:1, 8:8 + NX], ACT.Exp, accum_out=tiny[0:1, 5:6]
                                 ).then_inc(S("gate_exp"), 1)
            nc.scalar.activation(tiny[0:1, 16:18], tiny[0:1, 16:18], ACT.Exp).then_inc(S("gate_exp"), 1)
            def round_w1(e):
                act.wait_ge(S(f"w1_in{e}"), 16)
                for half in range(HC):
                    cp(w1_hi[:, e, half], e_w1[:, e, :, half:H:HC]).then_inc(S("w1_hi"), 1)

            def round_w2(e):
                act.wait_ge(S(f"w2_in{e}"), 16)
                cp(w2_hi[:, e], e_w2[:, e]).then_inc(S("w2_hi"), 1)

            round_w1(0)
            for i in range(12):
                e, half, chunk = i // 6, i // 3 % 2, i % 3
                n0, n1 = 512 * chunk, min(512 * (chunk + 1), NP)
                wait_filled(act, ("hid", i))
                if i % 6 == 0:
                    act.wait_ge(S(f"b1_in{e}"), 16)
                if i >= 2:
                    act.wait_ge(S("hid_lo"), i - 1)
                nc.scalar.activation(hid[:, i % 2, 0:n1 - n0], pt(("hid", i))[:, 0:n1 - n0], ACT.Gelu,
                                     bias=e_b1[:, e, half:half + 1]).then_inc(drained[turn[("hid", i)][0]], 1)
                wait_drained(act, ("hid", i))
                cp(hid_hi[:, HC * e + half, n0:n1], hid[:, i % 2, 0:n1 - n0]).then_inc(S("hid_hi"), 1)
                if i == 1:
                    round_w1(1)
                if i in (3, 5):
                    round_w2(i // 4)
            for i in range(2 * T):
                act.wait_ge(S("pre"), i + 1)
                if i >= 4:
                    act.wait_ge(S("y_ready"), (i - 4) // 2 + 1)
                nc.scalar.activation(post[:, i % 4, :], pre[:, i % 4, :], ACT.Gelu).then_inc(S("post"), 1)

        @block.vector
        def _(v):
            link_count = [0]

            def link(ins):
                link_count[0] += 1
                ins.then_inc(S("v_link"), 1)
                v.wait_ge(S("v_link"), link_count[0])

            tt, ts, tr = nc.vector.tensor_tensor, nc.vector.tensor_scalar, nc.vector.tensor_reduce
            v.memset(eps[:], EPS).then_inc(S("eps"), 1)
            v.wait_ge(S("dst_in"), 16)
            link(ts(hi_i[:], dst_all[:], 7, None, ALU.logical_shift_right))
            link(ts(lo_i[:], dst_all[:], 4, 7, ALU.logical_shift_right, ALU.bitwise_and))
            link(nc.vector.tensor_copy(hi_h[:], hi_i[:]))
            v.wait_ge(S("iota_i"), 2)
            nc.vector.tensor_copy(iota_h[:], iota_i[:]).then_inc(S("iota_h"), 1)
            v.wait_ge(S("iota_h"), 1)
            link(nc.vector.tensor_copy(lo_h[:], lo_i[:]))
            tt(hot_hi[:], hi_h[:].unsqueeze(2).to_broadcast([EP, EC, BH]),
               iota_h[0:EP, 0:BH].unsqueeze(1).to_broadcast([EP, EC, BH]), ALU.is_equal).then_inc(S("list_hot"), 1)
            tt(below_lo[:], lo_h[:].unsqueeze(2).to_broadcast([EP, EC, LOW + 1]),
               iota_h[0:EP, 0:LOW + 1].unsqueeze(1).to_broadcast([EP, EC, LOW + 1]), ALU.is_lt
               ).then_inc(S("list_hot"), 1)
            nc.vector.tensor_copy(iota_q[:], iota_i[:].unsqueeze(2).to_broadcast([P, SPAN, Q]))
            link(nc.vector.tensor_copy(part_f[:], part_i[:]))
            link(ts(low_i[:], part_i[:], LOW - 1, None, ALU.bitwise_and))
            link(nc.vector.tensor_copy(low_f[:], low_i[:]))
            link(ts(low_mask[:], iota_h[:, 0:LOW], low_f[:], None, ALU.is_equal))
            link(ts(base_f[:], part_f[:], float(P), None, ALU.mult))

            def moments_of(t):
                link(nc.vector.bn_stats(stats[:, t, :], x_sb[:, t, :]))
                return nc.vector.bn_aggr(moments[:, t, :], stats[:, t, :])

            v.wait_ge(S("x_in0"), 16)
            for t in range(2):
                link(moments_of(t))
            wait_filled(v, "count")
            nc.vector.tensor_copy(count_sb[:], pt("count")[0:BH, 0:LOW + 1]).then_inc(drained[0], 1)
            wait_filled(v, "start")
            link(tt(start_parts[:], pt("start")[0:NB, 0:LOW], low_mask[0:NB, :], ALU.mult))
            link(tr(start_f[:, 0:1], start_parts[:], AX.X, ALU.add))
            tt(start_f[:, 1:2], start_f[:, 0:1], pt("start")[0:NB, 16:17], ALU.add).then_inc(drained[1], 1)
            wait_drained(v, "start")
            ts(start_u[:], start_f[:, 1:2], float(NE - WE), None, ALU.min).then_inc(S("starts"), 1)
            for t in range(2, T):
                if t % 3 == 0 and t < T - 1:
                    v.wait_ge(S(f"x_in{t // 3}"), 16)
                if t == T - 1:
                    v.wait_ge(S("x_tail"), 16)
                ins = moments_of(t)
                if t < T - 1:
                    link(ins)
                else:
                    ins.then_inc(S("variances"), 1)
            v.wait_ge(S("variances"), 1)
            v.wait_ge(S("spread"), 1)
            link(nc.vector.reciprocal(rstd[:], spread[:]))
            for t in range(T):
                ts(xn[:, t, :], x_sb[:, t, :], moments[:, t, 0:1], rstd[:, t:t + 1], ALU.subtract, ALU.mult
                   ).then_inc(S("normed"), 1)
            v.wait_ge(S("window_in"), 48)
            link(ts(t_i[:, 0, :], dst_w[:], 3, None, ALU.logical_shift_left))
            link(ts(t_i[:, 3, :], src_w[:], float(BY_SPAN), None, ALU.mult))
            link(ts(t_i[:, 1, :], t_i[:, 3, :], 21, None, ALU.logical_shift_right))
            link(tt(t_i[:, 2, :], t_i[:, 0, :], t_i[:, 1, :], ALU.bitwise_or))
            ts(key_w[:], t_i[:, 2, :], base_f[0:NB, :], None, ALU.subtract).then_inc(S("window_keys"), 1)
            nc.vector.scalar_tensor_tensor(out=place_w[:], in0=t_i[:, 1, :], scalar=float(-SPAN), in1=src_w[:],
                                           op0=ALU.mult, op1=ALU.add).then_inc(S("window_keys"), 1)
            link(ts(t_i[:, 0, :], dst_w[:], 4, None, ALU.logical_shift_right))
            link(ts(t_i[:, 1, :], t_i[:, 0, :], part_f[0:NB, :], None, ALU.is_equal))
            tr(covered[:], t_i[:, 1, :], AX.X, ALU.add).then_inc(S("window_keys"), 1)
            wait_filled(v, "edges")
            by_tile = lambda a: a.rearrange("p (c b) -> p c b", c=WIN)
            to_tile = lambda a: a.rearrange("p (b c) -> p c b", c=WIN)
            link(nc.vector.tensor_copy(to_tile(key_h[:]), by_tile(pt("edges")[:, 0:NT])))
            nc.vector.tensor_copy(to_tile(place_h[:]), by_tile(pt("edges")[:, NT:2 * NT])).then_inc(drained[0], 1)
            wait_drained(v, "edges")
            wait_filled(v, "weights")
            wgt = by_tile(pt("weights")[:, 0:NT])
            rest = by_tile(wgt_r)
            link(nc.vector.tensor_copy(to_tile(wgt_b[:, 0, :]), wgt))
            tt(rest, wgt, to_tile(wgt_b[:, 0, :]), ALU.subtract).then_inc(drained[1], 1)
            wait_drained(v, "weights")
            link(nc.vector.tensor_copy(to_tile(wgt_b[:, 1, :]), rest))
            link(tt(to_tile(wgt_b[:, 2, :]), rest, to_tile(wgt_b[:, 1, :]), ALU.subtract))
            wait_filled(v, "covered")
            link(ts(tiny[0:1, 60:61], pt("covered")[0:1, 0:1], -1.0, float(NE), ALU.mult, ALU.add))
            nc.vector.tensor_copy(missing_i[:], tiny[0:1, 60:61]).then_inc(drained[1], 1)
            wait_drained(v, "covered")
            v.sem_inc(S("missing_known"), 1)

            def edge_tiles(a, b):
                for lot in range(a // Q, b // Q):
                    slot, tiles = lot % RING, slice(Q * lot, Q * (lot + 1))
                    if lot >= RING:
                        ends = [min((g + 1) * GB, NB) * WIN for g in range(NG)]
                        used = Q * (lot - RING + 1)
                        if used in ends:
                            wait_filled(v, ("adj", ends.index(used)))
                        else:
                            v.wait_ge(S("hot_used"), sum(n not in ends for n in range(Q, used + 1, Q)))
                    tt(hot_key[:, lot % 2], key_h[:, tiles].unsqueeze(1).to_broadcast([P, P, Q]), iota_q[:, 0:P, :],
                       ALU.is_equal).then_inc(S("hot_key"), 1)
                    tt(hot_col[:, slot], place_h[:, tiles].unsqueeze(1).to_broadcast([P, SPAN, Q]), iota_q[:],
                       ALU.is_equal)
                    v.wait_ge(S("hot_key"), lot + 1)
                    tt(hot_row[:, slot], hot_key[:, lot % 2].unsqueeze(1).to_broadcast([P, 3, P, Q]),
                       wgt_b[:, :, tiles].unsqueeze(2).to_broadcast([P, 3, P, Q]), ALU.mult
                       ).then_inc(S("hot_ready"), 1)

            def softmax_q(t):
                wait_filled(v, ("qk", t))
                if t == 0:
                    wait_drained(v, "b_qk")
                if t >= 4:
                    wait_filled(v, ("q_t", t - 4))
                link(tt(q_buf[:, t % 4, :], pt(("qk", t))[:, 0:D // 2], b_qk[:, 0:D // 2], ALU.add))
                tt(k_sb[:, t, :], pt(("qk", t))[:, D // 2:D], b_qk[:, D // 2:D], ALU.add
                   ).then_inc(drained[turn[("qk", t)][0]], 1)
                q = q_buf[:, t % 4, :].rearrange("p (h s) -> p h s", h=NH)
                link(tr(q_red[:, t, 0, :], q, AX.X, ALU.max))
                tt(q, q, q_red[:, t, 0, :].unsqueeze(2).to_broadcast([P, NH, SL]), ALU.subtract
                   ).then_inc(S("q_less"), 1)

            def share_q(t):
                v.wait_ge(S("q_exp"), t + 1)
                q = q_buf[:, t % 4, :].rearrange("p (h s) -> p h s", h=NH)
                link(tr(q_red[:, t, 1, :], q, AX.X, ALU.add))
                link(nc.vector.reciprocal(q_red[:, t, 2, :], q_red[:, t, 1, :]))
                tt(q, q, q_red[:, t, 2, :].unsqueeze(2).to_broadcast([P, NH, SL]), ALU.mult
                   ).then_inc(S("q_ready"), 1)

            for t in range(T + 2):
                if t < T:
                    edge_tiles(*slot_tiles(3 * t))
                if 1 <= t <= T:
                    softmax_q(t - 1)
                if t < T:
                    edge_tiles(*slot_tiles(3 * t + 1))
                if t >= 2:
                    share_q(t - 2)
                if t < T:
                    edge_tiles(*slot_tiles(3 * t + 2))

            link(ts(k_sb[:, T - 1, :], k_sb[:, T - 1, :], tail_far[:], None, ALU.add))
            tr(k_max[:], k_sb[:].rearrange("p t n -> p n t"), AX.X, ALU.max).then_inc(S("k_max"), 1)
            edge_tiles(*slot_tiles(3 * T))
            wait_filled(v, "k_max_t")
            tr(k_max_t[:], pt("k_max_t")[:, 0:2 * P].rearrange("p (h n) -> p h n", h=2), AX.X, ALU.max
               ).then_inc(drained[turn["k_max_t"][0]], 1)
            wait_drained(v, "k_max_t")
            for h in range(2):
                ts(k_diag[:, h, :], ident[:], k_max_t[:, h:h + 1], None, ALU.mult).then_inc(S("k_diag"), 1)
            edge_tiles(*slot_tiles(3 * T + 1))
            wait_filled(v, "k_max_b")
            tt(k_sb[:], k_sb[:], pt("k_max_b")[:, 0:2 * P].unsqueeze(1).to_broadcast([P, T, 2 * P]), ALU.subtract
               ).then_inc(drained[turn["k_max_b"][0]], 1)
            wait_drained(v, "k_max_b")
            v.sem_inc(S("k_less"), 1)
            for k in range(3 * T + 2, len(SLOTS)):
                edge_tiles(*slot_tiles(k))

            wait_filled(v, ("adj", NG - 1))
            wait_drained(v, ("adj", NG - 1))
            wait_drained(v, ("adj", NG - 2))
            v.wait_ge(S("list_in"), 32)
            missing = v.value_load(missing_i[0:1, 0:1], min_val=-NE, max_val=NE)
            with v.If(missing != 0):
                for half in range(2):
                    v.wait_ge(S(f"adj_out{half}"), 16 * ((NG + 1 - half) // 2))
                ts(hi_i[:], dst_all[:], 3, None, ALU.logical_shift_left).then_inc(S("rep_v"), 1)
                ts(lo_i[:], src_all[:], float(BY_SPAN), None, ALU.mult).then_inc(S("rep_v"), 1)
                v.wait_ge(S("rep_v"), 2)
                ts(lo_i[:], lo_i[:], 21, None, ALU.logical_shift_right).then_inc(S("rep_v"), 1)
                v.wait_ge(S("rep_v"), 3)
                tt(hi_i[:], hi_i[:], lo_i[:], ALU.bitwise_or).then_inc(S("rep_v"), 1)
                v.wait_ge(S("rep_v"), 4)
                nc.vector.tensor_copy(rep_key, hi_i[:]).then_inc(S("rep_v"), 1)
                nc.vector.scalar_tensor_tensor(out=rep_place, in0=lo_i[:], scalar=float(-SPAN), in1=src_all[:],
                                               op0=ALU.mult, op1=ALU.add).then_inc(S("rep_v"), 1)
                ts(rep_iota, iota_i[:, 0:P], float(-P), None, ALU.add).then_inc(S("rep_v"), 1)
                v.wait_ge(S("rep_v"), 7)
                with v.Fori(0, NB) as b:
                    nc.vector.memset(rep_acc, 0.0).then_inc(S("rep_zero"), 1)
                    v.wait_ge(S("rep_zero"), b + 1)
                    ts(rep_iota, rep_iota, float(P), None, ALU.add).then_inc(S("rep_moved"), 1)
                    with v.Fori(0, EC) as c:
                        v.wait_ge(S("rep_moved"), b + 1)
                        ts(rep_row[0:EP, :], rep_iota[0:EP, :], rep_key[:, bass.ds(c, 1)], None, ALU.is_equal)
                        ts(rep_col[0:EP, :], iota_i[0:EP, :], rep_place[:, bass.ds(c, 1)],
                           w_all[:, bass.ds(c, 1)], ALU.is_equal, ALU.mult).then_inc(S("rep_hot"), 1)
                        v.wait_ge(S("rep_done"), b * EC + c + 1)
                        tt(rep_acc, rep_acc, bank[0][:, 0:SPAN], ALU.add).then_inc(S("rep_added"), 1)
                        v.wait_ge(S("rep_added"), b * EC + c + 1)
                        v.nop()
                    v.sem_inc(S("block_summed"), 1)
                    v.wait_ge(S("block_out"), 16 * b + 16)
                    v.nop()
            with v.Else():
                v.nop()

            wait_filled(v, "k_sum")
            nc.vector.reciprocal(k_inv[:].rearrange("p h n -> p (h n)"), pt("k_sum")[:, 0:2 * P]
                                 ).then_inc(drained[turn["k_sum"][0]], 1)
            wait_drained(v, "k_sum")
            for i in range(2):
                wait_filled(v, ("kxn_t", i))
                tt(kxn_t[:, 2 * i:2 * i + 2], pt(("kxn_t", i))[:].rearrange("p (c h n) -> p c h n", c=2, h=2),
                   k_inv[:].unsqueeze(1).to_broadcast([P, 2, 2, P]), ALU.mult
                   ).then_inc(drained[turn[("kxn_t", i)][0]], 1)
            def rest_support(a, b):
                for t in range(a, b):
                    v.wait_ge(S("sup_round"), t + 1)
                    tt(sup_lo(t), support[:, t, :], sup_round[:, t % 2, :].bitcast(F32), ALU.subtract
                       ).then_inc(S("sup_lo"), 1)

            def rest_a(m):
                if m == 0:
                    for k in range(T):
                        v.wait_ge(S("a_hi"), k + 1)
                        tt(a_lo[:, 0, k, :], AT[:, k, 0:P], a_hi[:, 0, k, :].bitcast(F32), ALU.subtract
                           ).then_inc(S("a_lo"), 1)
                else:
                    v.wait_ge(S("a_hi"), T + m)
                    tt(a_lo[:, m % 2], AT[:, :, P * m:P * m + P], a_hi[:, m % 2].bitcast(F32), ALU.subtract
                       ).then_inc(S("a_lo"), 1)

            rest_support(0, LO_A)
            wait_filled(v, "mid_t")
            v.wait_ge(S("b_in_in"), 16)
            for p in range(C):
                for i in range(2):
                    rows = slice(HD * i, HD * i + HD)
                    col = 2 * SL * (p % 2) + SL * i
                    last = ts(mid_t[rows, p, col:col + SL], pt("mid_t")[rows, P * p + col:P * p + col + SL],
                              b_in_col[rows, p:p + 1], None, ALU.add)
                    if (p, i) == (C - 1, 1):
                        last.then_inc(drained[turn["mid_t"][0]], 1)
                    else:
                        link(last)
            rest_support(LO_A, T)
            rest_a(0)

            def pool_update(t):
                v.wait_ge(S("pool_add"), t)
                if t == 1:
                    before, total = xn[:, 0, :], ones[:, 0:1]
                else:
                    before, total = pool_acc, pool_sum[:]
                    v.wait_ge(S("pool_added"), 2 * (t - 1))
                nc.vector.scalar_tensor_tensor(out=pool_acc, in0=before, scalar=fade[:, t, 0:1],
                                               in1=pool_add[:, t % 2, :], op0=ALU.mult, op1=ALU.add
                                               ).then_inc(S("pool_added"), 1)
                nc.vector.scalar_tensor_tensor(out=pool_sum[:], in0=total, scalar=fade[:, t, 0:1],
                                               in1=fade[:, t, 1:2], op0=ALU.mult, op1=ALU.add
                                               ).then_inc(S("pool_added"), 1)

            def rest_x2(m):
                v.wait_ge(S("x2_hi"), m + 1)
                tt(x2_lo[:, :, P * m:P * m + P], pt(("x2_t", m))[:].rearrange("p (c n) -> p c n", c=C),
                   x2_hi[:, :, P * m:P * m + P].bitcast(F32), ALU.subtract
                   ).then_inc(drained[turn[("x2_t", m)][0]], 1)

            v.wait_ge(S("x_biased"), T)
            v.wait_ge(S("gate_in"), 64)
            for m in range(T + 1):
                if m + 1 < T:
                    rest_a(m + 1)
                if m < T:
                    wait_filled(v, ("out", m))
                    tt(x_sb[:, m, :], x_sb[:, m, :], pt(("out", m))[:], ALU.add
                       ).then_inc(drained[turn[("out", m)][0]], 1)
                    wait_drained(v, ("out", m))
                    moments_of(m).then_inc(S("moments2"), 1)
                if m >= 1:
                    t = m - 1
                    v.wait_ge(S("spread2"), t + 1)
                    v.wait_ge(S("moments2"), t + 1)
                    link(nc.vector.reciprocal(rstd[:, t:t + 1], spread[:, t:t + 1]))
                    ts(xn[:, t, :], x_sb[:, t, :], moments[:, t, 0:1], rstd[:, t:t + 1], ALU.subtract, ALU.mult
                       ).then_inc(S("normed2"), 1)
                    v.wait_ge(S("normed2"), t + 1)
                    link(nc.vector.tensor_tensor_reduce(out=junk, in0=xn[:, t, :], in1=aw_b[:], scale=1.0, scalar=0.0,
                                                        op0=ALU.mult, op1=ALU.add, accum_out=scores[:, t:t + 1]))
                    link(ts(neg[:, 2 * t + 1:2 * t + 2], scores[:, t:t + 1], ab_b[:], -1.0, ALU.add, ALU.mult))
                    if t == T - 1:
                        link(ts(neg[:, 2 * t + 1:2 * t + 2], neg[:, 2 * t + 1:2 * t + 2], tail_far[:], None,
                                ALU.subtract))
                    before = 2 * t if t else 1
                    tt(neg[:, 2 * t + 2:2 * t + 3], neg[:, before:before + 1], neg[:, 2 * t + 1:2 * t + 2], ALU.min
                       ).then_inc(S("score_top"), 1)
                    v.wait_ge(S("score_top"), t + 1)
                    if t >= 2:
                        pool_update(t - 1)
                if 2 <= m < T:
                    rest_x2(m - 2)
            wait_filled(v, "score_max")
            tr(tiny[0:1, 1:2], pt("score_max")[0:1, 0:P], AX.X, ALU.min).then_inc(drained[turn["score_max"][0]], 1)
            pool_update(T - 1)
            wait_filled(v, "score_b")
            nc.vector.tensor_copy(tiny[:, 2:3], pt("score_b")[:, 0:1]).then_inc(drained[turn["score_b"][0]], 1)
            wait_drained(v, "score_b")
            v.sem_inc(S("score_far"), 1)
            rest_x2(T - 2)
            rest_x2(T - 1)
            wait_filled(v, "pooled")
            nc.vector.tensor_copy(pooled[:], pt("pooled")[:, 0:C]).then_inc(S("pooled"), 1)
            nc.vector.reciprocal(tiny[0:1, 4:5], pt("pooled")[0:1, 8:9]).then_inc(drained[turn["pooled"][0]], 1)
            wait_drained(v, "pooled")
            wait_filled(v, "gates")
            nc.vector.scalar_tensor_tensor(out=tiny[0:1, 8:8 + NX], in0=pt("gates")[0:1, 0:NX], scalar=tiny[0:1, 4:5],
                                           in1=gb_row[:], op0=ALU.mult, op1=ALU.add
                                           ).then_inc(drained[turn["gates"][0]], 1)
            wait_drained(v, "gates")
            link(nc.vector.max(tiny[0:1, 16:24], tiny[0:1, 8:8 + NX]))
            nc.vector.max_index(g_idx[:], tiny[0:1, 16:24], tiny[0:1, 8:8 + NX]).then_inc(S("chosen"), 1)
            link(nc.vector.tensor_copy(tiny[0:1, 6:7], tiny[0:1, 16:17]))
            v.wait_ge(S("chosen"), 1)
            ts(tiny[0:1, 8:24], tiny[0:1, 8:24], tiny[0:1, 6:7], None, ALU.subtract).then_inc(S("gate_less"), 1)
            v.wait_ge(S("gate_exp"), 2)
            link(nc.vector.reciprocal(tiny[0:1, 7:8], tiny[0:1, 5:6]))
            link(ts(tiny[0:1, 16:18], tiny[0:1, 16:18], tiny[0:1, 7:8], None, ALU.mult))
            link(tt(tiny[0:1, 26:27], tiny[0:1, 16:17], tiny[0:1, 17:18], ALU.add))
            link(ts(tiny[0:1, 26:27], tiny[0:1, 26:27], 1e-9, None, ALU.add))
            link(nc.vector.reciprocal(tiny[0:1, 27:28], tiny[0:1, 26:27]))
            ts(tiny[0:1, 24:26], tiny[0:1, 16:18], tiny[0:1, 27:28], None, ALU.mult).then_inc(S("shares"), 1)

            def rest_w1(e):
                for half in range(HC):
                    v.wait_ge(S("w1_hi"), 2 * e + half + 1)
                    tt(w1_lo[:, e, half], e_w1[:, e, :, half:H:HC], w1_hi[:, e, half].bitcast(F32), ALU.subtract
                       ).then_inc(S("w1_lo"), 1)

            def rest_w2(e):
                v.wait_ge(S("w2_hi"), e + 1)
                tt(w2_lo[:, e], e_w2[:, e], w2_hi[:, e].bitcast(F32), ALU.subtract).then_inc(S("w2_lo"), 1)

            rest_w1(0)
            for i in range(12):
                e, half, chunk = i // 6, i // 3 % 2, i % 3
                n0, n1 = 512 * chunk, min(512 * (chunk + 1), NP)
                v.wait_ge(S("hid_hi"), i + 1)
                wait_drained(v, ("hid", i))
                tt(hid_lo[:, HC * e + half, n0:n1], hid[:, i % 2, 0:n1 - n0],
                   hid_hi[:, HC * e + half, n0:n1].bitcast(F32), ALU.subtract).then_inc(S("hid_lo"), 1)
                if i == 1:
                    wait_filled(v, "gates_b")
                    nc.vector.tensor_copy(gate_b2[:], pt("gates_b")[:, 0:2]).then_inc(drained[turn["gates_b"][0]], 1)
                    wait_drained(v, "gates_b")
                    rest_w1(1)
                if i in (3, 5):
                    rest_w2(i // 4)

            def combine(m):
                v.wait_ge(S("post"), 2 * m + 2)
                link(nc.vector.scalar_tensor_tensor(out=x_sb[:, m, :], in0=post[:, 2 * m % 4, :], scalar=gate_b2[:, 0:1],
                                                    in1=x_sb[:, m, :], op0=ALU.mult, op1=ALU.add))
                nc.vector.scalar_tensor_tensor(out=x_sb[:, m, :], in0=post[:, (2 * m + 1) % 4, :],
                                               scalar=gate_b2[:, 1:2], in1=x_sb[:, m, :], op0=ALU.mult,
                                               op1=ALU.add).then_inc(S("y_ready"), 1)

            for m in range(T):
                for e in range(2):
                    i = 2 * m + e
                    wait_filled(v, ("expert", i))
                    if m == 0:
                        v.wait_ge(S(f"b2_in{e}"), 16)
                    if i >= 4:
                        v.wait_ge(S("post"), i - 3)
                    tt(pre[:, i % 4, :], pt(("expert", i))[:], e_b2[:, e, :], ALU.add
                       ).then_inc(drained[turn[("expert", i)][0]], 1)
                    wait_drained(v, ("expert", i))
                    v.sem_inc(S("pre"), 1)
                if m >= 1:
                    combine(m - 1)
            combine(T - 1)


_INS = ["x", "src", "dst", "edge_weight", "L0_gnn_weight", "L0_gnn_bias", "L0_mix_W_in", "L0_mix_b_in", "L0_mix_Wq",
        "L0_mix_Wk", "L0_mix_Wv", "L0_mix_W_out", "L0_mix_b_out", "L0_ffn_attn_w", "L0_ffn_attn_b", "L0_ffn_gate_w",
        "L0_ffn_gate_b", "L0_ffn_w1", "L0_ffn_b1", "L0_ffn_w2", "L0_ffn_b2"]


def kernel(**inputs):
    import concourse.bacc as bacc
    from concourse.bass_utils import run_bass_kernel_spmd

    nc = bacc.Bacc("TRN2", target_bir_lowering=False, num_devices=1)
    arrays, args = {}, []
    for name in _INS:
        a = np.ascontiguousarray(inputs[name])
        arrays[f"in_{name}"] = a
        args.append(nc.dram_tensor(f"in_{name}", a.shape, mybir.dt.from_np(a.dtype), kind="ExternalInput").ap())
    shape = tuple(inputs["x"].shape)
    args.append(nc.dram_tensor("out_y", shape, F32, kind="ExternalOutput").ap())
    build(nc, *args)
    r = run_bass_kernel_spmd(nc, [arrays], core_ids=[0])
    return r.results[0]["out_y"]
```

```python
from contextlib import ExitStack

import numpy as np
import concourse.bass as bass
from concourse import mybir

ALU = mybir.AluOpType
ACT = mybir.ActivationFunctionType
AX = mybir.AxisListType
F32, F16, BF16 = mybir.dt.float32, mybir.dt.float16, mybir.dt.bfloat16
I32, U32 = mybir.dt.int32, mybir.dt.uint32
F32R = mybir.dt.float32r

P = 128
EPS = 1e-5
FAR = -1e30


def build(nc, x, src, dst, edge_weight, gnn_w, gnn_b, w_in, b_in, wq, wk, wv, w_out, b_out,
          attn_w, attn_b, gate_w, gate_b, w1, b1, w2, b2, out):
    N, D = x.shape
    NE = src.shape[0]
    HD, SL = wq.shape
    NH = D // HD
    NX, _, H = w1.shape
    T = (N + P - 1) // P
    NP = T * P
    TAIL = N - (T - 1) * P
    C = D // P
    HC = H // P
    RB = 16
    SEG = P // RB
    SPAN = NP // SEG
    BY_SPAN = (1 << 21) // SPAN + 1
    NB = NP // RB
    WIN = 3
    WE = WIN * P
    NT = NB * WIN
    GB = 512 // SPAN
    NG = (NB + GB - 1) // GB
    EP = 125
    EC = NE // EP
    LOW = 8
    BH = NB // LOW
    assert EP * EC == NE and D == 512 and NB <= P and NB % LOW == 0
    assert RB == SEG * 2 and P * N < 1 << 24 and (NP - 1) * BY_SPAN < 1 << 24
    assert all((i * BY_SPAN) >> 21 == i // SPAN for i in range(NP))
    Q = 4
    RING = 3
    SLOTS = [0, 0, 2] + [2, 2, 1] * 2 + [2, 1, 1] * (T - 3) + [2, 1, 5, 5, 4, 3]
    K_PARTS = [(0, 3), (3, 6), (6, T)]
    assert sum(SLOTS) * Q == NT and SLOTS[0] == SLOTS[1] == 0
    assert SLOTS[2] * Q <= GB * WIN

    adj = nc.dram_tensor("adjacency", (NP, NP), F32).ap()
    adj_blocks = adj.rearrange("(b r) (h l) -> b (r h) l", r=RB, h=SEG)

    ctx = ExitStack()
    with ctx:
        place = {}

        def sb(name, shape, dt=F32):
            tensor = ctx.enter_context(nc.sbuf_tensor(name, shape, dt))
            place[name] = nc.sbuf_base - int(np.prod(shape[1:])) * (2 if dt in (F16, BF16) else 4)
            return tensor

        def over(name, shape, dt, space, at=0):
            return nc.alloc_sbuf_tensor_at(name, shape, dt, offset=place[space] + at)

        def sem(name):
            return ctx.enter_context(nc.semaphore(name))

        bank = [ctx.enter_context(nc.psum_tensor(f"bank{i}", [P, 512], F32)) for i in range(8)]

        ident = sb("ident", [P, P])
        ones = sb("ones", [P, P])
        iota_i = sb("iota_i", [P, SPAN], I32)
        iota_h = sb("iota_h", [P, SPAN], F16)
        part_i = sb("part_i", [P, 1], I32)
        low_i = sb("low_i", [P, 1], I32)
        part_f = sb("part_f", [P, 1])
        low_f = sb("low_f", [P, 1])
        base_f = sb("base_f", [P, 1])
        low_mask = sb("low_mask", [P, LOW])
        is_high = sb("is_high", [BH, BH, LOW])
        above_high = sb("above_high", [BH, BH, LOW])
        tail_far = sb("tail_far", [P, 1])
        x_sb = sb("x_sb", [P, T, D])
        xn = sb("xn", [P, T, D])
        sup_hi = sb("sup_hi", [P, T, D], F32R)
        w_in_sb = sb("w_in_sb", [P, C, D])
        w_vo = sb("w_vo", [P, C, D])
        two_qk = sb("two_qk", [P, 2, 2, SL])
        two_v = sb("two_v", [P, P])
        two_vt = sb("two_vt", [P, P])
        b_in_col = sb("b_in_col", [P, C])
        b_qk = sb("b_qk", [P, D])
        b_qk_row = b_qk[0:1, :]
        b_sum = sb("b_sum", [P, D])
        dst_all = sb("dst_all", [EP, EC], I32)
        src_all = sb("src_all", [EP, EC], I32)
        w_all = sb("w_all", [EP, EC])
        hi_i = sb("hi_i", [EP, EC], I32)
        lo_i = sb("lo_i", [EP, EC], I32)
        hi_h = sb("hi_h", [EP, EC], F16)
        lo_h = sb("lo_h", [EP, EC], F16)
        count_sb = sb("count_sb", [BH, LOW + 1])
        start_parts = sb("start_parts", [NB, LOW])
        start_f = sb("start_f", [NB, 2])
        start_u = sb("start_u", [NB, 1], U32)
        wgt_w = sb("wgt_w", [NB, WE])
        covered = sb("covered", [NB, 1])
        missing_i = sb("missing_i", [1, 1], I32)
        key_h = sb("key_h", [P, NT], F16)
        place_h = sb("place_h", [P, NT], F16)
        wgt_b = sb("wgt_b", [P, 3, NT], BF16)
        iota_q = sb("iota_q", [P, SPAN, Q], F16)
        stage = sb("stage", [P, 2, GB, SPAN])
        stats = sb("stats", [P, T, 6])
        moments = sb("moments", [P, T, 2])
        spread = sb("spread", [P, T])
        rstd = sb("rstd", [P, T])
        eps = sb("eps", [P, 1])
        q_buf = sb("q_buf", [P, 4, D // 2])
        q_red = sb("q_red", [P, T, 3, NH])
        q_t = sb("q_t", [P, 2, NP])
        k_max_t = sb("k_max_t", [P, 2])
        k_inv = sb("k_inv", [P, 2, P])
        mid_t = sb("mid_t", [P, C, P])

        def carve(space, at, rows, dims, dt=F32):
            n = int(np.prod(dims))
            words = n if dt in (F32, I32) else (n + 1) // 2
            flat = space[0:rows, at:at + words]
            if dt is not F32:
                flat = flat.bitcast(dt)
            names = [f"d{i}" for i in range(len(dims))]
            view = flat[:, 0:n].rearrange(f"p ({' '.join(names)}) -> p {' '.join(names)}",
                                          **dict(zip(names[1:], dims[1:]))) if len(dims) > 1 else flat
            return view, at + words

        adj_space = sb("adj_space", [P, T * NP])
        AT = adj_space[:].rearrange("p (t n) -> p t n", t=T)
        at = 0
        w_gnn, at = carve(adj_space, at, P, [C, D])
        w_out_sb, at = carve(adj_space, at, P, [C, D])
        w_in_t, at = carve(adj_space, at, P, [C, D])
        at += C * D
        hot_hi, at = carve(adj_space, at, EP, [EC, BH], BF16)
        below_lo, at = carve(adj_space, at, EP, [EC, LOW + 1], BF16)
        dst_w, at = carve(adj_space, at, NB, [WE], I32)
        src_w, at = carve(adj_space, at, NB, [WE], I32)
        t_i, at = carve(adj_space, at, NB, [4, WE], I32)
        key_w, at = carve(adj_space, at, NB, [WE])
        assert at <= T * NP
        x2_space = sb("x2_space", [P, C * NP])
        k_sb, at = carve(x2_space, 0, P, [T, D // 2])
        kxn, at = carve(x2_space, at, P, [2, D])
        kxn_t, at = carve(x2_space, at, P, [C, 2, P])
        place_w, at = carve(x2_space, at, NB, [WE])
        assert at <= C * NP
        hot_space = sb("hot_space", [P, (RING * (3 * P + SPAN) + 2 * P) * Q // 2])
        hot_row, at = carve(hot_space, 0, P, [RING, 3, P, Q], BF16)
        hot_col, at = carve(hot_space, at, P, [RING, SPAN, Q], BF16)
        hot_key, at = carve(hot_space, at, P, [2, P, Q], BF16)
        b_out_b = stage[:].rearrange("p a b n -> p (a b n)")[:, NT:NT + D]
        wgt_r = stage[:].rearrange("p a b n -> p (a b n)")[:, 0:NT]
        x_t_space = sb("x_t_space", [P, 2 * C * P])
        k_diag, at = carve(x_t_space, 0, P, [2, P])
        k_max, at = carve(x_t_space, at, P, [D // 2])

        s = {}

        def S(name):
            if name not in s:
                s[name] = sem(name)
            return s[name]

        XT, SUP, QK, QT = [[(k, t) for t in range(T)] for k in ("x_t", "support", "qk", "q_t")]
        uses = [
            ["count", "edges"] + [("adj", g) for g in range(0, NG, 2)]
            + [("expert", i) for i in range(0, 2 * T, 4)],
            ["start", "weights"] + ["covered"] + [("adj", g) for g in range(1, NG, 2)]
            + [("expert", i) for i in range(1, 2 * T, 4)],
            ["two_vt", ("w_in_t", 0), ("w_in_t", 2), "b_qk_row"] + XT + ["k_max_t"]
            + [("x2_t", m) for m in range(0, T, 2)]  + [("expert", i) for i in range(2, 2 * T, 4)],
            [("w_in_t", 1), ("w_in_t", 3), "b_qk"] + QT + ["k_max_b"]
            + [("x2_t", m) for m in range(1, T, 2)]  + [("expert", i) for i in range(3, 2 * T, 4)],
            [("w_vo", 0), ("w_qk", 0)] + SUP[0::2] + [("kxn", 0)] + [("out", m) for m in range(0, T, 4)]
            + ["pooled"] + [("hid", i) for i in range(0, 12, 4)],
            [("w_vo", 1), ("w_qk", 1)] + SUP[1::2] + [("kxn", 1), ("z", 0)] + [("out", m) for m in range(1, T, 4)]
            + ["gates"] + [("hid", i) for i in range(1, 12, 4)],
            [("w_vo", 2), ("w_qk", 2)] + QK[0::2] + ["k_sum", ("kxn_t", 0), ("z", 1)]
            + [("out", m) for m in range(2, T, 4)] + ["score_max"] + [("hid", i) for i in range(2, 12, 4)],
            [("w_vo", 3), ("w_qk", 3)] + QK[1::2] + [("kxn_t", 1), "mid_t"] + [("out", m) for m in range(3, T, 4)]
            + ["score_b", "gates_b"]
            + [("hid", i) for i in range(3, 12, 4)],
        ]
        turn = {use: (b, n) for b, keys in enumerate(uses) for n, use in enumerate(keys)}
        filled = [sem(f"filled{b}") for b in range(8)]
        drained = [sem(f"drained{b}") for b in range(8)]

        def pt(use):
            return bank[turn[use][0]]

        def wait_free(eng, use):
            b, n = turn[use]
            if n:
                eng.wait_ge(drained[b], n)

        def wait_filled(eng, use):
            b, n = turn[use]
            eng.wait_ge(filled[b], n + 1)

        def wait_drained(eng, use):
            b, n = turn[use]
            eng.wait_ge(drained[b], n + 1)

        def groups_ended(before, after):
            ends = [min((g + 1) * GB, NB) * WIN for g in range(NG)]
            return [g for g in range(NG) if before < ends[g] <= after]

        EARLY = T - 2

        def early_row(g):
            k = g - (NG - EARLY)
            if k < 0:
                return None
            assert ((P // RB) * (k + 1) - 1) // GB <= g - 2
            return k

        def slot_tiles(k):
            return Q * sum(SLOTS[:k]), Q * sum(SLOTS[:k + 1])

        g_idx = [sb(f"g_idx{i}", [1, 8], U32) for i in range(1)][0]

        scores = sb("scores", [P, T])
        aw_b = sb("aw_b", [P, D])
        ab_b = sb("ab_b", [P, 1])
        tiny = sb("tiny", [P, 64])
        gw_sb = sb("gw_sb", [P, C, NX])
        gb_row = sb("gb_row", [1, NX])
        pooled = sb("pooled", [P, C])
        gate_b2 = sb("gate_b2", [P, 2])
        neg = sb("neg", [P, 2 * T + 1])
        fade = sb("fade", [P, T, 2])
        pool_sum = sb("pool_sum", [P, 1])
        pool_share = sb("pool_share", [P, 1])

        x_t_hi = over("x_t_hi", [P, 2, C, P], F32R, "x_t_space")
        x_t_lo = [over("x_t_lo0", [P, C, P], F32R, "aw_b"), over("x_t_lo1", [P, C, P], F32R, "x2_space", 4 * (C * NP - D))]
        w_gnn_hi = over("w_gnn_hi", [P, C, D], F32R, "adj_space", 4 * C * D)
        w_gnn_lo = over("w_gnn_lo", [P, C, D], F32R, "adj_space", 8 * C * D)
        w_qk_hi = over("w_qk_hi", [P, C, D], F32R, "adj_space", 12 * C * D)
        w_qk_lo = over("w_qk_lo", [P, C, D], F32R, "x2_space", 4 * T * D // 2)
        assert T * D // 2 + C * D <= C * NP - D
        b_parts = over("b_parts", [2 * 32, D], F32R, "b_qk")
        pick_b = over("pick_b", [2 * 32, P], F32R, "k_inv")
        sup_lo = over("sup_lo", [P, T, D], F32R, "x_sb")
        XA = (RING * (3 * P + SPAN) + 2 * P) * Q // 2 // D
        x_a = over("x_a", [P, XA, D], F32, "hot_space")
        x_b = over("x_b", [P, T - XA, D], F32, "w_in_sb")
        x_res = lambda t: x_a[:, t, :] if t < XA else x_b[:, t - XA, :]
        X_PIECES = [(0, 3), (3, XA), (XA, T - 1)]
        a_hi, a_lo = [[over(f"a_{part}{i}", [P, T, P], F32R, "x2_space", 4 * (2 * i + j) * T * P) for i in range(2)]
                      for j, part in enumerate(("hi", "lo"))]
        q_hi, q_lo = [over(f"q_{part}", [P, 2, 2, P], F32R, "q_buf", 16 * P * i) for i, part in enumerate(("hi", "lo"))]
        z_hi = over("z_hi", [P, 2, D], F32R, "x_t_space")
        z_lo = [over("z_lo0", [P, D], F32R, "b_qk"), over("z_lo1", [P, D], F32R, "w_in_sb", 4 * (C - 1) * D)]
        assert T - XA < C
        pooling = over("pooling", [P, 4, D], F32, "w_vo")
        junk, pool_acc, pool_add = pooling[:, 0, :], pooling[:, 1, :], pooling[:, 2:4, :]
        x2_hi = over("x2_hi", [P, C, NP], F32R, "adj_space")
        x2_lo = over("x2_lo", [P, C, NP], F32R, "adj_space", 4 * C * NP)
        assert 2 * C < T
        e_w1 = AT[:, 2 * C:2 * C + 2, 0:C * H].rearrange("p e (c h) -> p e c h", c=C)
        e_w2 = over("e_w2", [P, 2, HC, D], F32, "x_sb")
        e_b2 = over("e_b2", [P, 2, D], F32, "w_vo")
        e_b1 = tiny[:, 32:32 + 2 * HC].rearrange("p (e c) -> p e c", e=2)
        w1_hi = over("w1_hi", [P, 2, HC, C, P], F32R, "x2_space")
        w1_lo = over("w1_lo", [P, 2, HC, C, P], F32R, "x2_space", 8 * C * H)
        w2_hi = over("w2_hi", [P, 2, HC, D], F32R, "q_t")
        w2_lo = over("w2_lo", [P, 2, HC, D], F32R, "x_sb", 8 * HC * D)
        hid_hi = over("hid_hi", [P, 2 * HC, NP], F32R, "xn")
        hid_lo = over("hid_lo", [P, 2 * HC, NP], F32R, "sup_hi")
        hid = over("hid", [P, 2, 512], F32, "x_t_space")
        pick = over("pick", [2 * 32, P], F32R, "stage")
        b2_parts = over("b2_parts", [2 * 32, D], F32R, "mid_t")
        pre = over("pre", [P, 2, D], F32, "adj_space")
        post = over("post", [P, 4, D], F32, "adj_space", 16 * D)

        rep_iota = stage[:, 0, 0, 0:P]
        rep_row = stage[:, 0, 1, 0:P]
        rep_col = stage[:, 0, 2, :]
        rep_acc = stage[:, 1, 0, :]
        rep_key, at = carve(hot_space, 0, EP, [EC])
        rep_place, at = carve(hot_space, at, EP, [EC])

        block = ctx.enter_context(nc.Block())

        @block.sync
        def _(sp):
            as_list = lambda a: a.rearrange("(p c) -> p c", p=EP)
            sp.dma_start(dst_all[:], as_list(dst)).then_inc(S("dst_in"), 16)
            sp.wait_ge(S("x_pad"), 1)
            third = T // 3
            for i in range(3):
                sp.dma_start(x_sb[:, third * i:third * (i + 1), :],
                             x[P * third * i:P * third * (i + 1), :].rearrange("(t p) d -> p t d", p=P)
                             ).then_inc(S(f"x_in{i}"), 16)
            sp.dma_start(x_sb[0:TAIL, T - 1, :], x[P * (T - 1):N, :]).then_inc(S("x_tail"), 16)
            sp.dma_start(w_gnn[:], gnn_w.rearrange("(c p) n -> p c n", p=P)).then_inc(S("w_gnn_in"), 16)
            sp.dma_start(src_all[:], as_list(src)).then_inc(S("list_in"), 16)
            sp.dma_start(w_all[:], as_list(edge_weight)).then_inc(S("list_in"), 16)
            sp.dma_start(b_sum[:], gnn_b.partition_broadcast(P)).then_inc(S("b_sum_in"), 16)
            sp.dma_start(b_out_b, b_out.partition_broadcast(P)).then_inc(S("b_sum_in"), 16)
            sp.dma_start(ab_b[:], attn_b.partition_broadcast(P)).then_inc(S("gate_in"), 16)
            sp.dma_start(gw_sb[:], gate_w.rearrange("(c p) e -> p c e", p=P)).then_inc(S("gate_in"), 16)
            sp.dma_start(gb_row[:], gate_b.rearrange("(o e) -> o e", o=1)).then_inc(S("gate_in"), 16)
            for g in range(NG):
                nb = min(GB, NB - g * GB)
                wait_drained(sp, ("adj", g))
                sp.dma_start(adj_blocks[g * GB:g * GB + nb].rearrange("b q l -> q b l"),
                             stage[:, g % 2, 0:nb, :]).then_inc(S(f"adj_out{g % 2}"), 16)
                k = early_row(g)
                if k is not None:
                    if k == 0:
                        wait_filled(sp, ("qk", T - 1))
                    for half in range(2):
                        sp.wait_ge(S(f"adj_out{half}"), 16 * ((g - half) // 2))
                    sp.dma_start(AT[:, k, :], adj[P * k:P * (k + 1), :]).then_inc(S(f"adj_in{k}"), 16)
            for half in range(2):
                sp.wait_ge(S(f"adj_out{half}"), 16 * ((NG + 1 - half) // 2))
            sp.wait_ge(S("missing_known"), 1)
            missing = sp.value_load(missing_i[0:1, 0:1], min_val=-NE, max_val=NE)
            with sp.If(missing != 0):
                with sp.Fori(0, NB) as b:
                    sp.wait_ge(S("block_summed"), b + 1)
                    sp.dma_start(adj_blocks[bass.ds(b, 1)].rearrange("b q l -> q (b l)"),
                                 rep_acc[:]).then_inc(S("block_out"), 16)
                sp.wait_ge(S("block_out"), 16 * NB)
                for k in range(EARLY):
                    sp.wait_ge(S(f"adj_in{k}"), 16)
                    sp.dma_start(AT[:, k, :], adj[P * k:P * (k + 1), :]).then_inc(S("adj_again"), 16)
                sp.wait_ge(S("adj_again"), 16 * EARLY)
            with sp.Else():
                sp.nop()
            sp.sem_inc(S("rows_whole"), 1)
            for k in range(EARLY, T):
                sp.dma_start(AT[:, k, :], adj[P * k:P * (k + 1), :]).then_inc(S(f"adj_in{k}"), 16)
            sp.dma_start(aw_b[:], attn_w.rearrange("d o -> (d o)").partition_broadcast(P)).then_inc(S("gate_in"), 16)
            for i, (a, b) in enumerate(X_PIECES):
                if a == XA:
                    wait_filled(sp, "mid_t")
                to = x_a[:, a:b, :] if b <= XA else x_b[:, a - XA:b - XA, :]
                sp.dma_start(to, x[P * a:P * b, :].rearrange("(t p) d -> p t d", p=P)).then_inc(S(f"x_again{i}"), 16)
            sp.wait_ge(S("x_pad_again"), 1)
            sp.dma_start(x_b[0:TAIL, T - 1 - XA, :], x[P * (T - 1):N, :]).then_inc(S("x_tail_again"), 16)
            sp.wait_ge(S("chosen"), 1)
            wait_filled(sp, ("out", T - 1))
            for e in range(2):
                ex = sp.value_load(g_idx[0:1, e:e + 1], min_val=0, max_val=NX - 1)
                sp.dma_start(e_w1[:, e], w1[bass.ds(ex, 1)].rearrange("e (c p) h -> p (e c) h", p=P)
                             ).then_inc(S(f"w1_in{e}"), 16)
                sp.dma_start(e_b1[:, e, :], b1[bass.ds(ex, 1)].rearrange("e (p c) -> p (e c)", p=P)
                             ).then_inc(S(f"b1_in{e}"), 16)
                sp.dma_start(e_w2[:, e], w2[bass.ds(ex, 1)].rearrange("e (p c) h -> p (e c) h", p=P)
                             ).then_inc(S(f"w2_in{e}"), 16)
                sp.dma_start(e_b2[:, e, :], b2[bass.ds(ex, 1)].rearrange("e n -> (e n)").partition_broadcast(P)
                             ).then_inc(S(f"b2_in{e}"), 16)
            for m in range(T):
                rows = P if m < T - 1 else TAIL
                sp.wait_ge(S("y_ready"), m + 1)
                sp.dma_start(out[P * m:P * m + rows, :], x_res(m)[0:rows, :]).then_inc(S("y_out"), 16)
            sp.wait_ge(S("y_out"), 16 * T)

        @block.gpsimd
        def _(pool):
            pool.memset(x_sb[:, T - 1, :], 0.0).then_inc(S("x_pad"), 1)
            pool.iota(iota_i[:], [[1, SPAN]], base=0, channel_multiplier=0).then_inc(S("iota_i"), 1)
            pool.iota(part_i[:], [[0, 1]], base=0, channel_multiplier=1).then_inc(S("iota_i"), 1)
            pool.memset(two_qk[:], 0.0).then_inc(S("two_zero"), 1)
            pool.memset(two_v[:], 0.0).then_inc(S("two_zero"), 1)
            pool.memset(ident[:], 0.0).then_inc(S("const0"), 1)
            pool.memset(is_high[:], 0.0).then_inc(S("const0"), 1)
            pool.memset(above_high[:], 1.0).then_inc(S("const0"), 1)
            pool.memset(tail_far[:], 0.0).then_inc(S("const0"), 1)
            pool.wait_ge(S("const0"), 4)
            pool.affine_select(out=ident[:], in_=ident[:], compare_op=ALU.not_equal, fill=1.0, base=0,
                               pattern=[[-1, P]], channel_multiplier=1).then_inc(S("ident"), 1)
            pool.affine_select(out=is_high[:], in_=is_high[:], compare_op=ALU.not_equal, fill=1.0, base=0,
                               pattern=[[1, BH], [0, LOW]], channel_multiplier=-1).then_inc(S("digits"), 1)
            pool.affine_select(out=above_high[:], in_=above_high[:], compare_op=ALU.is_gt, fill=0.0, base=0,
                               pattern=[[1, BH], [0, LOW]], channel_multiplier=-1).then_inc(S("digits"), 1)
            pool.affine_select(out=tail_far[:], in_=tail_far[:], compare_op=ALU.is_ge, fill=FAR, base=TAIL - 1,
                               pattern=[[0, 1]], channel_multiplier=-1).then_inc(S("const"), 1)
            pool.memset(ones[:], 1.0).then_inc(S("const"), 1)
            pool.memset(mid_t[:], 0.0).then_inc(S("const"), 1)
            pool.memset(pick_b[:].bitcast(F32), 0.0).then_inc(S("pick_b"), 1)
            pool.wait_ge(S("pick_b"), 1)
            for row in (0, 32):
                pool.memset(pick_b[row:row + 1, :].bitcast(F32), 1.0).then_inc(S("pick_b"), 1)
            pool.wait_ge(S("pick_b"), 3)
            pool.wait_ge(S("starts"), 1)
            for dst_sb, table in ((dst_w, dst), (src_w, src), (wgt_w, edge_weight)):
                pool.indirect_dma_start(out=dst_sb[:], out_offset=None, in_=table.rearrange("(e o) -> e o", o=1),
                                        in_offset=bass.IndirectOffsetOnAxis(ap=start_u[:], axis=0)
                                        ).then_inc(S("window_in"), 16)
            pool.wait_ge(S("b_sum_in"), 32)
            pool.tensor_tensor(b_sum[:], b_sum[:], b_out_b, ALU.add).then_inc(S("b_sum"), 1)
            pool.wait_ge(S("b_sum"), 1)
            wait_filled(pool, "mid_t")
            pool.memset(x_res(T - 1), 0.0).then_inc(S("x_pad_again"), 1)
            pool.wait_ge(S("rows_whole"), 1)
            pool.memset(pick[:].bitcast(F32), 0.0).then_inc(S("pick"), 1)
            pool.wait_ge(S("pick"), 1)
            for row in (0, 32):
                pool.memset(pick[row:row + 1, :].bitcast(F32), 1.0).then_inc(S("pick"), 1)
            pool.wait_ge(S("pick"), 3)
            for t in range(T):
                for i, (a, b) in enumerate(X_PIECES):
                    if t == a:
                        pool.wait_ge(S(f"x_again{i}"), 16)
                if t == T - 1:
                    pool.wait_ge(S("x_tail_again"), 16)
                pool.tensor_tensor(x_res(t), x_res(t), b_sum[:], ALU.add).then_inc(S("x_biased"), 1)

        @block.tensor
        def _(pe):
            mm = nc.tensor.matmul

            def end(ins, use):
                ins.then_inc(filled[turn[use][0]], 1)

            pe.wait_ge(S("list_hot"), 2)
            for c in range(EC):
                last = mm(pt("count")[0:BH, 0:LOW + 1], hot_hi[:, c, :], below_lo[:, c, :],
                          start=(c == 0), stop=(c == EC - 1))
            end(last, "count")
            pe.wait_ge(S("digits"), 2)
            wait_drained(pe, "count")
            mm(pt("start")[0:NB, 0:LOW + 1], is_high[:].rearrange("h a b -> h (a b)"), count_sb[:],
               start=True, stop=True)
            end(mm(pt("start")[0:NB, 16:17], above_high[:].rearrange("h a b -> h (a b)"),
                   count_sb[:, LOW:LOW + 1], start=True, stop=True), "start")
            pe.wait_ge(S("ident"), 1)
            pe.wait_ge(S("two_in"), 16 * 6)
            wait_free(pe, "two_vt")
            end(nc.tensor.transpose(pt("two_vt")[:, 0:P], two_v[:], ident[:]), "two_vt")
            pe.wait_ge(S("w_in_in"), 16)
            for p in range(C):
                wait_free(pe, ("w_in_t", p))
                for c in range(C):
                    last = nc.tensor.transpose(pt(("w_in_t", p))[:, P * c:P * c + P],
                                               w_in_sb[:, c, P * p:P * p + P], ident[:])
                end(last, ("w_in_t", p))
            pe.wait_ge(S("const"), 3)
            wait_drained(pe, "two_vt")
            pe.wait_ge(S("w_out_in"), 16)
            for p in range(C):
                end(mm(pt(("w_vo", p))[:], two_vt[:], w_out_sb[:, p, :], start=True, stop=True), ("w_vo", p))
            for m in range(C):
                wait_free(pe, ("w_qk", m))
                view = pt(("w_qk", m))[:].rearrange("p (k n) -> p k n", k=2)
                for p in range(C):
                    wait_drained(pe, ("w_in_t", p))
                    last = mm(view[:, :, 2 * SL * p:2 * SL * (p + 1)], w_in_t[:, p, P * m:P * m + P],
                              two_qk[:].rearrange("p k h s -> p k (h s)"), start=True, stop=True)
                end(last, ("w_qk", m))
            wait_free(pe, "b_qk_row")
            pe.wait_ge(S("b_in_in"), 16)
            view = pt("b_qk_row")[:].rearrange("p (k n) -> p k n", k=2)
            for p in range(C):
                last = mm(view[0:1, :, 2 * SL * p:2 * SL * (p + 1)], b_in_col[:, p:p + 1],
                          two_qk[:].rearrange("p k h s -> p k (h s)"), start=True, stop=True)
            end(last, "b_qk_row")
            wait_drained(pe, "b_qk_row")
            wait_free(pe, "b_qk")
            end(mm(pt("b_qk")[:], ones[0:1, :], b_qk_row[:], start=True, stop=True), "b_qk")
            def turn_x(t):
                wait_free(pe, ("x_t", t))
                pe.wait_ge(S("normed"), t + 1)
                for c in range(C):
                    last = nc.tensor.transpose(pt(("x_t", t))[:, P * c:P * c + P], xn[:, t, P * c:P * c + P], ident[:])
                end(last, ("x_t", t))

            turn_x(0)
            pe.wait_ge(S("window_keys"), 3)
            wait_free(pe, "edges")
            for a, w in enumerate((key_w, place_w)):
                for c in range(WIN):
                    col = (a * WIN + c) * NB
                    last = nc.tensor.transpose(pt("edges")[:, col:col + NB], w[:, P * c:P * c + P], ident[0:NB, 0:NB])
            end(last, "edges")
            wait_free(pe, "weights")
            for c in range(WIN):
                last = nc.tensor.transpose(pt("weights")[:, NB * c:NB * c + NB], wgt_w[:, P * c:P * c + P],
                                           ident[0:NB, 0:NB])
            end(last, "weights")

            def adj_signal(a, b):
                for n in range(a, b):
                    blk, c = n // WIN, n % WIN
                    g, within = blk // GB, blk % GB
                    if within == 0 and c == 0:
                        wait_free(pe, ("adj", g))
                    pe.wait_ge(S("hot_ready"), n // Q + 1)
                    slot, i = n // Q % RING, n % Q
                    for k in range(3):
                        last = mm(pt(("adj", g))[:, SPAN * within:SPAN * (within + 1)], hot_row[:, slot, k, :, i],
                                  hot_col[:, slot, :, i], start=(c == 0 and k == 0),
                                  stop=(c == WIN - 1 and k == 2))
                    if c == WIN - 1 and (within == GB - 1 or blk == NB - 1):
                        end(last, ("adj", g))
                    elif i == Q - 1:
                        last.then_inc(S("hot_used"), 1)

            def turn_q(t):
                wait_free(pe, ("q_t", t))
                pe.wait_ge(S("q_ready"), t + 1)
                for h in range(2):
                    last = nc.tensor.transpose(pt(("q_t", t))[:, P * h:P * h + P],
                                               q_buf[:, t % 4, P * h:P * h + P], ident[:])
                end(last, ("q_t", t))

            def project(use, t, w_hi, w_lo, first):
                pairs = [(x_t_hi[:, t % 2], w_hi), (x_t_lo[t % 2], w_hi), (x_t_hi[:, t % 2], w_lo)]
                for i, (x_part, w_part) in enumerate(pairs):
                    for c in range(C):
                        last = mm(pt(use)[:], x_part[:, c, :], w_part[:, c, :], start=(first and i == c == 0),
                                  stop=(i == 2 and c == C - 1))
                end(last, use)

            for t in range(T + 2):
                if t < T:
                    adj_signal(*slot_tiles(3 * t))
                    wait_drained(pe, ("x_t", t))
                    wait_free(pe, ("support", t))
                    if t == 0:
                        pe.wait_ge(S("w_gnn_lo"), 1)
                    if t + 1 < T:
                        turn_x(t + 1)
                    project(("support", t), t, w_gnn_hi, w_gnn_lo, True)
                    adj_signal(*slot_tiles(3 * t + 1))
                    wait_free(pe, ("qk", t))
                    if t == 0:
                        for m in range(C):
                            wait_drained(pe, ("w_qk", m))
                        wait_drained(pe, "b_qk")
                        pe.wait_ge(S("pick_b"), 3)
                    mm(pt(("qk", t))[:], pick_b[:], b_parts[:], start=True, stop=False)
                    project(("qk", t), t, w_qk_hi, w_qk_lo, False)
                    if t == 0:
                        wait_free(pe, "covered")
                        end(mm(pt("covered")[0:1, 0:1], covered[:], ones[0:NB, 0:1], start=True, stop=True), "covered")
                    adj_signal(*slot_tiles(3 * t + 2))
                if t >= 2:
                    turn_q(t - 2)

            wait_free(pe, "k_max_t")
            pe.wait_ge(S("k_max"), 1)
            for h in range(2):
                last = nc.tensor.transpose(pt("k_max_t")[:, P * h:P * h + P], k_max[:, P * h:P * h + P], ident[:])
            end(last, "k_max_t")
            adj_signal(*slot_tiles(3 * T))
            wait_free(pe, "k_max_b")
            pe.wait_ge(S("k_diag"), 2)
            end(mm(pt("k_max_b")[:, 0:2 * P], ones[:], k_diag[:].rearrange("p h n -> p (h n)"),
                   start=True, stop=True), "k_max_b")
            adj_signal(*slot_tiles(3 * T + 1))
            for h in range(2):
                wait_free(pe, ("kxn", h))
                for t in range(T):
                    for i, (a, b) in enumerate(K_PARTS):
                        if h == 0 and t == a:
                            pe.wait_ge(S("k_exp"), i + 1)
                    last = mm(pt(("kxn", h))[:], k_sb[:, t, P * h:P * h + P], xn[:, t, :],
                              start=(t == 0), stop=(t == T - 1))
                    if t == T - 1:
                        end(last, ("kxn", h))
                    if t % (T // 2) == T // 2 - 1:
                        adj_signal(*slot_tiles(3 * T + 2 + 2 * h + t // (T // 2)))

            pe.wait_ge(S("missing_known"), 1)
            wait_drained(pe, ("adj", NG - 1))
            wait_drained(pe, ("adj", NG - 2))
            missing = pe.value_load(missing_i[0:1, 0:1], min_val=-NE, max_val=NE)
            with pe.If(missing != 0):
                with pe.Fori(0, NB * EC) as n:
                    pe.wait_ge(S("rep_hot"), n + 1)
                    mm(bank[0][:, 0:SPAN], rep_row[:], rep_col[:], start=True, stop=True).then_inc(S("rep_done"), 1)
            with pe.Else():
                pe.nop()

            wait_free(pe, "k_sum")
            for t in range(T):
                last = mm(pt("k_sum")[:, 0:2 * P], ones[:], k_sb[:, t, :], start=(t == 0), stop=(t == T - 1))
            end(last, "k_sum")
            for i in range(2):
                wait_free(pe, ("kxn_t", i))
                for h in range(2):
                    wait_drained(pe, ("kxn", h))
                    for j in range(2):
                        c = 2 * i + j
                        last = nc.tensor.transpose(pt(("kxn_t", i))[:, (2 * j + h) * P:(2 * j + h + 1) * P],
                                                   kxn[:, h, P * c:P * c + P], ident[:])
                end(last, ("kxn_t", i))
            def out_rows(m, ks):
                for k in ks:
                    if m == 0:
                        pe.wait_ge(S("a_lo"), k + 1)
                        wait_drained(pe, ("support", k))
                    hi, lo = a_hi[m % 2][:, k, :], a_lo[m % 2][:, k, :]
                    mm(pt(("out", m))[:], hi, sup_hi[:, k, :], start=(k == 0), stop=False)
                    mm(pt(("out", m))[:], hi, sup_lo[:, k, :], start=False, stop=False)
                    mm(pt(("out", m))[:], lo, sup_hi[:, k, :], start=False, stop=False)

            wait_free(pe, ("out", 0))
            wait_free(pe, "mid_t")
            for i in range(2):
                wait_drained(pe, ("kxn_t", i))
            for p in range(C):
                for c in range(C):
                    last = mm(pt("mid_t")[:, P * p:P * p + P], w_in_sb[:, c, P * p:P * p + P],
                              kxn_t[:, c, p // 2, :], start=(c == 0), stop=(c == C - 1))
            end(last, "mid_t")
            out_rows(0, range(T))
            wait_drained(pe, "mid_t")
            for h in range(2):
                wait_free(pe, ("z", h))
                for j in range(2):
                    last = mm(pt(("z", h))[:], mid_t[:, 2 * h + j, :], w_vo[:, 2 * h + j, :],
                              start=(j == 0), stop=(j == 1))
                end(last, ("z", h))

            def turn_x2(m):
                wait_free(pe, ("x2_t", m))
                pe.wait_ge(S("normed2"), m + 1)
                for c in range(C):
                    last = nc.tensor.transpose(pt(("x2_t", m))[:, P * c:P * c + P],
                                               xn[:, m, P * c:P * c + P], ident[:])
                end(last, ("x2_t", m))

            for m in range(T + 2):
                if m < T:
                    if m:
                        wait_free(pe, ("out", m))
                        pe.wait_ge(S("a_lo"), T + m)
                        out_rows(m, range(T))
                    pe.wait_ge(S("q_lo"), m + 1)
                    for h in range(2):
                        if m == 0:
                            wait_drained(pe, ("z", h))
                        mm(pt(("out", m))[:], q_hi[:, m % 2, h, :], z_hi[:, h, :], start=False, stop=False)
                        mm(pt(("out", m))[:], q_hi[:, m % 2, h, :], z_lo[h][:], start=False, stop=False)
                        last = mm(pt(("out", m))[:], q_lo[:, m % 2, h, :], z_hi[:, h, :], start=False, stop=(h == 1))
                    end(last, ("out", m))
                if m >= 2:
                    turn_x2(m - 2)

            wait_free(pe, "score_max")
            pe.wait_ge(S("score_top"), T)
            end(nc.tensor.transpose(pt("score_max")[0:1, 0:P], neg[:, 2 * T:2 * T + 1], ident[:]), "score_max")
            wait_drained(pe, "score_max")
            wait_free(pe, "score_b")
            end(mm(pt("score_b")[:, 0:1], ones[0:1, :], tiny[0:1, 1:2], start=True, stop=True), "score_b")
            pe.wait_ge(S("pool_share"), 1)
            pe.wait_ge(S("pool_added"), 2 * T - 2)
            wait_free(pe, "pooled")
            for c in range(C):
                mm(pt("pooled")[:, c:c + 1], pool_acc[:, P * c:P * c + P], pool_share[:], start=True, stop=True)
            end(mm(pt("pooled")[0:1, 8:9], pool_share[:], pool_sum[:], start=True, stop=True), "pooled")
            wait_drained(pe, "pooled")
            wait_free(pe, "gates")
            for c in range(C):
                last = mm(pt("gates")[0:1, 0:NX], pooled[:, c:c + 1], gw_sb[:, c, :], start=(c == 0), stop=(c == C - 1))
            end(last, "gates")
            for i in range(12):
                e, half, chunk = i // 6, i // 3 % 2, i % 3
                n0, n1 = 512 * chunk, min(512 * (chunk + 1), NP)
                wait_free(pe, ("hid", i))
                if i % 6 == 0:
                    for m in (T - 1, T - 2):
                        wait_drained(pe, ("x2_t", m))
                for w, x2 in ((w1_hi, x2_hi), (w1_hi, x2_lo), (w1_lo, x2_hi)):
                    if w is w1_hi and x2 is x2_hi:
                        pe.wait_ge(S("w1_hi"), 2 * e + half + 1)
                    if w is w1_lo:
                        pe.wait_ge(S("w1_lo"), 2 * e + half + 1)
                    for c in range(C):
                        last = mm(pt(("hid", i))[:, 0:n1 - n0], w[:, e, half, c, :], x2[:, c, n0:n1],
                                  start=(w is w1_hi and x2 is x2_hi and c == 0), stop=(w is w1_lo and c == C - 1))
                end(last, ("hid", i))
                if i == 0:
                    pe.wait_ge(S("shares"), 1)
                    wait_free(pe, "gates_b")
                    end(mm(pt("gates_b")[:, 0:2], ones[0:1, :], tiny[0:1, 24:26], start=True, stop=True), "gates_b")
            for m in range(T):
                for e in range(2):
                    use = ("expert", 2 * m + e)
                    wait_free(pe, use)
                    if m == 0:
                        pe.wait_ge(S("w2_hi"), e + 1)
                        pe.wait_ge(S("w2_lo"), e + 1)
                        pe.wait_ge(S("hid_lo"), 6 * e + 6)
                    if e == 1:
                        if m == 0:
                            pe.wait_ge(S("b2_parts"), 1)
                            pe.wait_ge(S("pick"), 3)
                        mm(pt(use)[:], pick[:], b2_parts[:], start=True, stop=False)
                    for a, w in ((hid_hi, w2_hi), (hid_lo, w2_hi), (hid_hi, w2_lo)):
                        for c in range(HC):
                            last = mm(pt(use)[:], a[:, HC * e + c, P * m:P * m + P], w[:, e, c, :],
                                      start=(e == 0 and a is hid_hi and w is w2_hi and c == 0),
                                      stop=(w is w2_lo and c == HC - 1))
                    end(last, use)

        @block.scalar
        def _(act):
            cp = nc.scalar.copy

            def drain(use, out_ap, in_ap):
                wait_filled(act, use)
                cp(out_ap, in_ap).then_inc(drained[turn[use][0]], 1)

            def drain_x2(m):
                wait_filled(act, ("x2_t", m))
                cp(x2_hi[:, :, P * m:P * m + P], pt(("x2_t", m))[:].rearrange("p (c n) -> p c n", c=C)
                   ).then_inc(S("x2_hi"), 1)

            def pool_tile(t):
                if t == 0:
                    return
                act.wait_ge(S("score_top"), t + 1)
                nc.scalar.activation(fade[:, t, :], neg[:, 2 * t:2 * t + 2], ACT.Exp, bias=neg[:, 2 * t + 2:2 * t + 3],
                                     scale=-1.0).then_inc(S("fade"), 1)
                act.wait_ge(S("fade"), t)
                if t >= 3:
                    act.wait_ge(S("pool_added"), 2 * (t - 2))
                nc.scalar.activation(pool_add[:, t % 2, :], xn[:, t, :], ACT.Identity, scale=fade[:, t, 1:2]
                                     ).then_inc(S("pool_add"), 1)

            act.dma_start(w_in_sb[:], w_in.rearrange("(c p) n -> p c n", p=P)).then_inc(S("w_in_in"), 16)
            act.wait_ge(S("two_zero"), 2)
            for i in range(2):
                act.dma_start(two_qk[HD * i:HD * i + HD, 0, i, :], wq).then_inc(S("two_in"), 16)
                act.dma_start(two_qk[HD * i:HD * i + HD, 1, i, :], wk).then_inc(S("two_in"), 16)
                act.dma_start(two_v[HD * i:HD * i + HD, HD * i:HD * i + HD], wv).then_inc(S("two_in"), 16)
            act.dma_start(w_out_sb[:], w_out.rearrange("(c p) n -> p c n", p=P)).then_inc(S("w_out_in"), 16)
            act.dma_start(b_in_col[:], b_in.rearrange("(c p) -> p c", p=P),
                          allow_slow_non_contiguous=True).then_inc(S("b_in_in"), 16)

            drain("two_vt", two_vt[:], pt("two_vt")[:, 0:P])
            for p in range(C):
                drain(("w_in_t", p), w_in_t[:, p, :], pt(("w_in_t", p))[:])
            act.wait_ge(S("variances"), 1)
            act.wait_ge(S("eps"), 1)
            nc.scalar.activation(spread[:], moments[:, :, 1], ACT.Sqrt, bias=eps[:]).then_inc(S("spread"), 1)
            for p in range(C):
                drain(("w_vo", p), w_vo[:, p, :], pt(("w_vo", p))[:])
            for m in range(C):
                wait_filled(act, ("w_qk", m))
                cp(w_qk_hi[:, m, :], pt(("w_qk", m))[:]).then_inc(S("w_qk_hi"), 1)
            drain("b_qk_row", b_qk_row[:], pt("b_qk_row")[0:1, :])
            act.wait_ge(S("w_gnn_in"), 16)
            wait_filled(act, ("w_vo", C - 1))
            cp(w_gnn_hi[:], w_gnn[:]).then_inc(S("w_gnn_hi"), 1)
            wait_filled(act, "b_qk")
            cp(b_parts[:], pt("b_qk")[0:64, :]).then_inc(S("b_round"), 1)

            def groups(k):
                for g in groups_ended(*slot_tiles(k)):
                    nb = min(GB, NB - g * GB)
                    if g >= 2:
                        act.wait_ge(S(f"adj_out{g % 2}"), 16 * (g // 2))
                    drain(("adj", g), stage[:, g % 2, 0:nb, :].rearrange("p b l -> p (b l)"),
                          pt(("adj", g))[:, 0:nb * SPAN])

            def round_x(t):
                if t >= 2:
                    wait_filled(act, ("qk", t - 2))
                wait_filled(act, ("x_t", t))
                cp(x_t_hi[:, t % 2].rearrange("p c n -> p (c n)"), pt(("x_t", t))[:]).then_inc(S("x_t_hi"), 1)

            round_x(0)
            act.wait_ge(S("b_sum"), 1)
            for t in range(T + 2):
                if t < T:
                    groups(3 * t)
                    if t + 1 < T:
                        round_x(t + 1)
                    wait_filled(act, ("support", t))
                    cp(sup_hi[:, t, :], pt(("support", t))[:]).then_inc(S("sup_hi"), 1)
                    groups(3 * t + 1)
                    groups(3 * t + 2)
                if 1 <= t <= T:
                    act.wait_ge(S("q_less"), t)
                    cp(k_sb[:, t - 1, :], pt(("qk", t - 1))[:, D // 2:D]).then_inc(drained[turn[("qk", t - 1)][0]], 1)
                    nc.scalar.activation(q_buf[:, (t - 1) % 4, :], q_buf[:, (t - 1) % 4, :], ACT.Exp
                                         ).then_inc(S("q_exp"), 1)
                if t >= 2:
                    wait_filled(act, ("q_t", t - 2))
                    cp(q_t[:, :, P * (t - 2):P * (t - 1)],
                       pt(("q_t", t - 2))[:, 0:2 * P].rearrange("p (h n) -> p h n", h=2)
                       ).then_inc(drained[turn[("q_t", t - 2)][0]], 1)
            groups(3 * T)
            groups(3 * T + 1)
            for i, (a, b) in enumerate(K_PARTS):
                if b < T:
                    act.wait_ge(S("k_less"), i + 1)
                else:
                    wait_drained(act, "k_max_b")
                nc.scalar.activation(k_sb[:, a:b, :], k_sb[:, a:b, :], ACT.Exp).then_inc(S("k_exp"), 1)
            for k in range(3 * T + 2, len(SLOTS)):
                groups(k)
            for h in range(2):
                drain(("kxn", h), kxn[:, h, :], pt(("kxn", h))[:])
            def round_a(m):
                if m == 0:
                    wait_filled(act, "k_sum")
                    act.wait_ge(S("rows_whole"), 1)
                    for k in range(T):
                        act.wait_ge(S(f"adj_in{k}"), 16)
                        cp(a_hi[0][:, k, :], AT[:, k, 0:P]).then_inc(S("a_hi"), 1)
                else:
                    wait_filled(act, ("out", m - 2) if m >= 2 else "mid_t")
                    cp(a_hi[m % 2][:], AT[:, :, P * m:P * m + P]).then_inc(S("a_hi"), 1)

            def round_q(m):
                if m >= 2:
                    wait_filled(act, ("out", m - 2))
                cp(q_hi[:, m % 2], q_t[:, :, P * m:P * m + P]).then_inc(S("q_hi"), 1)

            wait_drained(act, ("q_t", T - 1))
            round_a(0)
            round_q(0)
            round_a(1)
            round_q(1)
            for h in range(2):
                wait_filled(act, ("z", h))
                cp(z_hi[:, h, :], pt(("z", h))[:]).then_inc(S("z_hi"), 1)
            for m in range(T):
                if 1 <= m < T - 1:
                    round_a(m + 1)
                    round_q(m + 1)
                act.wait_ge(S("moments2"), m + 1)
                nc.scalar.activation(spread[:, m:m + 1], moments[:, m, 1:2], ACT.Sqrt, bias=eps[:]
                                     ).then_inc(S("spread2"), 1)
                if m >= 2:
                    drain_x2(m - 2)
                    pool_tile(m - 2)
            pool_tile(T - 2)
            drain_x2(T - 2)
            drain_x2(T - 1)
            pool_tile(T - 1)
            act.wait_ge(S("score_far"), 1)
            nc.scalar.activation(pool_share[:], neg[:, 2 * T:2 * T + 1], ACT.Exp, bias=tiny[:, 2:3], scale=-1.0
                                 ).then_inc(S("pool_share"), 1)
            act.wait_ge(S("gate_less"), 1)
            nc.scalar.activation(tiny[0:1, 8:8 + NX], tiny[0:1, 8:8 + NX], ACT.Exp, accum_out=tiny[0:1, 5:6]
                                 ).then_inc(S("gate_exp"), 1)
            nc.scalar.activation(tiny[0:1, 16:18], tiny[0:1, 16:18], ACT.Exp).then_inc(S("gate_exp"), 1)
            def round_w1(e):
                act.wait_ge(S(f"w1_in{e}"), 16)
                for half in range(HC):
                    cp(w1_hi[:, e, half], e_w1[:, e, :, half:H:HC]).then_inc(S("w1_hi"), 1)

            def round_w2(e):
                act.wait_ge(S(f"w2_in{e}"), 16)
                cp(w2_hi[:, e], e_w2[:, e]).then_inc(S("w2_hi"), 1)

            round_w1(0)
            for i in range(12):
                e, half, chunk = i // 6, i // 3 % 2, i % 3
                n0, n1 = 512 * chunk, min(512 * (chunk + 1), NP)
                wait_filled(act, ("hid", i))
                if i % 6 == 0:
                    act.wait_ge(S(f"b1_in{e}"), 16)
                if i >= 2:
                    act.wait_ge(S("hid_lo"), i - 1)
                nc.scalar.activation(hid[:, i % 2, 0:n1 - n0], pt(("hid", i))[:, 0:n1 - n0], ACT.Gelu,
                                     bias=e_b1[:, e, half:half + 1]).then_inc(drained[turn[("hid", i)][0]], 1)
                wait_drained(act, ("hid", i))
                cp(hid_hi[:, HC * e + half, n0:n1], hid[:, i % 2, 0:n1 - n0]).then_inc(S("hid_hi"), 1)
                if i == 1:
                    round_w1(1)
                if i in (3, 5):
                    round_w2(i // 4)
                if i == 5:
                    act.wait_ge(S("b2_in1"), 16)
                    cp(b2_parts[:], e_b2[0:64, 1, :]).then_inc(S("b2_round"), 1)
            for i in range(2 * T):
                m, e = i // 2, i % 2
                if i >= 4:
                    act.wait_ge(S("y_ready"), (i - 4) // 2 + 1)
                if e == 0:
                    act.wait_ge(S("pre"), m + 1)
                    nc.scalar.activation(post[:, i % 4, :], pre[:, m % 2, :], ACT.Gelu).then_inc(S("post"), 1)
                else:
                    wait_filled(act, ("expert", i))
                    nc.scalar.activation(post[:, i % 4, :], pt(("expert", i))[:], ACT.Gelu
                                         ).then_inc(drained[turn[("expert", i)][0]], 1)

        @block.vector
        def _(v):
            link_count = [0]

            def link(ins):
                link_count[0] += 1
                ins.then_inc(S("v_link"), 1)
                v.wait_ge(S("v_link"), link_count[0])

            tt, ts, tr = nc.vector.tensor_tensor, nc.vector.tensor_scalar, nc.vector.tensor_reduce
            v.memset(eps[:], EPS).then_inc(S("eps"), 1)
            v.wait_ge(S("dst_in"), 16)
            link(ts(hi_i[:], dst_all[:], 7, None, ALU.logical_shift_right))
            link(ts(lo_i[:], dst_all[:], 4, 7, ALU.logical_shift_right, ALU.bitwise_and))
            link(nc.vector.tensor_copy(hi_h[:], hi_i[:]))
            v.wait_ge(S("iota_i"), 2)
            nc.vector.tensor_copy(iota_h[:], iota_i[:]).then_inc(S("iota_h"), 1)
            v.wait_ge(S("iota_h"), 1)
            link(nc.vector.tensor_copy(lo_h[:], lo_i[:]))
            tt(hot_hi[:], hi_h[:].unsqueeze(2).to_broadcast([EP, EC, BH]),
               iota_h[0:EP, 0:BH].unsqueeze(1).to_broadcast([EP, EC, BH]), ALU.is_equal).then_inc(S("list_hot"), 1)
            tt(below_lo[:], lo_h[:].unsqueeze(2).to_broadcast([EP, EC, LOW + 1]),
               iota_h[0:EP, 0:LOW + 1].unsqueeze(1).to_broadcast([EP, EC, LOW + 1]), ALU.is_lt
               ).then_inc(S("list_hot"), 1)
            nc.vector.tensor_copy(iota_q[:], iota_i[:].unsqueeze(2).to_broadcast([P, SPAN, Q]))
            link(nc.vector.tensor_copy(part_f[:], part_i[:]))
            link(ts(low_i[:], part_i[:], LOW - 1, None, ALU.bitwise_and))
            link(nc.vector.tensor_copy(low_f[:], low_i[:]))
            link(ts(low_mask[:], iota_h[:, 0:LOW], low_f[:], None, ALU.is_equal))
            link(ts(base_f[:], part_f[:], float(P), None, ALU.mult))

            def moments_of(t, row):
                link(nc.vector.bn_stats(stats[:, t, :], row))
                return nc.vector.bn_aggr(moments[:, t, :], stats[:, t, :])

            v.wait_ge(S("x_in0"), 16)
            for t in range(2):
                link(moments_of(t, x_sb[:, t, :]))
            wait_filled(v, "count")
            nc.vector.tensor_copy(count_sb[:], pt("count")[0:BH, 0:LOW + 1]).then_inc(drained[0], 1)
            wait_filled(v, "start")
            link(tt(start_parts[:], pt("start")[0:NB, 0:LOW], low_mask[0:NB, :], ALU.mult))
            link(tr(start_f[:, 0:1], start_parts[:], AX.X, ALU.add))
            tt(start_f[:, 1:2], start_f[:, 0:1], pt("start")[0:NB, 16:17], ALU.add).then_inc(drained[1], 1)
            wait_drained(v, "start")
            ts(start_u[:], start_f[:, 1:2], float(NE - WE), None, ALU.min).then_inc(S("starts"), 1)
            for t in range(2, T):
                if t % 3 == 0 and t < T - 1:
                    v.wait_ge(S(f"x_in{t // 3}"), 16)
                if t == T - 1:
                    v.wait_ge(S("x_tail"), 16)
                ins = moments_of(t, x_sb[:, t, :])
                if t < T - 1:
                    link(ins)
                else:
                    ins.then_inc(S("variances"), 1)
            v.wait_ge(S("variances"), 1)
            v.wait_ge(S("spread"), 1)
            link(nc.vector.reciprocal(rstd[:], spread[:]))
            for t in range(T):
                ts(xn[:, t, :], x_sb[:, t, :], moments[:, t, 0:1], rstd[:, t:t + 1], ALU.subtract, ALU.mult
                   ).then_inc(S("normed"), 1)
            v.wait_ge(S("window_in"), 48)
            link(ts(t_i[:, 0, :], dst_w[:], 3, None, ALU.logical_shift_left))
            link(ts(t_i[:, 3, :], src_w[:], float(BY_SPAN), None, ALU.mult))
            link(ts(t_i[:, 1, :], t_i[:, 3, :], 21, None, ALU.logical_shift_right))
            link(tt(t_i[:, 2, :], t_i[:, 0, :], t_i[:, 1, :], ALU.bitwise_or))
            ts(key_w[:], t_i[:, 2, :], base_f[0:NB, :], None, ALU.subtract).then_inc(S("window_keys"), 1)
            nc.vector.scalar_tensor_tensor(out=place_w[:], in0=t_i[:, 1, :], scalar=float(-SPAN), in1=src_w[:],
                                           op0=ALU.mult, op1=ALU.add).then_inc(S("window_keys"), 1)
            link(ts(t_i[:, 0, :], dst_w[:], 4, None, ALU.logical_shift_right))
            link(ts(t_i[:, 1, :], t_i[:, 0, :], part_f[0:NB, :], None, ALU.is_equal))
            tr(covered[:], t_i[:, 1, :], AX.X, ALU.add).then_inc(S("window_keys"), 1)
            def rest_x(t):
                v.wait_ge(S("x_t_hi"), t + 1)
                tt(x_t_lo[t % 2].rearrange("p c n -> p (c n)"), pt(("x_t", t))[:],
                   x_t_hi[:, t % 2].rearrange("p c n -> p (c n)").bitcast(F32), ALU.subtract
                   ).then_inc(drained[turn[("x_t", t)][0]], 1)

            v.wait_ge(S("w_gnn_hi"), 1)
            tt(w_gnn_lo[:], w_gnn[:], w_gnn_hi[:].bitcast(F32), ALU.subtract).then_inc(S("w_gnn_lo"), 1)
            rest_x(0)
            for m in range(C):
                v.wait_ge(S("w_qk_hi"), m + 1)
                tt(w_qk_lo[:, m, :], pt(("w_qk", m))[:], w_qk_hi[:, m, :].bitcast(F32), ALU.subtract
                   ).then_inc(drained[turn[("w_qk", m)][0]], 1)
            v.wait_ge(S("b_round"), 1)
            tt(b_parts[32:64, :], pt("b_qk")[32:64, :], b_parts[32:64, :].bitcast(F32), ALU.subtract
               ).then_inc(drained[turn["b_qk"][0]], 1)

            wait_filled(v, "edges")
            by_tile = lambda a: a.rearrange("p (c b) -> p c b", c=WIN)
            to_tile = lambda a: a.rearrange("p (b c) -> p c b", c=WIN)
            link(nc.vector.tensor_copy(to_tile(key_h[:]), by_tile(pt("edges")[:, 0:NT])))
            nc.vector.tensor_copy(to_tile(place_h[:]), by_tile(pt("edges")[:, NT:2 * NT])).then_inc(drained[0], 1)
            wait_drained(v, "edges")
            wait_filled(v, "weights")
            wgt = by_tile(pt("weights")[:, 0:NT])
            rest = by_tile(wgt_r)
            link(nc.vector.tensor_copy(to_tile(wgt_b[:, 0, :]), wgt))
            tt(rest, wgt, to_tile(wgt_b[:, 0, :]), ALU.subtract).then_inc(drained[1], 1)
            wait_drained(v, "weights")
            link(nc.vector.tensor_copy(to_tile(wgt_b[:, 1, :]), rest))
            link(tt(to_tile(wgt_b[:, 2, :]), rest, to_tile(wgt_b[:, 1, :]), ALU.subtract))

            def edge_tiles(a, b):
                for lot in range(a // Q, b // Q):
                    slot, tiles = lot % RING, slice(Q * lot, Q * (lot + 1))
                    if lot >= RING:
                        ends = [min((g + 1) * GB, NB) * WIN for g in range(NG)]
                        used = Q * (lot - RING + 1)
                        if used in ends:
                            wait_filled(v, ("adj", ends.index(used)))
                        else:
                            v.wait_ge(S("hot_used"), sum(n not in ends for n in range(Q, used + 1, Q)))
                    tt(hot_key[:, lot % 2], key_h[:, tiles].unsqueeze(1).to_broadcast([P, P, Q]), iota_q[:, 0:P, :],
                       ALU.is_equal).then_inc(S("hot_key"), 1)
                    tt(hot_col[:, slot], place_h[:, tiles].unsqueeze(1).to_broadcast([P, SPAN, Q]), iota_q[:],
                       ALU.is_equal)
                    v.wait_ge(S("hot_key"), lot + 1)
                    tt(hot_row[:, slot], hot_key[:, lot % 2].unsqueeze(1).to_broadcast([P, 3, P, Q]),
                       wgt_b[:, :, tiles].unsqueeze(2).to_broadcast([P, 3, P, Q]), ALU.mult
                       ).then_inc(S("hot_ready"), 1)

            def softmax_q(t):
                wait_filled(v, ("qk", t))
                if t >= 4:
                    wait_filled(v, ("q_t", t - 4))
                wide = pt(("qk", t))[:, 0:D // 2].rearrange("p (h s) -> p h s", h=NH)
                q = q_buf[:, t % 4, :].rearrange("p (h s) -> p h s", h=NH)
                link(tr(q_red[:, t, 0, :], wide, AX.X, ALU.max))
                tt(q, wide, q_red[:, t, 0, :].unsqueeze(2).to_broadcast([P, NH, SL]), ALU.subtract
                   ).then_inc(S("q_less"), 1)

            def rest_support(t):
                v.wait_ge(S("normed"), T)
                v.wait_ge(S("sup_hi"), t + 1)
                tt(sup_lo[:, t, :], pt(("support", t))[:], sup_hi[:, t, :].bitcast(F32), ALU.subtract
                   ).then_inc(drained[turn[("support", t)][0]], 1)

            def share_q(t):
                v.wait_ge(S("q_exp"), t + 1)
                q = q_buf[:, t % 4, :].rearrange("p (h s) -> p h s", h=NH)
                link(tr(q_red[:, t, 1, :], q, AX.X, ALU.add))
                link(nc.vector.reciprocal(q_red[:, t, 2, :], q_red[:, t, 1, :]))
                tt(q, q, q_red[:, t, 2, :].unsqueeze(2).to_broadcast([P, NH, SL]), ALU.mult
                   ).then_inc(S("q_ready"), 1)

            for t in range(T + 2):
                if t < T:
                    edge_tiles(*slot_tiles(3 * t))
                if 1 <= t <= T:
                    softmax_q(t - 1)
                    rest_support(t - 1)
                if t < T:
                    edge_tiles(*slot_tiles(3 * t + 1))
                if t + 1 < T:
                    rest_x(t + 1)
                if t >= 2:
                    share_q(t - 2)
                if t < T:
                    edge_tiles(*slot_tiles(3 * t + 2))
                if t == 0:
                    wait_filled(v, "covered")
                    link(ts(tiny[0:1, 60:61], pt("covered")[0:1, 0:1], -1.0, float(NE), ALU.mult, ALU.add))
                    nc.vector.tensor_copy(missing_i[:], tiny[0:1, 60:61]).then_inc(drained[1], 1)
                    wait_drained(v, "covered")
                    v.sem_inc(S("missing_known"), 1)

            for t in (T - 1, T - 2):
                wait_drained(v, ("qk", t))
            link(ts(k_sb[:, T - 1, :], k_sb[:, T - 1, :], tail_far[:], None, ALU.add))
            tr(k_max[:], k_sb[:].rearrange("p t n -> p n t"), AX.X, ALU.max).then_inc(S("k_max"), 1)
            edge_tiles(*slot_tiles(3 * T))
            wait_filled(v, "k_max_t")
            tr(k_max_t[:], pt("k_max_t")[:, 0:2 * P].rearrange("p (h n) -> p h n", h=2), AX.X, ALU.max
               ).then_inc(drained[turn["k_max_t"][0]], 1)
            wait_drained(v, "k_max_t")
            for h in range(2):
                ts(k_diag[:, h, :], ident[:], k_max_t[:, h:h + 1], None, ALU.mult).then_inc(S("k_diag"), 1)
            edge_tiles(*slot_tiles(3 * T + 1))
            wait_filled(v, "k_max_b")
            for a, b in K_PARTS:
                last = tt(k_sb[:, a:b, :], k_sb[:, a:b, :],
                          pt("k_max_b")[:, 0:2 * P].unsqueeze(1).to_broadcast([P, b - a, 2 * P]), ALU.subtract)
                last.then_inc(S("k_less") if b < T else drained[turn["k_max_b"][0]], 1)
            for k in range(3 * T + 2, len(SLOTS)):
                edge_tiles(*slot_tiles(k))

            wait_filled(v, ("adj", NG - 1))
            wait_drained(v, ("adj", NG - 1))
            wait_drained(v, ("adj", NG - 2))
            v.wait_ge(S("list_in"), 32)
            missing = v.value_load(missing_i[0:1, 0:1], min_val=-NE, max_val=NE)
            with v.If(missing != 0):
                for half in range(2):
                    v.wait_ge(S(f"adj_out{half}"), 16 * ((NG + 1 - half) // 2))
                ts(hi_i[:], dst_all[:], 3, None, ALU.logical_shift_left).then_inc(S("rep_v"), 1)
                ts(lo_i[:], src_all[:], float(BY_SPAN), None, ALU.mult).then_inc(S("rep_v"), 1)
                v.wait_ge(S("rep_v"), 2)
                ts(lo_i[:], lo_i[:], 21, None, ALU.logical_shift_right).then_inc(S("rep_v"), 1)
                v.wait_ge(S("rep_v"), 3)
                tt(hi_i[:], hi_i[:], lo_i[:], ALU.bitwise_or).then_inc(S("rep_v"), 1)
                v.wait_ge(S("rep_v"), 4)
                nc.vector.tensor_copy(rep_key, hi_i[:]).then_inc(S("rep_v"), 1)
                nc.vector.scalar_tensor_tensor(out=rep_place, in0=lo_i[:], scalar=float(-SPAN), in1=src_all[:],
                                               op0=ALU.mult, op1=ALU.add).then_inc(S("rep_v"), 1)
                ts(rep_iota, iota_i[:, 0:P], float(-P), None, ALU.add).then_inc(S("rep_v"), 1)
                v.wait_ge(S("rep_v"), 7)
                with v.Fori(0, NB) as b:
                    nc.vector.memset(rep_acc, 0.0).then_inc(S("rep_zero"), 1)
                    v.wait_ge(S("rep_zero"), b + 1)
                    ts(rep_iota, rep_iota, float(P), None, ALU.add).then_inc(S("rep_moved"), 1)
                    with v.Fori(0, EC) as c:
                        v.wait_ge(S("rep_moved"), b + 1)
                        ts(rep_row[0:EP, :], rep_iota[0:EP, :], rep_key[:, bass.ds(c, 1)], None, ALU.is_equal)
                        ts(rep_col[0:EP, :], iota_i[0:EP, :], rep_place[:, bass.ds(c, 1)],
                           w_all[:, bass.ds(c, 1)], ALU.is_equal, ALU.mult).then_inc(S("rep_hot"), 1)
                        v.wait_ge(S("rep_done"), b * EC + c + 1)
                        tt(rep_acc, rep_acc, bank[0][:, 0:SPAN], ALU.add).then_inc(S("rep_added"), 1)
                        v.wait_ge(S("rep_added"), b * EC + c + 1)
                        v.nop()
                    v.sem_inc(S("block_summed"), 1)
                    v.wait_ge(S("block_out"), 16 * b + 16)
                    v.nop()
            with v.Else():
                v.nop()

            wait_filled(v, "k_sum")
            nc.vector.reciprocal(k_inv[:].rearrange("p h n -> p (h n)"), pt("k_sum")[:, 0:2 * P]
                                 ).then_inc(drained[turn["k_sum"][0]], 1)
            wait_drained(v, "k_sum")
            for i in range(2):
                wait_filled(v, ("kxn_t", i))
                tt(kxn_t[:, 2 * i:2 * i + 2], pt(("kxn_t", i))[:].rearrange("p (c h n) -> p c h n", c=2, h=2),
                   k_inv[:].unsqueeze(1).to_broadcast([P, 2, 2, P]), ALU.mult
                   ).then_inc(drained[turn[("kxn_t", i)][0]], 1)
            def rest_a(m):
                if m == 0:
                    for k in range(T):
                        v.wait_ge(S("a_hi"), k + 1)
                        tt(a_lo[0][:, k, :], AT[:, k, 0:P], a_hi[0][:, k, :].bitcast(F32), ALU.subtract
                           ).then_inc(S("a_lo"), 1)
                else:
                    v.wait_ge(S("a_hi"), T + m)
                    tt(a_lo[m % 2][:], AT[:, :, P * m:P * m + P], a_hi[m % 2][:].bitcast(F32), ALU.subtract
                       ).then_inc(S("a_lo"), 1)

            rest_a(0)
            wait_filled(v, "mid_t")
            v.wait_ge(S("b_in_in"), 16)
            for p in range(C):
                for i in range(2):
                    rows = slice(HD * i, HD * i + HD)
                    col = 2 * SL * (p % 2) + SL * i
                    last = ts(mid_t[rows, p, col:col + SL], pt("mid_t")[rows, P * p + col:P * p + col + SL],
                              b_in_col[rows, p:p + 1], None, ALU.add)
                    if (p, i) == (C - 1, 1):
                        last.then_inc(drained[turn["mid_t"][0]], 1)
                    else:
                        link(last)

            def pool_update(t):
                v.wait_ge(S("pool_add"), t)
                if t == 1:
                    before, total = xn[:, 0, :], ones[:, 0:1]
                else:
                    before, total = pool_acc, pool_sum[:]
                    v.wait_ge(S("pool_added"), 2 * (t - 1))
                nc.vector.scalar_tensor_tensor(out=pool_acc, in0=before, scalar=fade[:, t, 0:1],
                                               in1=pool_add[:, t % 2, :], op0=ALU.mult, op1=ALU.add
                                               ).then_inc(S("pool_added"), 1)
                nc.vector.scalar_tensor_tensor(out=pool_sum[:], in0=total, scalar=fade[:, t, 0:1],
                                               in1=fade[:, t, 1:2], op0=ALU.mult, op1=ALU.add
                                               ).then_inc(S("pool_added"), 1)

            def rest_x2(m):
                v.wait_ge(S("x2_hi"), m + 1)
                tt(x2_lo[:, :, P * m:P * m + P], pt(("x2_t", m))[:].rearrange("p (c n) -> p c n", c=C),
                   x2_hi[:, :, P * m:P * m + P].bitcast(F32), ALU.subtract
                   ).then_inc(drained[turn[("x2_t", m)][0]], 1)

            def rest_q(m):
                v.wait_ge(S("q_hi"), m + 1)
                tt(q_lo[:, m % 2], q_t[:, :, P * m:P * m + P], q_hi[:, m % 2].bitcast(F32), ALU.subtract
                   ).then_inc(S("q_lo"), 1)

            rest_q(0)
            for h in range(2):
                v.wait_ge(S("z_hi"), h + 1)
                tt(z_lo[h][:], pt(("z", h))[:], z_hi[:, h, :].bitcast(F32), ALU.subtract
                   ).then_inc(drained[turn[("z", h)][0]], 1)

            v.wait_ge(S("gate_in"), 64)
            for m in range(T + 1):
                if m + 1 < T:
                    rest_a(m + 1)
                    rest_q(m + 1)
                if m < T:
                    wait_filled(v, ("out", m))
                    v.wait_ge(S("x_biased"), m + 1)
                    tt(x_res(m), x_res(m), pt(("out", m))[:], ALU.add
                       ).then_inc(drained[turn[("out", m)][0]], 1)
                    wait_drained(v, ("out", m))
                    moments_of(m, x_res(m)).then_inc(S("moments2"), 1)
                if m >= 1:
                    t = m - 1
                    v.wait_ge(S("spread2"), t + 1)
                    v.wait_ge(S("moments2"), t + 1)
                    link(nc.vector.reciprocal(rstd[:, t:t + 1], spread[:, t:t + 1]))
                    ts(xn[:, t, :], x_res(t), moments[:, t, 0:1], rstd[:, t:t + 1], ALU.subtract, ALU.mult
                       ).then_inc(S("normed2"), 1)
                    v.wait_ge(S("normed2"), t + 1)
                    link(nc.vector.tensor_tensor_reduce(out=junk, in0=xn[:, t, :], in1=aw_b[:], scale=1.0, scalar=0.0,
                                                        op0=ALU.mult, op1=ALU.add, accum_out=scores[:, t:t + 1]))
                    link(ts(neg[:, 2 * t + 1:2 * t + 2], scores[:, t:t + 1], ab_b[:], -1.0, ALU.add, ALU.mult))
                    if t == T - 1:
                        link(ts(neg[:, 2 * t + 1:2 * t + 2], neg[:, 2 * t + 1:2 * t + 2], tail_far[:], None,
                                ALU.subtract))
                    before = 2 * t if t else 1
                    tt(neg[:, 2 * t + 2:2 * t + 3], neg[:, before:before + 1], neg[:, 2 * t + 1:2 * t + 2], ALU.min
                       ).then_inc(S("score_top"), 1)
                    v.wait_ge(S("score_top"), t + 1)
                    if t >= 2:
                        pool_update(t - 1)
                if 2 <= m < T:
                    rest_x2(m - 2)
            wait_filled(v, "score_max")
            tr(tiny[0:1, 1:2], pt("score_max")[0:1, 0:P], AX.X, ALU.min).then_inc(drained[turn["score_max"][0]], 1)
            pool_update(T - 1)
            wait_filled(v, "score_b")
            nc.vector.tensor_copy(tiny[:, 2:3], pt("score_b")[:, 0:1]).then_inc(drained[turn["score_b"][0]], 1)
            wait_drained(v, "score_b")
            v.sem_inc(S("score_far"), 1)
            rest_x2(T - 2)
            rest_x2(T - 1)
            wait_filled(v, "pooled")
            nc.vector.tensor_copy(pooled[:], pt("pooled")[:, 0:C]).then_inc(S("pooled"), 1)
            nc.vector.reciprocal(tiny[0:1, 4:5], pt("pooled")[0:1, 8:9]).then_inc(drained[turn["pooled"][0]], 1)
            wait_drained(v, "pooled")
            wait_filled(v, "gates")
            nc.vector.scalar_tensor_tensor(out=tiny[0:1, 8:8 + NX], in0=pt("gates")[0:1, 0:NX], scalar=tiny[0:1, 4:5],
                                           in1=gb_row[:], op0=ALU.mult, op1=ALU.add
                                           ).then_inc(drained[turn["gates"][0]], 1)
            wait_drained(v, "gates")
            link(nc.vector.max(tiny[0:1, 16:24], tiny[0:1, 8:8 + NX]))
            nc.vector.max_index(g_idx[:], tiny[0:1, 16:24], tiny[0:1, 8:8 + NX]).then_inc(S("chosen"), 1)
            link(nc.vector.tensor_copy(tiny[0:1, 6:7], tiny[0:1, 16:17]))
            v.wait_ge(S("chosen"), 1)
            ts(tiny[0:1, 8:24], tiny[0:1, 8:24], tiny[0:1, 6:7], None, ALU.subtract).then_inc(S("gate_less"), 1)
            v.wait_ge(S("gate_exp"), 2)
            link(nc.vector.reciprocal(tiny[0:1, 7:8], tiny[0:1, 5:6]))
            link(ts(tiny[0:1, 16:18], tiny[0:1, 16:18], tiny[0:1, 7:8], None, ALU.mult))
            link(tt(tiny[0:1, 26:27], tiny[0:1, 16:17], tiny[0:1, 17:18], ALU.add))
            link(ts(tiny[0:1, 26:27], tiny[0:1, 26:27], 1e-9, None, ALU.add))
            link(nc.vector.reciprocal(tiny[0:1, 27:28], tiny[0:1, 26:27]))
            ts(tiny[0:1, 24:26], tiny[0:1, 16:18], tiny[0:1, 27:28], None, ALU.mult).then_inc(S("shares"), 1)

            def rest_w1(e):
                for half in range(HC):
                    v.wait_ge(S("w1_hi"), 2 * e + half + 1)
                    tt(w1_lo[:, e, half], e_w1[:, e, :, half:H:HC], w1_hi[:, e, half].bitcast(F32), ALU.subtract
                       ).then_inc(S("w1_lo"), 1)

            def rest_w2(e):
                v.wait_ge(S("w2_hi"), e + 1)
                tt(w2_lo[:, e], e_w2[:, e], w2_hi[:, e].bitcast(F32), ALU.subtract).then_inc(S("w2_lo"), 1)

            rest_w1(0)
            wait_filled(v, "gates_b")
            nc.vector.tensor_copy(gate_b2[:], pt("gates_b")[:, 0:2]).then_inc(drained[turn["gates_b"][0]], 1)
            wait_drained(v, "gates_b")
            for i in range(12):
                e, half, chunk = i // 6, i // 3 % 2, i % 3
                n0, n1 = 512 * chunk, min(512 * (chunk + 1), NP)
                v.wait_ge(S("hid_hi"), i + 1)
                wait_drained(v, ("hid", i))
                tt(hid_lo[:, HC * e + half, n0:n1], hid[:, i % 2, 0:n1 - n0],
                   hid_hi[:, HC * e + half, n0:n1].bitcast(F32), ALU.subtract).then_inc(S("hid_lo"), 1)
                if i == 1:
                    rest_w1(1)
                if i in (3, 5):
                    rest_w2(i // 4)
                if i == 5:
                    v.wait_ge(S("b2_round"), 1)
                    tt(b2_parts[32:64, :], e_b2[32:64, 1, :], b2_parts[32:64, :].bitcast(F32), ALU.subtract
                       ).then_inc(S("b2_parts"), 1)

            def combine(m):
                v.wait_ge(S("post"), m + 1)
                link(nc.vector.scalar_tensor_tensor(out=x_res(m), in0=post[:, 2 * m % 4, :], scalar=gate_b2[:, 0:1],
                                                    in1=x_res(m), op0=ALU.mult, op1=ALU.add))
                wait_drained(v, ("expert", 2 * m + 1))
                nc.vector.scalar_tensor_tensor(out=x_res(m), in0=post[:, (2 * m + 1) % 4, :],
                                               scalar=gate_b2[:, 1:2], in1=x_res(m), op0=ALU.mult,
                                               op1=ALU.add).then_inc(S("y_ready"), 1)

            for m in range(T):
                i = 2 * m
                wait_filled(v, ("expert", i))
                if m == 0:
                    v.wait_ge(S("b2_in0"), 16)
                if m >= 2:
                    v.wait_ge(S("post"), m - 1)
                tt(pre[:, m % 2, :], pt(("expert", i))[:], e_b2[:, 0, :], ALU.add
                   ).then_inc(drained[turn[("expert", i)][0]], 1)
                wait_drained(v, ("expert", i))
                v.sem_inc(S("pre"), 1)
                if m >= 1:
                    combine(m - 1)
            combine(T - 1)


_INS = ["x", "src", "dst", "edge_weight", "L0_gnn_weight", "L0_gnn_bias", "L0_mix_W_in", "L0_mix_b_in", "L0_mix_Wq",
        "L0_mix_Wk", "L0_mix_Wv", "L0_mix_W_out", "L0_mix_b_out", "L0_ffn_attn_w", "L0_ffn_attn_b", "L0_ffn_gate_w",
        "L0_ffn_gate_b", "L0_ffn_w1", "L0_ffn_b1", "L0_ffn_w2", "L0_ffn_b2"]


def kernel(**inputs):
    import concourse.bacc as bacc
    from concourse.bass_utils import run_bass_kernel_spmd

    nc = bacc.Bacc("TRN2", target_bir_lowering=False, num_devices=1)
    arrays, args = {}, []
    for name in _INS:
        a = np.ascontiguousarray(inputs[name])
        arrays[f"in_{name}"] = a
        args.append(nc.dram_tensor(f"in_{name}", a.shape, mybir.dt.from_np(a.dtype), kind="ExternalInput").ap())
    shape = tuple(inputs["x"].shape)
    args.append(nc.dram_tensor("out_y", shape, F32, kind="ExternalOutput").ap())
    build(nc, *args)
    r = run_bass_kernel_spmd(nc, [arrays], core_ids=[0])
    return r.results[0]["out_y"]
```
